# Optimizing a Trainium2 kernel written in Bass

```python
import numpy as np
import jax
import jax.numpy as jnp

def _softmax(x, axis=-1):
    return jax.nn.softmax(x, axis=axis)

def _gelu(x):
    return jax.nn.gelu(x, approximate=True)

def _silu(x):
    return jax.nn.silu(x)

def _sigmoid(x):
    return jax.nn.sigmoid(x)

def _layernorm(x, axis=-1, eps=1e-05):
    m = jnp.mean(x, axis=axis, keepdims=True)
    v = jnp.var(x, axis=axis, keepdims=True)
    return (x - m) / jnp.sqrt(v + eps)

def _scatter_add(tgt, idx, src, axis=0):
    return tgt.at[idx].add(src)

def _segment_sum(src, seg, n):
    return jax.ops.segment_sum(src, seg, n)
kernel_name = 'mk_vit_tower_d1_tok_img768_r4_a4e7ed'

def setup_inputs(seed: int=0):
    np.random.seed(seed)
    _w = jnp.asarray

    def _rec_inputs():
        import jax
        import jax.numpy as jnp
        _rk = jax.random.key(seed)
        x = -0.000596345 + 1.00056 * jax.random.normal(jax.random.fold_in(_rk, 1), (16, 3, 64, 64), jnp.float32)
        return x
    x = _rec_inputs()

    def _L0_tok_setup():
        import jax, jax.numpy as jnp
        import numpy as np
        B = 16
        IMG = 64
        CH = 3
        EMBED = 64
        GP = 16
        PRE = [1, 2, 4]
        N_LEVELS = 3
        FUSED = EMBED * N_LEVELS

        def hilbert_flat_indices(n):
            t = np.arange(n * n, dtype=np.int64)
            x = np.zeros(n * n, dtype=np.int64)
            y = np.zeros(n * n, dtype=np.int64)
            s = 1
            while s < n:
                rx = 1 & t // 2
                ry = 1 & (t ^ rx)
                swap = ry == 0
                flip = swap & (rx == 1)
                x = np.where(flip, s - 1 - x, x)
                y = np.where(flip, s - 1 - y, y)
                x2 = np.where(swap, y, x)
                y2 = np.where(swap, x, y)
                x, y = (x2, y2)
                x = x + s * rx
                y = y + s * ry
                t = t // 4
                s *= 2
            return y * n + x

        def _level(x, idx, W, b, p, gp):
            Bsz, C, H, _ = x.shape
            h = H // p
            t = x.reshape(Bsz, C, h, p, h, p).transpose(0, 2, 4, 3, 5, 1).reshape(Bsz, h * h, p * p * C)
            t = t[:, idx]
            t = t.reshape(Bsz, h * h // gp, gp * p * p * C)
            return t @ W.T + b

        def _interp_linear(x, n_out):
            L = x.shape[1]
            pos = (jnp.arange(n_out, dtype=jnp.float32) + 0.5) * (L / n_out) - 0.5
            pos = jnp.clip(pos, 0.0, L - 1)
            i0 = jnp.floor(pos).astype(jnp.int32)
            i1 = jnp.minimum(i0 + 1, L - 1)
            w = (pos - i0).astype(x.dtype)
            return x[:, i0] * (1.0 - w)[None, :, None] + x[:, i1] * w[None, :, None]
        key = jax.random.key(seed)
        ks = jax.random.split(key, 9)
        inp = {'x': jax.random.normal(ks[0], (B, CH, IMG, IMG), jnp.float32)}
        for i, p in enumerate(PRE):
            din = CH * p * p * GP
            inp[f'W{i}'] = jax.random.normal(ks[1 + 2 * i], (EMBED, din), jnp.float32) * din ** (-0.5)
            inp[f'b{i}'] = jax.random.normal(ks[2 + 2 * i], (EMBED,), jnp.float32) * 0.02
        inp['Wf'] = jax.random.normal(ks[7], (FUSED, FUSED), jnp.float32) * FUSED ** (-0.5)
        inp['bf'] = jax.random.normal(ks[8], (FUSED,), jnp.float32) * 0.02
        for i, p in enumerate(PRE):
            inp[f'idx{i}'] = jnp.asarray(hilbert_flat_indices(IMG // p), jnp.int32)
        return inp
    _L0_tok_all = _L0_tok_setup()
    _L0_tok_in = {k: v for k, v in _L0_tok_all.items() if k in ('W0', 'b0', 'W1', 'b1', 'W2', 'b2', 'Wf', 'bf', 'idx0', 'idx1', 'idx2')}
    del _L0_tok_all

    def _L0_attn_setup():
        import jax, jax.numpy as jnp
        import numpy as np
        EMBED = 192
        HEADS = 12
        HEAD_DIM = EMBED // HEADS
        LN_EPS = 1e-05
        key = jax.random.key(seed)
        k1, k2, k3 = jax.random.split(key, 3)
        B, T = (2, 1024)
        x = jax.random.normal(k1, (B, T, EMBED), dtype=jnp.float32)
        w_qkv = jax.random.normal(k2, (EMBED, 3 * EMBED), dtype=jnp.float32) * EMBED ** (-0.5)
        w_out = jax.random.normal(k3, (EMBED, EMBED), dtype=jnp.float32) * EMBED ** (-0.5)
        b_out = jnp.zeros((EMBED,), dtype=jnp.float32)
        ln_g = jnp.ones((EMBED,), dtype=jnp.float32)
        ln_b = jnp.zeros((EMBED,), dtype=jnp.float32)
        return {'x': x, 'w_qkv': w_qkv, 'w_out': w_out, 'b_out': b_out, 'ln_g': ln_g, 'ln_b': ln_b}
    _L0_attn_all = _L0_attn_setup()
    _L0_attn_in = {k: v for k, v in _L0_attn_all.items() if k in ('w_qkv', 'w_out', 'b_out', 'ln_g', 'ln_b')}
    del _L0_attn_all

    def _L0_ffn_setup():
        import jax, jax.numpy as jnp
        import numpy as np
        D_MODEL = 192
        N_EXPERTS = 16
        TOP_K = 2
        D_FF = 4 * D_MODEL
        B, L = (4, 512)
        key = jax.random.key(seed)
        ks = jax.random.split(key, 6)
        s_in = 1.0 / np.sqrt(D_MODEL)
        s_ff = 1.0 / np.sqrt(D_FF)
        x = jax.random.normal(ks[0], (B, L, D_MODEL), dtype=jnp.float32)
        Wr = jax.random.uniform(ks[1], (N_EXPERTS, D_MODEL), jnp.float32, -s_in, s_in)
        W1 = jax.random.uniform(ks[2], (N_EXPERTS, D_MODEL, D_FF), jnp.float32, -s_in, s_in)
        b1 = jax.random.uniform(ks[3], (N_EXPERTS, D_FF), jnp.float32, -s_in, s_in)
        W2 = jax.random.uniform(ks[4], (N_EXPERTS, D_FF, D_MODEL), jnp.float32, -s_ff, s_ff)
        b2 = jax.random.uniform(ks[5], (N_EXPERTS, D_MODEL), jnp.float32, -s_ff, s_ff)
        return {'x': x, 'Wr': Wr, 'W1': W1, 'b1': b1, 'W2': W2, 'b2': b2}
    _L0_ffn_all = _L0_ffn_setup()
    _L0_ffn_in = {k: v for k, v in _L0_ffn_all.items() if k in ('Wr', 'W1', 'b1', 'W2', 'b2')}
    del _L0_ffn_all
    return {'x': x, 'L0_tok_W0': _L0_tok_in['W0'], 'L0_tok_b0': _L0_tok_in['b0'], 'L0_tok_W1': _L0_tok_in['W1'], 'L0_tok_b1': _L0_tok_in['b1'], 'L0_tok_W2': _L0_tok_in['W2'], 'L0_tok_b2': _L0_tok_in['b2'], 'L0_tok_Wf': _L0_tok_in['Wf'], 'L0_tok_bf': _L0_tok_in['bf'], 'L0_tok_idx0': _L0_tok_in['idx0'], 'L0_tok_idx1': _L0_tok_in['idx1'], 'L0_tok_idx2': _L0_tok_in['idx2'], 'L0_attn_w_qkv': _L0_attn_in['w_qkv'], 'L0_attn_w_out': _L0_attn_in['w_out'], 'L0_attn_b_out': _L0_attn_in['b_out'], 'L0_attn_ln_g': _L0_attn_in['ln_g'], 'L0_attn_ln_b': _L0_attn_in['ln_b'], 'L0_ffn_Wr': _L0_ffn_in['Wr'], 'L0_ffn_W1': _L0_ffn_in['W1'], 'L0_ffn_b1': _L0_ffn_in['b1'], 'L0_ffn_W2': _L0_ffn_in['W2'], 'L0_ffn_b2': _L0_ffn_in['b2']}

def reference(x, L0_tok_W0, L0_tok_b0, L0_tok_W1, L0_tok_b1, L0_tok_W2, L0_tok_b2, L0_tok_Wf, L0_tok_bf, L0_tok_idx0, L0_tok_idx1, L0_tok_idx2, L0_attn_w_qkv, L0_attn_w_out, L0_attn_b_out, L0_attn_ln_g, L0_attn_ln_b, L0_ffn_Wr, L0_ffn_W1, L0_ffn_b1, L0_ffn_W2, L0_ffn_b2):
    import jax
    import jax.numpy as jnp

    def _L0_tok_ref(x, W0, b0, W1, b1, W2, b2, Wf, bf, idx0, idx1, idx2):
        import jax, jax.numpy as jnp
        import numpy as np
        B = 16
        IMG = 64
        CH = 3
        EMBED = 64
        GP = 16
        PRE = [1, 2, 4]
        N_LEVELS = 3
        FUSED = EMBED * N_LEVELS

        def hilbert_flat_indices(n):
            t = np.arange(n * n, dtype=np.int64)
            x = np.zeros(n * n, dtype=np.int64)
            y = np.zeros(n * n, dtype=np.int64)
            s = 1
            while s < n:
                rx = 1 & t // 2
                ry = 1 & (t ^ rx)
                swap = ry == 0
                flip = swap & (rx == 1)
                x = np.where(flip, s - 1 - x, x)
                y = np.where(flip, s - 1 - y, y)
                x2 = np.where(swap, y, x)
                y2 = np.where(swap, x, y)
                x, y = (x2, y2)
                x = x + s * rx
                y = y + s * ry
                t = t // 4
                s *= 2
            return y * n + x

        def _level(x, idx, W, b, p, gp):
            Bsz, C, H, _ = x.shape
            h = H // p
            t = x.reshape(Bsz, C, h, p, h, p).transpose(0, 2, 4, 3, 5, 1).reshape(Bsz, h * h, p * p * C)
            t = t[:, idx]
            t = t.reshape(Bsz, h * h // gp, gp * p * p * C)
            return t @ W.T + b

        def _interp_linear(x, n_out):
            L = x.shape[1]
            pos = (jnp.arange(n_out, dtype=jnp.float32) + 0.5) * (L / n_out) - 0.5
            pos = jnp.clip(pos, 0.0, L - 1)
            i0 = jnp.floor(pos).astype(jnp.int32)
            i1 = jnp.minimum(i0 + 1, L - 1)
            w = (pos - i0).astype(x.dtype)
            return x[:, i0] * (1.0 - w)[None, :, None] + x[:, i1] * w[None, :, None]
        Ws = [(idx0, W0, b0, PRE[0]), (idx1, W1, b1, PRE[1]), (idx2, W2, b2, PRE[2])]
        outs = [_level(x, idx, W, b, p, GP) for idx, W, b, p in Ws]
        n_tokens = outs[0].shape[1]
        outs = [outs[0]] + [_interp_linear(o, n_tokens) for o in outs[1:]]
        y = jnp.concatenate(outs, axis=-1)
        return y @ Wf.T + bf

    def _L0_attn_ref(x, w_qkv, w_out, b_out, ln_g, ln_b):
        import jax, jax.numpy as jnp
        import numpy as np
        EMBED = 192
        HEADS = 12
        HEAD_DIM = EMBED // HEADS
        LN_EPS = 1e-05
        B, T, E = x.shape
        qkv = jnp.einsum('bte,ef->btf', x, w_qkv)
        q, k, v = jnp.split(qkv, 3, axis=-1)

        def split_heads(t):
            return t.reshape(B, T, HEADS, HEAD_DIM).transpose(0, 2, 1, 3)
        q, k, v = map(split_heads, (q, k, v))
        scores = jnp.einsum('bhtd,bhsd->bhts', q, k) / jnp.sqrt(jnp.float32(HEAD_DIM))
        attn = jax.nn.softmax(scores, axis=-1)
        out = jnp.einsum('bhts,bhsd->bhtd', attn, v)
        out = out.transpose(0, 2, 1, 3).reshape(B, T, E)
        y = jnp.einsum('bte,ef->btf', out, w_out) + b_out
        mu = jnp.mean(y, axis=-1, keepdims=True)
        var = jnp.var(y, axis=-1, keepdims=True)
        y = (y - mu) * jax.lax.rsqrt(var + LN_EPS) * ln_g + ln_b
        return y

    def _L0_ffn_ref(x, Wr, W1, b1, W2, b2):
        import jax, jax.numpy as jnp
        import numpy as np
        D_MODEL = 192
        N_EXPERTS = 16
        TOP_K = 2
        D_FF = 4 * D_MODEL
        B, L = (4, 512)
        logits = jnp.einsum('bld,ed->ble', x, Wr)
        probs = jax.nn.softmax(logits, axis=-1)
        top_p, top_idx = jax.lax.top_k(probs, TOP_K)
        gating = jnp.sum(jax.nn.one_hot(top_idx, N_EXPERTS, dtype=probs.dtype) * top_p[..., None], axis=-2)
        gate_e = jnp.moveaxis(gating, -1, 0)

        def step(y, params):
            W1e, b1e, W2e, b2e, ge = params
            h = jax.nn.gelu(jnp.einsum('bld,df->blf', x, W1e) + b1e, approximate=False)
            out = jnp.einsum('blf,fd->bld', h, W2e) + b2e
            return (y + ge[..., None] * out, None)
        y0 = jnp.zeros_like(x)
        y, _ = jax.lax.scan(step, y0, (W1, b1, W2, b2, gate_e))
        return x + y
    h = _L0_tok_ref(x, L0_tok_W0, L0_tok_b0, L0_tok_W1, L0_tok_b1, L0_tok_W2, L0_tok_b2, L0_tok_Wf, L0_tok_bf, L0_tok_idx0, L0_tok_idx1, L0_tok_idx2)
    h = h + _L0_attn_ref(_layernorm(h, axis=-1), L0_attn_w_qkv, L0_attn_w_out, L0_attn_b_out, L0_attn_ln_g, L0_attn_ln_b)
    h = h + _L0_ffn_ref(_layernorm(h, axis=-1), L0_ffn_Wr, L0_ffn_W1, L0_ffn_b1, L0_ffn_W2, L0_ffn_b2)
    return h

_drawn_inputs = setup_inputs


def setup_inputs(seed=0):
    import zlib

    import numpy as np

    out = dict(_drawn_inputs(seed))
    spreads = {'L0_attn_b_out': (0.0, 0.1), 'L0_attn_ln_g': (1.0, 0.2), 'L0_attn_ln_b': (0.0, 0.1)}
    factors = {'L0_ffn_Wr': 3.468,
     'L0_ffn_W1': 3.513,
     'L0_ffn_b1': 8.0,
     'L0_ffn_W2': 3.254,
     'L0_ffn_b2': 8.0}
    for name, (base, spread) in spreads.items():
        noise = np.random.default_rng([zlib.crc32(name.encode()), seed]).standard_normal(out[name].shape)
        drawn = base * np.exp(spread * noise) if base else spread * noise
        out[name] = jnp.asarray(drawn.astype(out[name].dtype))
    for name, factor in factors.items():
        out[name] = (out[name] * factor).astype(out[name].dtype)
    return out
```

```python
import concourse.bass as bass
from concourse import mybir
from contextlib import ExitStack


def vit_tower(nc, x0, x1, x2, w0t, w1t, w2t, b012, wft, bf, idx0, idx1, idx2, w_qkv, w_out, b_out, ln_g, ln_b,
              wrt, ew1, eb1, ew2, eb2, c_ident, c_tri, c_interp1, c_interp2, c_kone, c_iota, out):
    fp32, i32 = mybir.dt.float32, mybir.dt.int32
    ALU, ACT, AX = mybir.AluOpType, mybir.ActivationFunctionType, mybir.AxisListType
    ds = bass.ds

    P = 128
    B, T, E = out.shape
    TT = T // P
    NT = B * TT
    GP = 16
    C0, C1, C2 = (a.shape[1] // B for a in (x0, x1, x2))
    T1, T2 = idx1.shape[0] // GP, idx2.shape[0] // GP
    EM = w0t.shape[1]
    KH = E // 2
    HD, HEADS = 16, E // 16
    U, HU = 4, HEADS // 4
    G = HEADS // 4
    NX1, NX2 = GP * C1 // KH, GP * C2 // KH
    NE, DM, FF = ew1.shape
    FC = FF // P
    TOPK = 2
    NTILE = TOPK * NT + NE - 1
    ROW = E + 2
    ID, GATE = E, E + 1
    EPS = 1e-5
    SCALE = 1.0 / HD ** 0.5
    HILO = 512 // P

    xs_d = nc.dram_tensor("slot_rows", (NTILE * P, ROW), fp32).ap()
    acc_d = nc.dram_tensor("acc_rows", (NT * P + P, E), fp32).ap()

    ctx = ExitStack()
    with ctx:
        def sb(name, shape, dt=fp32):
            return ctx.enter_context(nc.sbuf_tensor(name, shape, dt))

        def ps(name, shape):
            return ctx.enter_context(nc.psum_tensor(name, shape, fp32))

        def sem(name):
            return ctx.enter_context(nc.semaphore(name))

        ident = sb("ident", [P, P])
        tri = sb("tri", [P, P])
        ones = sb("ones", [P, P])
        kone = sb("kone", [P, 1])
        mhalf = sb("mhalf", [P, TT])
        epsc = sb("epsc", [P, TT])
        m1c = sb("m1c", [T1, T])
        m2c = sb("m2c", [T2, T])
        w0s = sb("w0s", [GP * C0, EM])
        w1s = sb("w1s", [KH, NX1, EM])
        w2s = sb("w2s", [KH, NX2, EM])
        bias01 = sb("bias01", [P, 1])
        bias2 = sb("bias2", [EM, 1])
        wfa = sb("wfa", [P, E])
        wfb = sb("wfb", [EM + 1, E])
        wq = sb("wq", [KH, 2, G * P])
        wk = sb("wk", [KH, 2, G * P])
        wv = sb("wv", [KH, 2, E])
        wo = sb("wo", [KH, 2, E])
        wr = sb("wr", [KH, 2, NE])
        bout_b = sb("bout_b", [P, E])
        lng_b = sb("lng_b", [P, E])
        lnb_b = sb("lnb_b", [P, E])
        i0 = sb("i0", [P, TT, GP], i32)
        i1 = sb("i1", [T1, GP], i32)
        i2 = sb("i2", [T2, GP], i32)
        n_shared = GP * B * (C2 + C1 + TT * C0)
        shared = sb("shared", [P, n_shared])

        def carve():
            at = [0]

            def part(shape, dt=fp32):
                n = 1
                for d in shape[1:]:
                    n *= d
                a = shared[0:shape[0], at[0]:at[0] + n]
                at[0] += n
                assert at[0] <= n_shared
                if dt != fp32:
                    a = a.bitcast(dt)
                names = "abcd"[:len(shape) - 1]
                if len(shape) == 2:
                    return a
                return a.rearrange(f"p ({' '.join(names)}) -> p {' '.join(names)}",
                                   **dict(zip(names[1:], shape[2:])))
            return part

        early = carve()
        g2 = early([T2, GP, B * C2])
        g1 = early([T1, GP, B * C1])
        g0 = early([P, TT, GP, B * C0])
        xs0 = sb("xs0", [P, TT, GP, C0])
        xs1 = sb("xs1", [T1, GP, C1])
        xs2 = sb("xs2", [T2, GP, C2])
        x0T = sb("x0T", [GP * C0, T])
        x12T = sb("x12T", [KH, NX1 * T1 + NX2 * T2])
        o12 = sb("o12", [T1, 2 * EM])
        y01 = sb("y01", [P, T])
        y2 = sb("y2", [EM + 1, T])
        hr = sb("hr", [P, NT, E])
        st1 = sb("st1", [P, TT, 6])
        mv1 = sb("mv1", [P, TT, 2])
        rs1 = sb("rs1", [P, TT])
        var1 = sb("var1", [P, TT])
        xn1 = sb("xn1", [P, TT, E])
        x1T = sb("x1T", [KH, 2, T])
        qT = [sb(f"qT{p}", [P, G, T]) for p in range(2)]
        kT = [sb(f"kT{p}", [P, G, T]) for p in range(2)]
        v = [sb(f"v{p}", [P, TT, HEADS, 2 * HD]) for p in range(2)]
        negmax = sb("negmax", [P, TT, HEADS, 32])
        qa = sb("qa", [P, G, T])
        pT = [sb(f"pT{p}", [P, HU, 2 * T]) for p in range(2)]
        oT = sb("oT", [HU * 32, U, T])
        rden = sb("rden", [P, TT, HEADS])
        on = sb("on", [P, TT, HEADS, HD])
        onT = sb("onT", [KH, 2 * T])
        yb = sb("yb", [P, TT, E])
        st2 = sb("st2", [P, TT, 6])
        mv2 = sb("mv2", [P, TT, 2])
        rs2 = sb("rs2", [P, TT])
        var2 = sb("var2", [P, TT])
        yn = sb("yn", [P, TT, E])
        yg = sb("yg", [P, TT, E])
        yl = sb("yl", [P, TT, E])
        st3 = sb("st3", [P, TT, 6])
        mv3 = sb("mv3", [P, TT, 2])
        rs3 = sb("rs3", [P, TT])
        var3 = sb("var3", [P, TT])
        xrow = sb("xrow", [P, NT, ROW])
        x2T = sb("x2T", [KH, 2 * T])
        lg = sb("lg", [P, NT, NE])

        x2c = sb("x2c", [P, TT, E])
        padrow = sb("padrow", [P, ROW])
        late = carve()
        iota = sb("iota", [P, NTILE])
        r_mx = late([P, NT])
        r_ls = late([P, NT, NE])
        r_p = late([P, NT, NE])
        r_sum = late([P, NT])
        r_gate = [late([P, NT]) for k in range(2)]
        r_eq = late([P, NT, NE])
        r_key = late([P, NT, NE])
        r_km = late([P, NT])
        r_hot = [late([P, NT, NE]) for k in range(2)]
        r_cnt = late([P, NT, NE])
        r_ta = [late([P, NT, NE]) for k in range(2)]
        r_sl = late([P, NT, NE])
        r_ci = late([P, NE], i32)
        r_ti = late([P, NE], i32)
        r_tn = late([P, NE])
        r_te = [late([P, NE]) for k in range(2)]
        r_base = late([P, NE])
        r_slf = late([P, NT])
        slot = [late([P, NT], i32) for k in range(2)]
        r_tt = late([P, NTILE, NE])
        r_tf = late([P, NTILE])
        tab = late([P, NTILE], i32)
        w1b = [late([KH + 1, 2, FF]) for p in range(2)]
        w2b = [late([P, FC, E]) for p in range(2)]
        b2b = [late([P, E]) for p in range(2)]
        xt = [late([P, E]) for p in range(2)]
        meta = [late([P, ROW - E]) for p in range(2)]
        xtT = [late([KH + 1, 2, P]) for p in range(2)]
        hT = [late([P, FF]) for p in range(2)]
        ysum = [late([P, E]) for p in range(2)]
        yg8 = [late([P, E]) for p in range(2)]

        BK = ps("BK", [P, 8, 512])
        S, ST, M0, M1 = BK[:, 0:HU, :], BK[:, HU:2 * HU, :], BK[:, 6, :], BK[:, 7, :]
        H = [BK[:, 2 * p:2 * p + 2, :].rearrange("p b n -> p (b n)")[:, 0:FF] for p in range(2)]
        XT = [BK[:, 4 + p, :] for p in range(2)]
        Y = [BK[:, 6 + p, 0:E] for p in range(2)]

        names = ("ld_const ld_idx0 ld_idx1 ld_idx2 ga0 ga1 ga2 ld_w dve_init pool_init pool_zero ld_pad pool_xs "
                 "pe_xT pe_o12 pe_y pe_h pe_x1T pe_q01 pe_q2k0 pe_k12 pe_v pe_s pe_nmT pe_st pe_pv "
                 "pe_oT pe_onT pe_yat pe_x2T pe_lg act_xT act_o12 act_y act_x1T act_q01 act_q2k0 act_exp "
                 "act_oT act_onT act_x2T dve_max dve_qa dve_on dve_rden dve_h dve_st1 dve_mv1 dve_x1 dve_k12 dve_v "
                 "dve_yb dve_st2 dve_mv2 dve_yn dve_st3 dve_mv3 dve_x2 dve_lg pool_rs1 pool_rs2 pool_rs3 "
                 "pool_var1 pool_var2 pool_var3 pool_ln pool_h2 pool_r st_acc "
                 "r_dve r_ls r_exp r_cnt pe_rank pe_tot r_slot r_gate1 r_gate2 r_tab sc1 sc2 "
                 "m_x0 m_x1 m_wa0 m_wa1 m_wb0 m_wb1 m_b0 m_b1 m_tr m_xT m_s1 m_gelu m_s2 m_y m_yg m_add m_meta0 m_meta1 out_done").split()
        s = {n: sem(n) for n in names}

        n_const = 20 * 16

        block = ctx.enter_context(nc.Block())

        def over_images(eng, step):
            step(-1, 1, True, False, False)
            step(0, 0, True, True, False)
            step(1, 1, True, True, True)
            step(2, 0, True, True, True)
            with eng.Fori(1, (B - 2) // 2) as k:
                step(2 * k + 1, 1, True, True, True)
                step(2 * k + 2, 0, True, True, True)
            step(B - 1, (B - 1) % 2, False, True, True)
            step(B, B % 2, False, False, True)

        def apart(eng):
            eng.wait_ge(s["ld_const"], n_const)

        def wait_prev(eng, which, count):
            if not (isinstance(count, int) and count <= 0):
                eng.wait_ge(which, count)

        def moe_loads(sp):
            sp.wait_ge(s["r_tab"], 1)
            sp.wait_ge(s["sc2"], 16 * NT)
            sp.wait_ge(s["sc1"], 16 * NT)

            def load(t, k, p):
                e = sp.value_load(tab[0:1, ds(t, 1)], min_val=0, max_val=NE - 1)
                wait_prev(sp, s["m_tr"], t - 1)
                sp.dma_start(xt[p][:, :], xs_d[ds(t * P, P), 0:E]).then_inc(s[f"m_x{p}"], 16)
                wait_prev(sp, s["m_s1"], t - 1)
                sp.dma_start(w1b[p][0:KH, :, :], ew1[ds(e, 1), :, :].rearrange("a (c p) f -> p (a c) f", p=KH)) \
                    .then_inc(s[f"m_wa{p}"], 16)
                sp.dma_start(w1b[p][KH:KH + 1, 1, :], eb1[ds(e, 1), :]).then_inc(s[f"m_wa{p}"], 16)
                wait_prev(sp, s["m_s2"], t - 1)
                sp.dma_start(w2b[p][:, :, :], ew2[ds(e, 1), :, :].rearrange("a (c p) d -> p (a c) d", p=P)) \
                    .then_inc(s[f"m_wb{p}"], 16)
                wait_prev(sp, s["m_y"], t - 1)
                sp.dma_start(b2b[p][:, :], eb2[ds(e, 1), :].rearrange("a d -> (a d)").partition_broadcast(P)) \
                    .then_inc(s[f"m_b{p}"], 16)

            load(0, 0, 0)
            load(1, 0, 1)
            with sp.Fori(1, NTILE // 2) as k:
                load(2 * k, k, 0)
                load(2 * k + 1, k, 1)
            load(NTILE - 1, NTILE // 2, 0)
            sp.wait_ge(s["m_add"], 16 * NTILE)
            sp.dma_start(out.rearrange("b t e -> (b t) e"), acc_d[0:NT * P, :]).then_inc(s["out_done"], 16)
            sp.wait_ge(s["out_done"], 16)

        def moe_tensor(pe):
            pe.wait_ge(s["r_cnt"], 1)
            f = r_cnt[:, :, :].rearrange("p t e -> p (t e)")
            nc.tensor.matmul(M0, tri[:, :], f, start=True, stop=True).then_inc(s["pe_rank"], 1)
            nc.tensor.matmul(M1, ones[:, :], f, start=True, stop=True).then_inc(s["pe_tot"], 1)

            def rows_T(t, k, p):
                pe.wait_ge(s[f"m_x{p}"], 16 * k + 16)
                wait_prev(pe, s["m_xT"], t - 1)
                for c in range(2):
                    last = nc.tensor.matmul(XT[p][0:KH, c * P:(c + 1) * P], xt[p][:, c * KH:(c + 1) * KH],
                                            ident[:, :], start=True, stop=True, is_transpose=True)
                last.then_inc(s["m_tr"], 1)

            def up(t, k, p):
                pe.wait_ge(s["m_xT"], t + 1)
                pe.wait_ge(s[f"m_wa{p}"], 32 * k + 32)
                wait_prev(pe, s["m_gelu"], t - 1)
                for c in range(FC):
                    o = H[p][:, c * P:(c + 1) * P]
                    nc.tensor.matmul(o, w1b[p][0:KH, 0, c * P:(c + 1) * P], xtT[p][0:KH, 0, :], start=True, stop=False)
                    last = nc.tensor.matmul(o, w1b[p][:, 1, c * P:(c + 1) * P], xtT[p][:, 1, :],
                                            start=False, stop=True)
                last.then_inc(s["m_s1"], 1)

            def down(t, k, p):
                pe.wait_ge(s["m_gelu"], t + 1)
                pe.wait_ge(s[f"m_wb{p}"], 16 * k + 16)
                wait_prev(pe, s["m_y"], t - 1)
                for c in range(FC):
                    last = nc.tensor.matmul(Y[p], hT[p][:, c * P:(c + 1) * P], w2b[p][:, c, :],
                                            start=(c == 0), stop=(c == FC - 1))
                last.then_inc(s["m_s2"], 1)

            rows_T(0, 0, 0)
            rows_T(1, 0, 1)
            up(0, 0, 0)
            up(1, 0, 1)
            rows_T(2, 1, 0)
            down(0, 0, 0)
            up(2, 1, 0)
            rows_T(3, 1, 1)
            down(1, 0, 1)
            with pe.Fori(1, (NTILE - 3) // 2) as k:
                up(2 * k + 1, k, 1)
                rows_T(2 * k + 2, k + 1, 0)
                down(2 * k, k, 0)
                up(2 * k + 2, k + 1, 0)
                rows_T(2 * k + 3, k + 1, 1)
                down(2 * k + 1, k, 1)
            t = NTILE - 3
            up(t + 1, t // 2, 1)
            rows_T(t + 2, t // 2 + 1, 0)
            down(t, t // 2, 0)
            up(t + 2, t // 2 + 1, 0)
            down(t + 1, t // 2, 1)
            down(t + 2, t // 2 + 1, 0)

        def moe_scalar(act):
            act.wait_ge(s["r_ls"], 1)
            nc.scalar.activation(r_p[:, :, :], r_ls[:, :, :], ACT.Exp).then_inc(s["r_exp"], 1)

            def gelu(t, k, p):
                act.wait_ge(s["m_s1"], t + 1)
                wait_prev(act, s["m_s2"], t - 1)
                nc.scalar.activation(hT[p][:, :], H[p], ACT.Gelu).then_inc(s["m_gelu"], 1)

            gelu(0, 0, 0)
            gelu(1, 0, 1)
            with act.Fori(1, NTILE // 2) as k:
                gelu(2 * k, k, 0)
                gelu(2 * k + 1, k, 1)
            gelu(NTILE - 1, NTILE // 2, 0)

        def moe_vector(dve):
            done = [0]

            def then(ins):
                done[0] += 1
                ins.then_inc(s["r_dve"], 1)
                dve.wait_ge(s["r_dve"], done[0])

            def over_e(a):
                return a.unsqueeze(2).to_broadcast([P, NT, NE])

            V = nc.vector
            for p in range(2):
                V.memset(xtT[p][KH:KH + 1, :, :], 1.0)
            dve.wait_ge(s["dve_lg"], B)
            then(V.tensor_reduce(r_mx[:, :], lg[:, :, :], AX.X, ALU.max))
            V.tensor_tensor(r_ls[:, :, :], lg[:, :, :], over_e(r_mx[:, :]), ALU.subtract).then_inc(s["r_ls"], 1)
            dve.wait_ge(s["r_exp"], 1)
            then(V.tensor_reduce(r_sum[:, :], r_p[:, :, :], AX.X, ALU.add))
            then(V.reciprocal(r_mx[:, :], r_sum[:, :]))
            then(V.tensor_tensor(r_p[:, :, :], r_p[:, :, :], over_e(r_mx[:, :]), ALU.mult))
            for k in range(TOPK):
                then(V.tensor_reduce(r_gate[k][:, :], r_p[:, :, :], AX.X, ALU.max))
                then(V.tensor_tensor(r_eq[:, :, :], r_p[:, :, :], over_e(r_gate[k][:, :]), ALU.is_equal))
                then(V.scalar_tensor_tensor(r_key[:, :, :], r_eq[:, :, :], -float(NE),
                                            iota[:, 0:NE].unsqueeze(1).to_broadcast([P, NT, NE]), ALU.mult, ALU.add))
                then(V.tensor_reduce(r_km[:, :], r_key[:, :, :], AX.X, ALU.min))
                then(V.tensor_tensor(r_hot[k][:, :, :], r_key[:, :, :], over_e(r_km[:, :]), ALU.is_equal))
                if k == 0:
                    then(V.scalar_tensor_tensor(r_p[:, :, :], r_hot[0][:, :, :], -2.0, r_p[:, :, :],
                                                ALU.mult, ALU.add))
            V.tensor_tensor(r_cnt[:, :, :], r_hot[0][:, :, :], r_hot[1][:, :, :], ALU.add).then_inc(s["r_cnt"], 1)
            V.tensor_copy(xrow[:, :, GATE], r_gate[0][:, :]).then_inc(s["r_gate1"], 1)
            dve.wait_ge(s["pe_tot"], 1)
            tot = M1.rearrange("p (t e) -> p t e", e=NE)
            then(V.tensor_copy(r_ta[0][:, :, :], tot))
            a, b, sh = 0, 1, 1
            while sh < NT:
                V.tensor_copy(r_ta[b][:, 0:sh, :], r_ta[a][:, 0:sh, :])
                then(V.tensor_tensor(r_ta[b][:, sh:NT, :], r_ta[a][:, sh:NT, :], r_ta[a][:, 0:NT - sh, :], ALU.add))
                a, b, sh = b, a, 2 * sh
            then(V.tensor_scalar(r_ci[:, :], r_ta[a][:, NT - 1, :], float(P - 1), None, ALU.add))
            then(V.tensor_scalar(r_ti[:, :], r_ci[:, :], P.bit_length() - 1, None, ALU.arith_shift_right))
            then(V.tensor_copy(r_tn[:, :], r_ti[:, :]))
            then(V.tensor_copy(r_te[0][:, :], r_tn[:, :]))
            c, d, sh = 0, 1, 1
            while sh < NE:
                V.tensor_copy(r_te[d][:, 0:sh], r_te[c][:, 0:sh])
                then(V.tensor_tensor(r_te[d][:, sh:NE], r_te[c][:, sh:NE], r_te[c][:, 0:NE - sh], ALU.add))
                c, d, sh = d, c, 2 * sh
            then(V.tensor_tensor(r_base[:, :], r_te[c][:, :], r_tn[:, :], ALU.subtract))
            then(V.scalar_tensor_tensor(r_sl[:, :, :], r_base[:, :].unsqueeze(1).to_broadcast([P, NT, NE]), float(P),
                                        r_ta[a][:, :, :], ALU.mult, ALU.add))
            then(V.tensor_tensor(r_sl[:, :, :], r_sl[:, :, :], tot, ALU.subtract))
            dve.wait_ge(s["pe_rank"], 1)
            then(V.tensor_tensor(r_sl[:, :, :], r_sl[:, :, :], M0.rearrange("p (t e) -> p t e", e=NE), ALU.add))
            for k in range(TOPK):
                then(V.tensor_tensor(r_eq[:, :, :], r_sl[:, :, :], r_hot[k][:, :, :], ALU.mult))
                then(V.tensor_reduce(r_slf[:, :], r_eq[:, :, :], AX.X, ALU.add))
                ins = V.tensor_copy(slot[k][:, :], r_slf[:, :])
                then(ins) if k == 0 else ins.then_inc(s["r_slot"], 1)
            then(V.tensor_tensor(r_tt[:, :, :], r_te[c][:, :].unsqueeze(1).to_broadcast([P, NTILE, NE]),
                                 iota[:, :].unsqueeze(2).to_broadcast([P, NTILE, NE]), ALU.is_le))
            then(V.tensor_reduce(r_tf[:, :], r_tt[:, :, :], AX.X, ALU.add))
            V.tensor_scalar(tab[:, :], r_tf[:, :], float(NE - 1), None, ALU.min).then_inc(s["r_tab"], 1)
            dve.wait_ge(s["sc1"], 16 * NT)
            V.tensor_copy(xrow[:, :, GATE], r_gate[1][:, :]).then_inc(s["r_gate2"], 1)

            def rows_T(t, k, p):
                dve.wait_ge(s["m_tr"], t + 1)
                wait_prev(dve, s["m_s1"], t - 1)
                V.tensor_copy(xtT[p][0:KH, :, :], XT[p][0:KH, 0:2 * P].rearrange("p (c t) -> p c t", c=2)) \
                    .then_inc(s["m_xT"], 1)

            def biased(t, k, p):
                dve.wait_ge(s["m_s2"], t + 1)
                dve.wait_ge(s[f"m_b{p}"], 16 * k + 16)
                wait_prev(dve, s["m_yg"], t - 1)
                V.tensor_tensor(ysum[p][:, :], Y[p], b2b[p][:, :], ALU.add).then_inc(s["m_y"], 1)

            rows_T(0, 0, 0)
            rows_T(1, 0, 1)
            rows_T(2, 1, 0)
            biased(0, 0, 0)
            rows_T(3, 1, 1)
            biased(1, 0, 1)
            with dve.Fori(1, (NTILE - 3) // 2) as k:
                rows_T(2 * k + 2, k + 1, 0)
                biased(2 * k, k, 0)
                rows_T(2 * k + 3, k + 1, 1)
                biased(2 * k + 1, k, 1)
            t = NTILE - 3
            rows_T(t + 2, t // 2 + 1, 0)
            biased(t, t // 2, 0)
            biased(t + 1, t // 2, 1)
            biased(t + 2, t // 2 + 1, 0)

        def moe_gpsimd(pool):
            pool.wait_ge(s["ld_pad"], 32)
            pool.wait_ge(s["r_slot"], 1)
            pool.wait_ge(s["r_gate1"], 1)
            pool.wait_ge(s["pool_r"], B)
            for t in range(NT):
                nc.gpsimd.indirect_dma_start(xs_d, bass.IndirectOffsetOnAxis(slot[0][:, t:t + 1], 0),
                                             xrow[:, t, :], None).then_inc(s["sc1"], 16)
            pool.wait_ge(s["r_gate2"], 1)
            for t in range(NT):
                nc.gpsimd.indirect_dma_start(xs_d, bass.IndirectOffsetOnAxis(slot[1][:, t:t + 1], 0),
                                             xrow[:, t, :], None).then_inc(s["sc2"], 16)
            pool.wait_ge(s["st_acc"], 16 * B)

            def load_meta(t, p):
                pool.dma_start(meta[p][:, :], xs_d[ds(t * P, P), E:ROW]).then_inc(s[f"m_meta{p}"], 16)

            def add(t, k, p, more=True):
                pool.wait_ge(s["m_y"], t + 1)
                pool.wait_ge(s[f"m_meta{p}"], 16 * k + 16)
                wait_prev(pool, s["m_add"], 16 * t)
                nc.gpsimd.tensor_tensor(yg8[p][:, :], ysum[p][:, :], meta[p][:, 1:2].to_broadcast([P, E]),
                                        ALU.mult).then_inc(s["m_yg"], 1)
                if more:
                    load_meta(t + 1, 1 - p)
                apart(pool)
                pool.wait_ge(s["m_yg"], t + 1)
                nc.gpsimd.indirect_dma_start(acc_d, bass.IndirectOffsetOnAxis(meta[p][:, 0:1].bitcast(i32), 0),
                                             yg8[p][:, :], None, compute_op=ALU.add).then_inc(s["m_add"], 16)

            pool.wait_ge(s["sc2"], 16 * NT)
            pool.wait_ge(s["sc1"], 16 * NT)
            load_meta(0, 0)
            add(0, 0, 0)
            add(1, 0, 1)
            with pool.Fori(1, NTILE // 2) as k:
                add(2 * k, k, 0)
                add(2 * k + 1, k, 1)
            add(NTILE - 1, NTILE // 2, 0, more=False)

        @block.sync
        def _(sp):
            sp.dma_start(i0[:, :, :], idx0.rearrange("(c p g) -> p c g", c=TT, g=GP)).then_inc(s["ld_idx0"], 16)
            sp.dma_start(i2[:, :], idx2.rearrange("(p g) -> p g", g=GP)).then_inc(s["ld_idx2"], 16)
            sp.dma_start(i1[:, :], idx1.rearrange("(p g) -> p g", g=GP)).then_inc(s["ld_idx1"], 16)
            consts = [
                (ident[:, :], c_ident), (tri[:, :], c_tri), (kone[:, :], c_kone), (m1c[:, :], c_interp1),
                (m2c[:, :], c_interp2), (iota[:, :], c_iota), (w0s[:, :], w0t),
                (w1s[:, :, :], w1t.rearrange("(c p) e -> p c e", p=KH)),
                (w2s[:, :, :], w2t.rearrange("(c p) e -> p c e", p=KH)),
                (bias01[:, :], b012[0:P, :]), (bias2[:, :], b012[P:P + EM, :]),
                (wfa[:, :], wft[0:P, :]), (wfb[0:EM, :], wft[P:E, :]), (wfb[EM:EM + 1, :], bf),
                (wv[:, :, :], w_qkv[:, 2 * E:3 * E].rearrange("(c p) n -> p c n", p=KH)),
                (wo[:, :, :], w_out.rearrange("(c p) n -> p c n", p=KH)),
                (wr[:, :, :], wrt.rearrange("(c p) n -> p c n", p=KH)),
                (bout_b[:, :], b_out.partition_broadcast(P)), (lng_b[:, :], ln_g.partition_broadcast(P)),
                (lnb_b[:, :], ln_b.partition_broadcast(P)),
            ]
            for dst, src in consts:
                sp.dma_start(dst, src).then_inc(s["ld_const"], 16)
            sp.wait_ge(s["dve_init"], 1)
            for dst, at in ((wq, 0), (wk, E)):
                for c in range(2):
                    sp.dma_start(dst[:, c, :].rearrange("p (h d) -> p h d", d=32)[:, :, 0:HD],
                                 w_qkv[c * KH:(c + 1) * KH, at:at + E].rearrange("p (h d) -> p h d", d=HD)) \
                        .then_inc(s["ld_w"], 16)
            sp.wait_ge(s["pool_init"], 3)
            sp.dma_start(xs_d.rearrange("(t p) n -> p t n", p=P),
                         padrow[:, :].unsqueeze(1).to_broadcast([P, NTILE, ROW])).then_inc(s["ld_pad"], 16)
            sp.dma_start(acc_d[NT * P:NT * P + P, :], padrow[:, 0:E]).then_inc(s["ld_pad"], 16)
            with sp.Fori(0, B) as j:
                sp.wait_ge(s["pool_r"], j + 1)
                sp.dma_start(acc_d[ds(j * T, T), :].rearrange("(t p) e -> p t e", p=P),
                             hr[:, ds(TT * j, TT), :]).then_inc(s["st_acc"], 16)
            moe_loads(sp)

        @block.tensor
        def _(pe):
            pe.wait_ge(s["ld_const"], n_const)
            pe.wait_ge(s["ld_w"], 64)
            pe.wait_ge(s["dve_init"], 2)

            def transpose(dst, src, n):
                return nc.tensor.matmul(dst, src, ident[0:n, 0:n], start=True, stop=True, is_transpose=True)

            def f_xT(n):
                for c in range(TT):
                    transpose(M0[0:GP * C0, c * P:(c + 1) * P], xs0[:, c, :, :].rearrange("p g c -> p (g c)"), P)
                f = xs1[:, :, :].rearrange("p g c -> p (g c)")
                for c in range(NX1):
                    transpose(M0[0:KH, T + c * T1:T + (c + 1) * T1], f[:, c * KH:(c + 1) * KH], T1)
                f = xs2[:, :, :].rearrange("p g c -> p (g c)")
                at = T + NX1 * T1
                for c in range(NX2):
                    last = transpose(M0[0:KH, at + c * T2:at + (c + 1) * T2], f[:, c * KH:(c + 1) * KH], T2)
                last.then_inc(s["pe_xT"], 1)

            def f_o12(n):
                pe.wait_ge(s["act_xT"], n + 1)
                for c in range(NX1):
                    nc.tensor.matmul(M0[0:T1, 0:EM], x12T[:, c * T1:(c + 1) * T1], w1s[:, c, :],
                                     start=(c == 0), stop=(c == NX1 - 1))
                at = NX1 * T1
                for c in range(NX2):
                    last = nc.tensor.matmul(M0[0:T2, EM:2 * EM], x12T[:, at + c * T2:at + (c + 1) * T2],
                                            w2s[:, c, :], start=(c == 0), stop=(c == NX2 - 1))
                last.then_inc(s["pe_o12"], 1)

            def f_y(n):
                apart(pe)
                pe.wait_ge(s["act_o12"], n + 1)
                nc.tensor.matmul(M0[0:EM, 0:T], w0s[:, :], x0T[:, :], start=True, stop=True)
                nc.tensor.matmul(M0[EM:2 * EM, 0:T], o12[:, 0:EM], m1c[:, :], start=True, stop=True)
                nc.tensor.matmul(M0[0:EM, T:2 * T], o12[0:T2, EM:2 * EM], m2c[:, :], start=True, stop=True) \
                    .then_inc(s["pe_y"], 1)

            def f_h(n):
                pe.wait_ge(s["act_y"], n + 1)
                for c in range(TT):
                    o = M0[:, c * E:(c + 1) * E]
                    nc.tensor.matmul(o, y01[:, c * P:(c + 1) * P], wfa[:, :], start=True, stop=False)
                    last = nc.tensor.matmul(o, y2[:, c * P:(c + 1) * P], wfb[:, :], start=False, stop=True)
                last.then_inc(s["pe_h"], 1)

            def f_x1T(n):
                pe.wait_ge(s["dve_x1"], n + 1)
                for c in range(2):
                    for t in range(TT):
                        last = transpose(M0[0:KH, (c * TT + t) * P:(c * TT + t + 1) * P],
                                         xn1[:, t, c * KH:(c + 1) * KH], P)
                last.then_inc(s["pe_x1T"], 1)

            def project(dst, w, g):
                for c in range(2):
                    last = nc.tensor.matmul(dst, w[:, c, g * P:(g + 1) * P], x1T[:, c, :],
                                            start=(c == 0), stop=(c == 1))
                return last

            def f_q01(n):
                pe.wait_ge(s["act_x1T"], n + 1)
                project(M0[:, 0:T], wq, 0)
                project(M0[:, T:2 * T], wq, 1).then_inc(s["pe_q01"], 1)

            def f_q2k0(n):
                pe.wait_ge(s["act_q01"], n + 1)
                project(M0[:, 0:T], wq, 2)
                project(M0[:, T:2 * T], wk, 0).then_inc(s["pe_q2k0"], 1)

            def f_k12(n):
                pe.wait_ge(s["act_q2k0"], n + 1)
                project(M0[:, 0:T], wk, 1)
                project(M0[:, T:2 * T], wk, 2).then_inc(s["pe_k12"], 1)

            def f_v(n):
                pe.wait_ge(s["dve_k12"], n + 1)
                for t in range(TT):
                    for c in range(2):
                        last = nc.tensor.matmul(M0[:, t * E:(t + 1) * E], x1T[:, c, t * P:(t + 1) * P],
                                                wv[:, c, :], start=(c == 0), stop=(c == 1))
                last.then_inc(s["pe_v"], 1)

            def a_s(i, p, u):
                if u == 0:
                    pe.wait_ge(s["act_q2k0"], i + 1)
                    pe.wait_ge(s["dve_k12"], i + 1)
                wait_prev(pe, s["dve_max"], U * i + u)
                for t in range(TT):
                    for a in range(HU):
                        g, r = divmod(HU * u + a, 4)
                        rows = slice(32 * r, 32 * r + 32)
                        last = nc.tensor.matmul(S[:, a, t * T:(t + 1) * T], qT[p][rows, g, t * P:(t + 1) * P],
                                                kT[p][rows, g, :], start=True, stop=True)
                last.then_inc(s["pe_s"], 1)

            def a_nmT(i, g):
                pe.wait_ge(s["dve_max"], U * i + g + 2)
                for t in range(TT):
                    last = transpose(M1[:, t * P:(t + 1) * P],
                                     negmax[:, t, 4 * g:4 * g + 4, :].rearrange("p h d -> p (h d)"), P)
                last.then_inc(s["pe_nmT"], 1)

            def a_st(i, p, u):
                pe.wait_ge(s["dve_qa"], G * i + min(u + 1, G))
                wait_prev(pe, s["act_exp"], U * i + u)
                for t in range(TT):
                    for a in range(HU):
                        g, r = divmod(HU * u + a, 4)
                        rows = slice(32 * r, 32 * r + 32)
                        last = nc.tensor.matmul(ST[:, a, t * T:(t + 1) * T], kT[p][rows, g, t * P:(t + 1) * P],
                                                qa[rows, g, :], start=True, stop=True)
                last.then_inc(s["pe_st"], 1)

            def a_pv(i, p, u):
                if u == 0:
                    pe.wait_ge(s["dve_v"], i + 1)
                pe.wait_ge(s["act_exp"], U * i + u + 1)
                for t in range(TT):
                    for a in range(HU):
                        last = nc.tensor.matmul(M1[32 * a:32 * a + 32, 0:T], v[p][:, t, HU * u + a, :],
                                                pT[u % 2][:, a, t * T:(t + 1) * T],
                                                start=(t == 0), stop=(t == TT - 1))
                last.then_inc(s["pe_pv"], 1)

            def b_oT(j, t):
                if t == 0:
                    pe.wait_ge(s["act_oT"], U * j + U)
                else:
                    pe.wait_ge(s["dve_on"], TT * j + t)
                for u in range(U):
                    last = transpose(M1[:, u * HU * 32:(u + 1) * HU * 32], oT[:, u, t * P:(t + 1) * P], HU * 32)
                last.then_inc(s["pe_oT"], 1)

            def b_onT(j):
                pe.wait_ge(s["dve_on"], TT * j + TT)
                for c in range(2):
                    for t in range(TT):
                        f = on[:, t, :, :].rearrange("p h d -> p (h d)")
                        last = transpose(M1[0:KH, (c * TT + t) * P:(c * TT + t + 1) * P],
                                         f[:, c * KH:(c + 1) * KH], P)
                last.then_inc(s["pe_onT"], 1)

            def b_y(j):
                pe.wait_ge(s["act_onT"], j + 1)
                for t in range(TT):
                    for c in range(2):
                        last = nc.tensor.matmul(M1[:, t * E:(t + 1) * E],
                                                onT[:, (c * TT + t) * P:(c * TT + t + 1) * P], wo[:, c, :],
                                                start=(c == 0), stop=(c == 1))
                last.then_inc(s["pe_yat"], 1)

            def b_x2T(j):
                pe.wait_ge(s["dve_x2"], j + 1)
                for c in range(2):
                    for t in range(TT):
                        last = transpose(M1[0:KH, (c * TT + t) * P:(c * TT + t + 1) * P],
                                         x2c[:, t, c * KH:(c + 1) * KH], P)
                last.then_inc(s["pe_x2T"], 1)

            def b_lg(j):
                pe.wait_ge(s["act_x2T"], j + 1)
                for t in range(TT):
                    for c in range(2):
                        last = nc.tensor.matmul(M1[:, t * NE:(t + 1) * NE],
                                                x2T[:, (c * TT + t) * P:(c * TT + t + 1) * P], wr[:, c, :],
                                                start=(c == 0), stop=(c == 1))
                last.then_inc(s["pe_lg"], 1)

            def step(i, p, tok, att, clo):
                n, j = i + 1, i - 1
                if att:
                    a_s(i, p, 0)
                if clo:
                    b_oT(j, 0)
                if att:
                    a_s(i, p, 1)
                if clo:
                    b_oT(j, 1)
                if att:
                    if clo:
                        pe.wait_ge(s["dve_on"], TT * j + TT)
                    if tok:
                        pe.wait_ge(s["dve_v"], n)
                        pe.wait_ge(s["pool_xs"], n + 1)
                    a_nmT(i, 0)
                if tok:
                    if not att:
                        pe.wait_ge(s["pool_xs"], n + 1)
                    f_xT(n)
                if att:
                    a_st(i, p, 0)
                    a_s(i, p, 2)
                if tok:
                    f_o12(n)
                if clo:
                    if att:
                        pe.wait_ge(s["dve_qa"], G * i + 1)
                    b_onT(j)
                if att:
                    pe.wait_ge(s["act_onT"], j + 1) if clo else pe.wait_ge(s["dve_qa"], G * i + 1)
                    a_nmT(i, 1)
                    a_st(i, p, 1)
                if tok:
                    f_y(n)
                if att:
                    pe.wait_ge(s["dve_qa"], G * i + 2)
                    a_pv(i, p, 0)
                    a_s(i, p, 3)
                if clo:
                    if att:
                        pe.wait_ge(s["act_oT"], U * i + 1)
                    b_y(j)
                if tok:
                    f_h(n)
                if att:
                    pe.wait_ge(s["dve_yb"], j + 1) if clo else pe.wait_ge(s["act_oT"], U * i + 1)
                    a_nmT(i, 2)
                    a_st(i, p, 2)
                    pe.wait_ge(s["dve_qa"], G * i + 3)
                    a_pv(i, p, 1)
                    a_st(i, p, 3)
                if tok:
                    f_x1T(n)
                if att:
                    pe.wait_ge(s["act_oT"], U * i + 2)
                    a_pv(i, p, 2)
                if tok:
                    f_q01(n)
                    f_q2k0(n)
                if att:
                    pe.wait_ge(s["act_oT"], U * i + 3)
                    a_pv(i, p, 3)
                if tok:
                    f_k12(n)
                if clo:
                    pe.wait_ge(s["act_oT"], U * i + 4) if att else pe.wait_ge(s["dve_yb"], j + 1)
                    b_x2T(j)
                    b_lg(j)
                if tok:
                    f_v(n)
                if clo and att:
                    pe.wait_ge(s["dve_lg"], j + 1)

            over_images(pe, step)
            moe_tensor(pe)

        @block.scalar
        def _(act):
            act.wait_ge(s["ld_const"], n_const)

            def f_xT(n):
                act.wait_ge(s["pe_xT"], n + 1)
                wait_prev(act, s["pe_y"], n)
                nc.scalar.activation(x0T[:, :], M0[0:GP * C0, 0:T], ACT.Copy)
                nc.scalar.activation(x12T[:, :], M0[0:KH, T:2 * T], ACT.Copy).then_inc(s["act_xT"], 1)

            def f_o12(n):
                act.wait_ge(s["pe_o12"], n + 1)
                nc.scalar.activation(o12[:, 0:EM], M0[0:T1, 0:EM], ACT.Copy)
                nc.scalar.activation(o12[0:T2, EM:2 * EM], M0[0:T2, EM:2 * EM], ACT.Copy) \
                    .then_inc(s["act_o12"], 1)

            def f_y(n):
                act.wait_ge(s["pe_y"], n + 1)
                wait_prev(act, s["pe_h"], n)
                nc.scalar.activation(y01[:, :], M0[:, 0:T], ACT.Identity, bias=bias01[:, :])
                nc.scalar.activation(y2[0:EM, :], M0[0:EM, T:2 * T], ACT.Identity, bias=bias2[:, :]) \
                    .then_inc(s["act_y"], 1)

            def f_x1T(n):
                act.wait_ge(s["pe_x1T"], n + 1)
                wait_prev(act, s["pe_v"], n)
                nc.scalar.activation(x1T[:, :, :].rearrange("p c t -> p (c t)"), M0[0:KH, :], ACT.Copy) \
                    .then_inc(s["act_x1T"], 1)

            def f_q01(n, p):
                act.wait_ge(s["pe_q01"], n + 1)
                wait_prev(act, s["pe_s"], U * (n - 1))
                wait_prev(act, s["pe_st"], U * (n - 1))
                wait_prev(act, s["dve_qa"], G * (n - 1))
                nc.scalar.activation(qT[p][:, 0:2, :].rearrange("p g t -> p (g t)"), M0[:, :], ACT.Copy,
                                     scale=SCALE).then_inc(s["act_q01"], 1)

            def f_q2k0(n, p):
                act.wait_ge(s["pe_q2k0"], n + 1)
                nc.scalar.activation(qT[p][:, 2, :], M0[:, 0:T], ACT.Copy, scale=SCALE)
                nc.scalar.activation(kT[p][:, 0, :], M0[:, T:2 * T], ACT.Identity, bias=kone[:, :]) \
                    .then_inc(s["act_q2k0"], 1)

            def a_exp(i, u):
                act.wait_ge(s["pe_st"], U * i + u + 1)
                wait_prev(act, s["pe_pv"], U * i + u - 1)
                nc.scalar.activation(pT[u % 2][:, :, :], ST[:, :, :], ACT.Exp).then_inc(s["act_exp"], 1)

            def a_oT(i, u):
                act.wait_ge(s["pe_pv"], U * i + u + 1)
                if u == 0:
                    wait_prev(act, s["pe_oT"], TT * i)
                nc.scalar.activation(oT[:, u, :], M1[0:HU * 32, 0:T], ACT.Copy).then_inc(s["act_oT"], 1)

            def b_onT(j):
                act.wait_ge(s["pe_onT"], j + 1)
                wait_prev(act, s["pe_yat"], j)
                nc.scalar.activation(onT[:, :], M1[0:KH, :], ACT.Copy).then_inc(s["act_onT"], 1)

            def b_x2T(j):
                act.wait_ge(s["pe_x2T"], j + 1)
                wait_prev(act, s["pe_lg"], j)
                nc.scalar.activation(x2T[:, :], M1[0:KH, :], ACT.Copy).then_inc(s["act_x2T"], 1)

            def step(i, p, tok, att, clo):
                n, j = i + 1, i - 1
                if tok:
                    f_xT(n)
                if att:
                    a_exp(i, 0)
                if tok:
                    f_o12(n)
                if clo:
                    b_onT(j)
                if att:
                    a_exp(i, 1)
                if tok:
                    f_y(n)
                if att:
                    a_oT(i, 0)
                    a_exp(i, 2)
                    a_oT(i, 1)
                    a_exp(i, 3)
                if tok:
                    f_x1T(n)
                if att:
                    a_oT(i, 2)
                if tok:
                    f_q01(n, 1 - p)
                    f_q2k0(n, 1 - p)
                if att:
                    a_oT(i, 3)
                if clo:
                    b_x2T(j)

            over_images(act, step)
            moe_scalar(act)

        @block.vector
        def _(dve):
            nc.vector.memset(wq[:, :, :], 0.0)
            nc.vector.memset(wk[:, :, :], 0.0).then_inc(s["dve_init"], 1)
            for p in range(2):
                nc.vector.memset(v[p][:, :, :, :], 1.0)
            nc.vector.memset(negmax[:, :, :, :], 0.0)
            nc.vector.memset(ones[:, :], 1.0)
            nc.vector.memset(y2[EM:EM + 1, :], 1.0).then_inc(s["dve_init"], 1)
            dve.wait_ge(s["dve_init"], 2)
            dve.wait_ge(s["ld_const"], n_const)

            def norm_stats(src, st, mv, done_st, done_mv, n):
                for t in range(TT):
                    last = nc.vector.bn_stats(st[:, t, :], src(t))
                last.then_inc(done_st, 1)
                apart(dve)
                dve.wait_ge(done_st, n + 1)
                for t in range(TT):
                    last = nc.vector.bn_aggr(mv[:, t, :], st[:, t, :])
                last.then_inc(done_mv, 1)

            def normalize(dst, src, mv, rs):
                for t in range(TT):
                    last = nc.vector.tensor_scalar(dst(t), src(t), mv[:, t, 0:1], rs[:, t:t + 1],
                                                   ALU.subtract, ALU.mult)
                return last

            def f_h(n):
                dve.wait_ge(s["pe_h"], n + 1)
                dst = hr[:, ds(TT * n, TT), :]
                nc.vector.tensor_copy(dst, M0[:, 0:TT * E].rearrange("p (t e) -> p t e", e=E)) \
                    .then_inc(s["dve_h"], 1)
                apart(dve)
                dve.wait_ge(s["dve_h"], n + 1)
                wait_prev(dve, s["pool_rs1"], n)
                norm_stats(lambda t: hr[:, ds(TT * n + t, 1), :].rearrange("p a e -> p (a e)"),
                           st1, mv1, s["dve_st1"], s["dve_mv1"], n)

            def f_x1(n):
                dve.wait_ge(s["pool_rs1"], n + 1)
                wait_prev(dve, s["pe_x1T"], n)
                normalize(lambda t: xn1[:, t, :], lambda t: hr[:, ds(TT * n + t, 1), :].rearrange("p a e -> p (a e)"),
                          mv1, rs1).then_inc(s["dve_x1"], 1)

            def f_k12(n, p):
                dve.wait_ge(s["pe_k12"], n + 1)
                wait_prev(dve, s["pe_st"], U * (n - 1))
                nc.vector.tensor_scalar(kT[p][:, 1:3, :].rearrange("p g t -> p (g t)"), M0[:, :], kone[:, :],
                                        None, ALU.add).then_inc(s["dve_k12"], 1)

            def f_v(n, p):
                dve.wait_ge(s["pe_v"], n + 1)
                wait_prev(dve, s["pe_pv"], U * (n - 1))
                nc.vector.tensor_copy(v[p][:, :, :, 0:HD],
                                      M0[:, 0:TT * E].rearrange("p (t h d) -> p t h d", t=TT, d=HD)) \
                    .then_inc(s["dve_v"], 1)

            def a_max(i, u):
                dve.wait_ge(s["pe_s"], U * i + u + 1)
                if u == 0:
                    wait_prev(dve, s["pe_nmT"], G * i)
                nc.vector.tensor_reduce(negmax[:, :, HU * u:HU * u + HU, HD].rearrange("p t h -> p h t"),
                                        S[:, :, :].rearrange("p a (t k) -> p a t k", t=TT), AX.X, ALU.max,
                                        negate=True).then_inc(s["dve_max"], 1)

            def a_qa(i, p, g):
                dve.wait_ge(s["pe_nmT"], G * i + g + 1)
                if g == 0:
                    wait_prev(dve, s["pe_st"], U * i)
                nc.vector.tensor_tensor(qa[:, g, :], M1[:, 0:T], qT[p][:, g, :], ALU.add) \
                    .then_inc(s["dve_qa"], 1)

            def b_on(j, t):
                dve.wait_ge(s["pe_oT"], TT * j + t + 1)
                if t == 0:
                    wait_prev(dve, s["pe_onT"], j)
                m = M1[:, 0:HEADS * 32].rearrange("p (h d) -> p h d", d=32)
                nc.vector.reciprocal(rden[:, t, :], m[:, :, HD]).then_inc(s["dve_rden"], 1)
                dve.wait_ge(s["dve_rden"], TT * j + t + 1)
                nc.vector.tensor_tensor(on[:, t, :, :], m[:, :, 0:HD],
                                        rden[:, t, :].unsqueeze(2).to_broadcast([P, HEADS, HD]), ALU.mult) \
                    .then_inc(s["dve_on"], 1)

            def b_yb(j):
                dve.wait_ge(s["pe_yat"], j + 1)
                nc.vector.tensor_tensor(yb[:, :, :], M1[:, 0:TT * E].rearrange("p (t e) -> p t e", e=E),
                                        bout_b[:, :].unsqueeze(1).to_broadcast([P, TT, E]), ALU.add) \
                    .then_inc(s["dve_yb"], 1)
                apart(dve)
                dve.wait_ge(s["dve_yb"], j + 1)
                norm_stats(lambda t: yb[:, t, :], st2, mv2, s["dve_st2"], s["dve_mv2"], j)

            def b_yn(j):
                dve.wait_ge(s["pool_rs2"], j + 1)
                wait_prev(dve, s["pool_h2"], j)
                normalize(lambda t: yn[:, t, :], lambda t: yb[:, t, :], mv2, rs2).then_inc(s["dve_yn"], 1)

            def b_stats(j):
                apart(dve)
                dve.wait_ge(s["pool_h2"], j + 1)
                wait_prev(dve, s["pool_rs3"], j)
                norm_stats(lambda t: hr[:, ds(TT * j + t, 1), :].rearrange("p a e -> p (a e)"),
                           st3, mv3, s["dve_st3"], s["dve_mv3"], j)

            def b_x2(j):
                dve.wait_ge(s["pool_rs3"], j + 1)
                wait_prev(dve, s["pool_r"], j)
                wait_prev(dve, s["pe_x2T"], j)
                normalize(lambda t: x2c[:, t, :], lambda t: hr[:, ds(TT * j + t, 1), :].rearrange("p a e -> p (a e)"),
                          mv3, rs3).then_inc(s["dve_x2"], 1)

            def b_lg(j):
                dve.wait_ge(s["pe_lg"], j + 1)
                nc.vector.tensor_copy(lg[:, ds(TT * j, TT), :], M1[:, 0:TT * NE].rearrange("p (t e) -> p t e", e=NE)) \
                    .then_inc(s["dve_lg"], 1)

            def step(i, p, tok, att, clo):
                n, j = i + 1, i - 1
                if att:
                    a_max(i, 0)
                if clo:
                    b_on(j, 0)
                if att:
                    a_max(i, 1)
                if clo:
                    b_on(j, 1)
                if att:
                    a_qa(i, p, 0)
                    a_max(i, 2)
                    a_qa(i, p, 1)
                    a_max(i, 3)
                if clo:
                    b_yb(j)
                if tok:
                    f_h(n)
                if att:
                    a_qa(i, p, 2)
                if clo:
                    b_yn(j)
                if tok:
                    f_x1(n)
                if clo:
                    b_stats(j)
                if tok:
                    f_k12(n, 1 - p)
                if clo:
                    b_x2(j)
                    b_lg(j)
                if tok:
                    f_v(n, 1 - p)

            over_images(dve, step)
            moe_vector(dve)

        @block.gpsimd
        def _(pool):
            nc.gpsimd.memset(mhalf[:, :], -0.5)
            nc.gpsimd.memset(epsc[:, :], EPS)
            nc.gpsimd.memset(padrow[:, :], 0.0).then_inc(s["pool_init"], 1)
            pool.wait_ge(s["pool_init"], 1)
            nc.gpsimd.iota(padrow[:, ID:ID + 1].bitcast(i32), [[0, 1]], base=NT * P, channel_multiplier=1) \
                .then_inc(s["pool_init"], 1)
            nc.gpsimd.iota(xrow[:, :, ID].bitcast(i32), [[P, NT]], base=0, channel_multiplier=1) \
                .then_inc(s["pool_init"], 1)
            pool.wait_ge(s["ld_idx2"], 16)
            for g in range(GP):
                nc.gpsimd.indirect_dma_start(g2[:, g, :], None, x2,
                                             bass.IndirectOffsetOnAxis(i2[:, g:g + 1], 0)).then_inc(s["ga2"], 16)
            pool.wait_ge(s["ld_idx1"], 16)
            for g in range(GP):
                nc.gpsimd.indirect_dma_start(g1[:, g, :], None, x1,
                                             bass.IndirectOffsetOnAxis(i1[:, g:g + 1], 0)).then_inc(s["ga1"], 16)
            pool.wait_ge(s["ld_idx0"], 16)
            for c in range(TT):
                for g in range(GP):
                    nc.gpsimd.indirect_dma_start(g0[:, c, g, :], None, x0,
                                                 bass.IndirectOffsetOnAxis(i0[:, c, g:g + 1], 0)) \
                        .then_inc(s["ga0"], 16)
            for k, n in (("ga2", GP), ("ga1", GP), ("ga0", TT * GP)):
                pool.wait_ge(s[k], 16 * n)

            def f_xs(n):
                wait_prev(pool, s["pe_xT"], n)
                nc.gpsimd.tensor_copy(xs2[:, :, :], g2[:, :, ds(n * C2, C2)])
                nc.gpsimd.tensor_copy(xs1[:, :, :], g1[:, :, ds(n * C1, C1)])
                nc.gpsimd.tensor_copy(xs0[:, :, :, :].rearrange("p t g c -> p (t g) c"),
                                      g0[:, :, :, ds(n * C0, C0)].rearrange("p t g c -> p (t g) c")) \
                    .then_inc(s["pool_xs"], 1)

            def rsqrt(rs, mv, var, ready, free, added, done, n):
                pool.wait_ge(ready, n + 1)
                wait_prev(pool, free, n)
                nc.gpsimd.tensor_tensor(var[:, :], mv[:, :, 1], epsc[:, :], ALU.add).then_inc(added, 1)
                pool.wait_ge(added, n + 1)
                nc.gpsimd.tensor_tensor(rs[:, :], var[:, :], mhalf[:, :], ALU.pow).then_inc(done, 1)

            def step(i, p, tok, att, clo):
                n, j = i + 1, i - 1
                if tok:
                    f_xs(n)
                if clo:
                    rsqrt(rs2, mv2, var2, s["dve_mv2"], s["dve_yn"], s["pool_var2"], s["pool_rs2"], j)
                if tok:
                    rsqrt(rs1, mv1, var1, s["dve_mv1"], s["dve_x1"], s["pool_var1"], s["pool_rs1"], n)
                if clo:
                    hj = hr[:, ds(TT * j, TT), :]
                    pool.wait_ge(s["dve_yn"], j + 1)
                    nc.gpsimd.tensor_tensor(yg[:, :, :], yn[:, :, :], lng_b[:, :].unsqueeze(1).to_broadcast([P, TT, E]),
                                            ALU.mult).then_inc(s["pool_ln"], 1)
                    pool.wait_ge(s["pool_ln"], 2 * j + 1)
                    nc.gpsimd.tensor_tensor(yl[:, :, :], yg[:, :, :], lnb_b[:, :].unsqueeze(1).to_broadcast([P, TT, E]),
                                            ALU.add).then_inc(s["pool_ln"], 1)
                    pool.wait_ge(s["pool_ln"], 2 * j + 2)
                    nc.gpsimd.tensor_tensor(hj, hj, yl[:, :, :], ALU.add).then_inc(s["pool_h2"], 1)
                    pool.wait_ge(s["pool_h2"], j + 1)
                    rsqrt(rs3, mv3, var3, s["dve_mv3"], s["dve_x2"], s["pool_var3"], s["pool_rs3"], j)
                    pool.wait_ge(s["dve_x2"], j + 1)
                    nc.gpsimd.tensor_copy(xrow[:, ds(TT * j, TT), 0:E], x2c[:, :, :])
                    nc.gpsimd.tensor_tensor(hj, hj, x2c[:, :, :], ALU.add).then_inc(s["pool_r"], 1)

            over_images(pool, step)
            moe_gpsimd(pool)


def _interpolation(n_in, n_out):
    import numpy as np
    pos = (np.arange(n_out, dtype=np.float32) + np.float32(0.5)) * np.float32(n_in / n_out) - np.float32(0.5)
    pos = np.clip(pos, 0.0, n_in - 1).astype(np.float32)
    lo = np.floor(pos).astype(np.int64)
    hi = np.minimum(lo + 1, n_in - 1)
    w = (pos - lo).astype(np.float32)
    m = np.zeros((n_in, n_out), np.float32)
    m[lo, np.arange(n_out)] += 1 - w
    m[hi, np.arange(n_out)] += w
    return m


def kernel(**inputs):
    import numpy as np
    import concourse.bacc as bacc
    from concourse import mybir
    from concourse.bass_utils import run_bass_kernel_spmd

    a = {k: np.asarray(v) for k, v in inputs.items()}
    x = a["x"]
    B, C, H, _ = x.shape
    T, P = 256, 128

    def patches(p):
        h = H // p
        t = x.reshape(B, C, h, p, h, p).transpose(2, 4, 0, 3, 5, 1)
        return t.reshape(h * h, B * p * p * C)

    k = "L0_tok_"
    arrays = {
        "x0": patches(1), "x1": patches(2), "x2": patches(4),
        "w0t": a[k + "W0"].T, "w1t": a[k + "W1"].T, "w2t": a[k + "W2"].T,
        "b012": np.concatenate([a[k + "b0"], a[k + "b1"], a[k + "b2"]])[:, None],
        "wft": a[k + "Wf"].T, "bf": a[k + "bf"][None, :],
        "idx0": a[k + "idx0"], "idx1": a[k + "idx1"], "idx2": a[k + "idx2"],
        "w_qkv": a["L0_attn_w_qkv"], "w_out": a["L0_attn_w_out"], "b_out": a["L0_attn_b_out"],
        "ln_g": a["L0_attn_ln_g"], "ln_b": a["L0_attn_ln_b"], "wrt": a["L0_ffn_Wr"].T,
        "ew1": a["L0_ffn_W1"], "eb1": a["L0_ffn_b1"], "ew2": a["L0_ffn_W2"], "eb2": a["L0_ffn_b2"],
        "c_ident": np.eye(P, dtype=np.float32), "c_tri": np.triu(np.ones((P, P), np.float32), 1),
        "c_interp1": _interpolation(a[k + "idx1"].size // 16, T),
        "c_interp2": _interpolation(a[k + "idx2"].size // 16, T),
        "c_kone": (np.arange(P) % 32 == 16).astype(np.float32)[:, None],
        "c_iota": np.tile(np.arange(2 * B * T // P + 15, dtype=np.float32), (P, 1)),
    }
    arrays = {n: np.ascontiguousarray(v) for n, v in arrays.items()}
    nc = bacc.Bacc("TRN2", target_bir_lowering=False, num_devices=1)
    args = [nc.dram_tensor(n, v.shape, mybir.dt.from_np(v.dtype), kind="ExternalInput").ap()
            for n, v in arrays.items()]
    args.append(nc.dram_tensor("out", (B, T, 192), mybir.dt.float32, kind="ExternalOutput").ap())
    vit_tower(nc, *args)
    r = run_bass_kernel_spmd(nc, [arrays], core_ids=[0])
    return r.results[0]["out"]
```

```python
import concourse.bass as bass
from concourse import mybir
from contextlib import ExitStack


def vit_tower(nc, x0, x1, x2, w0t, w1t, w2t, b012, wft, bf, idx0, idx1, idx2, w_qkv, w_out, b_out, ln_g, ln_b,
              wrt, ew1, eb1, ew2, eb2, c_ident, c_tri, c_interp1, c_interp2, c_iota, out):
    fp32, bf16, i32 = mybir.dt.float32, mybir.dt.bfloat16, mybir.dt.int32
    ALU, ACT, AX = mybir.AluOpType, mybir.ActivationFunctionType, mybir.AxisListType
    ds = bass.ds

    P = 128
    B, T, E = out.shape
    TT = T // P
    NT = B * TT
    GP = 16
    C0, C1, C2 = (a.shape[1] // B for a in (x0, x1, x2))
    T1, T2 = idx1.shape[0] // GP, idx2.shape[0] // GP
    EM = w0t.shape[1]
    KH = E // 2
    HD, HEADS = 16, E // 16
    U, HU = 4, HEADS // 4
    HH = HEADS // 2
    NPART = 3
    QPART, KPART = (0, 0, 1, 1, 0, 2), (0, 1, 0, 1, 2, 0)
    KS = len(QPART) * HD
    KM = KS + NPART
    NX1, NX2 = GP * C1 // KH, GP * C2 // KH
    NE, DM, FF = ew1.shape
    FC = FF // P
    TOPK = 2
    NTILE = TOPK * NT + NE - 1
    ROW = E + 2
    ID, GATE = E, E + 1
    EPS = 1e-5
    SCALE = 1.0 / HD ** 0.5
    HILO = 512 // P

    xs_d = nc.dram_tensor("slot_rows", (NTILE * P, ROW), fp32).ap()
    g2_d = nc.dram_tensor("level2_patches", (idx2.shape[0], x2.shape[1]), fp32).ap()
    qk_d = nc.dram_tensor("qk_parts", (2, 2, NPART, E, T), bf16).ap()
    acc_d = nc.dram_tensor("acc_rows", (NT * P + P, E), fp32).ap()

    ctx = ExitStack()
    with ctx:
        def sb(name, shape, dt=fp32):
            return ctx.enter_context(nc.sbuf_tensor(name, shape, dt))

        def ps(name, shape):
            return ctx.enter_context(nc.psum_tensor(name, shape, fp32))

        def sem(name):
            return ctx.enter_context(nc.semaphore(name))

        ident = sb("ident", [P, P])
        ident16 = sb("ident16", [P, P], bf16)
        tri = sb("tri", [P, P])
        ones = sb("ones", [P, P])
        mhalf = sb("mhalf", [P, TT])
        epsc = sb("epsc", [P, TT])
        bd = sb("bd", [P, P])
        rr = sb("rr", [P, T])
        bd2 = sb("bd2", [P, EM])
        rr2 = sb("rr2", [P, T])
        w1s = sb("w1s", [KH, NX1, EM])
        w2s = sb("w2s", [KH, NX2, EM])
        bias01 = sb("bias01", [P, 1])
        bias2 = sb("bias2", [EM, 1])
        wfa = sb("wfa", [P, E])
        wfb = sb("wfb", [EM + 1, E])
        wqkv = sb("wqkv", [KH, 2, 3 * E])
        wo = sb("wo", [KH, 2, E])
        wr = sb("wr", [KH, 2, NE])
        bout_b = sb("bout_b", [P, E])
        lng_b = sb("lng_b", [P, E])
        lnb_b = sb("lnb_b", [P, E])
        i0 = sb("i0", [P, TT, GP], i32)
        i1 = sb("i1", [T1, GP], i32)
        i2 = sb("i2", [P, T2 * GP // P], i32)
        g1 = sb("g1", [T1, GP, B * C1])
        g0 = sb("g0", [P, TT, GP, B * C0])
        g2 = sb("g2", [P, T2 * GP // P, B * C2])
        n_shared = 17000
        shared = sb("shared", [P, n_shared])

        def carve():
            at = [0]

            def part(shape, dt=fp32):
                n = 1
                for d in shape[1:]:
                    n *= d
                if dt == bf16:
                    n //= 2
                a = shared[0:shape[0], at[0]:at[0] + n]
                at[0] += n
                assert at[0] <= n_shared
                if dt != fp32:
                    a = a.bitcast(dt)
                names = "abcd"[:len(shape) - 1]
                if len(shape) == 2:
                    return a
                return a.rearrange(f"p ({' '.join(names)}) -> p {' '.join(names)}",
                                   **dict(zip(names[1:], shape[2:])))
            return part

        xs0 = sb("xs0", [P, TT, GP, C0])
        xs1 = sb("xs1", [T1, GP, C1])
        xs2 = [sb(f"xs2{p}", [T2, GP, C2]) for p in range(2)]
        x12T = sb("x12T", [KH, NX1 * T1 + NX2 * T2])
        y01 = sb("y01", [P, T])
        y2 = sb("y2", [EM + 1, T])
        hr = sb("hr", [P, NT, E])
        st1 = sb("st1", [P, TT, 6])
        mv1 = sb("mv1", [P, TT, 2])
        rs1 = sb("rs1", [P, TT])
        var1 = sb("var1", [P, TT])
        xn1 = sb("xn1", [P, TT, E])
        x1T = sb("x1T", [KH, 2, T])
        early = carve()
        qk = early([KH, 2, NPART, 2, T], bf16)
        qkr = [early([KH, 2 * T]) for which in range(2)]
        qs = [early([KM, HEADS, T], bf16) for p in range(2)]
        ks = [early([KM, HEADS, T], bf16) for p in range(2)]
        v = [sb(f"v{p}", [P, TT, HEADS, 2 * HD]) for p in range(2)]
        negmax = sb("negmax", [P, TT, HEADS])
        nmr = sb("nmr", [P, 2, TT, HH])
        nm = sb("nm", [P, 2, TT, NPART, HH], bf16)
        nmT = sb("nmT", [NPART * HH, 2, T], bf16)
        pT = [early([P, HU, 2 * T]) for p in range(2)]
        oT = sb("oT", [HU * 32, U, T])
        rden = sb("rden", [P, TT, HEADS])
        on = sb("on", [P, TT, HEADS, HD])
        onT = sb("onT", [KH, 2 * T])
        yb = sb("yb", [P, TT, E])
        st2 = sb("st2", [P, TT, 6])
        mv2 = sb("mv2", [P, TT, 2])
        rs2 = sb("rs2", [P, TT])
        var2 = sb("var2", [P, TT])
        yn = sb("yn", [P, TT, E])
        yg = sb("yg", [P, TT, E])
        yl = sb("yl", [P, TT, E])
        st3 = sb("st3", [P, TT, 6])
        mv3 = sb("mv3", [P, TT, 2])
        rs3 = sb("rs3", [P, TT])
        var3 = sb("var3", [P, TT])
        xrow = sb("xrow", [P, NT, ROW])
        x2T = sb("x2T", [KH, 2 * T])
        lg = sb("lg", [P, NT, NE])

        x2c = sb("x2c", [P, TT, E])
        padrow = sb("padrow", [P, ROW])
        late = carve()
        iota = sb("iota", [P, NTILE])
        r_mx = late([P, NT])
        r_ls = late([P, NT, NE])
        r_p = late([P, NT, NE])
        r_sum = late([P, NT])
        r_gate = [late([P, NT]) for k in range(2)]
        r_eq = late([P, NT, NE])
        r_key = late([P, NT, NE])
        r_km = late([P, NT])
        r_hot = [late([P, NT, NE]) for k in range(2)]
        r_cnt = late([P, NT, NE])
        r_ta = [late([P, NT, NE]) for k in range(2)]
        r_sl = late([P, NT, NE])
        r_ci = late([P, NE], i32)
        r_ti = late([P, NE], i32)
        r_tn = late([P, NE])
        r_te = [late([P, NE]) for k in range(2)]
        r_base = late([P, NE])
        r_slf = late([P, NT])
        slot = [late([P, NT], i32) for k in range(2)]
        r_tt = late([P, NTILE, NE])
        r_tf = late([P, NTILE])
        tab = late([P, NTILE], i32)
        w1b = [late([KH + 1, 2, FF]) for p in range(2)]
        w2b = [late([P, FC, E]) for p in range(2)]
        b2b = [late([P, E]) for p in range(2)]
        xt = [late([P, E]) for p in range(2)]
        meta = [late([P, ROW - E]) for p in range(2)]
        xtT = [late([KH + 1, 2, P]) for p in range(2)]
        hT = [late([P, FF]) for p in range(2)]
        ysum = [late([P, E]) for p in range(2)]
        yg8 = [late([P, E]) for p in range(2)]

        BK = ps("BK", [P, 8, 512])
        S, ST, M0, M1 = BK[:, 0:HU, :], BK[:, HU:2 * HU, :], BK[:, 6, :], BK[:, 7, :]
        H = [BK[:, 2 * p:2 * p + 2, :].rearrange("p b n -> p (b n)")[:, 0:FF] for p in range(2)]
        XT = [BK[:, 4 + p, :] for p in range(2)]
        Y = [BK[:, 6 + p, 0:E] for p in range(2)]

        names = ("ld_const ld_idx0 ld_idx1 ld_idx2 ga0 ga1 ga2 ld_w dve_init pool_init pool_zero ld_pad pool_xs "
                 "pe_xT pe_o12 pe_y pe_h pe_x1T pe_q pe_k pe_v pe_s pe_nmT pe_st pe_pv "
                 "pe_oT pe_onT pe_yat pe_x2T pe_lg act_xT act_o12 act_y act_x1T act_q act_k act_nmT act_exp "
                 "act_oT act_onT act_x2T dve_max dve_nmp dve_nm dve_on dve_rden dve_h dve_st1 dve_mv1 dve_x1 dve_q dve_k dve_q3 dve_k3 pool_q pool_k dve_v "
                 "dve_yb dve_st2 dve_mv2 dve_yn dve_st3 dve_mv3 dve_x2 dve_lg pool_rs1 pool_rs2 pool_rs3 "
                 "ld_xs20 ld_xs21 st_g2 st_qk0 st_qk1 ld_qk0 ld_qk1 ld_mx0 ld_mx1 pool_var1 pool_var2 pool_var3 pool_ln pool_h2 pool_r st_acc "
                 "r_dve r_ls r_exp r_cnt pe_rank pe_tot r_slot r_gate1 r_gate2 r_tab sc1 sc2 "
                 "m_x0 m_x1 m_wa0 m_wa1 m_wb0 m_wb1 m_b0 m_b1 m_tr m_xT m_s1 m_gelu m_s2 m_y m_yg m_add m_meta0 m_meta1 out_done").split()
        s = {n: sem(n) for n in names}

        N_QK = 16 * 2 * len(QPART)
        n_const = 16 * 16

        block = ctx.enter_context(nc.Block())

        def over_images(eng, step):
            step(-1, 1, True, False, False)
            step(0, 0, True, True, False)
            step(1, 1, True, True, True)
            step(2, 0, True, True, True)
            with eng.Fori(1, B // 2 - 2) as k:
                step(2 * k + 1, 1, True, True, True)
                step(2 * k + 2, 0, True, True, True)
            step(B - 3, (B - 3) % 2, True, True, True)
            step(B - 2, (B - 2) % 2, True, True, True)
            step(B - 1, (B - 1) % 2, False, True, True)
            step(B, B % 2, False, False, True)

        def apart(eng):
            eng.wait_ge(s["ld_const"], n_const)

        def more(n):
            return not isinstance(n, int) or n + 1 < B

        def half(i, p):
            return (i - p) // 2

        def wait_prev(eng, which, count):
            if not (isinstance(count, int) and count <= 0):
                eng.wait_ge(which, count)

        def moe_loads(sp):
            sp.wait_ge(s["r_tab"], 1)
            sp.wait_ge(s["sc2"], 16 * NT)
            sp.wait_ge(s["sc1"], 16 * NT)

            def load(t, k, p):
                e = sp.value_load(tab[0:1, ds(t, 1)], min_val=0, max_val=NE - 1)
                wait_prev(sp, s["m_tr"], t - 1)
                sp.dma_start(xt[p][:, :], xs_d[ds(t * P, P), 0:E]).then_inc(s[f"m_x{p}"], 16)
                wait_prev(sp, s["m_s1"], t - 1)
                sp.dma_start(w1b[p][0:KH, :, :], ew1[ds(e, 1), :, :].rearrange("a (c p) f -> p (a c) f", p=KH)) \
                    .then_inc(s[f"m_wa{p}"], 16)
                sp.dma_start(w1b[p][KH:KH + 1, 1, :], eb1[ds(e, 1), :]).then_inc(s[f"m_wa{p}"], 16)
                wait_prev(sp, s["m_s2"], t - 1)
                sp.dma_start(w2b[p][:, :, :], ew2[ds(e, 1), :, :].rearrange("a (c p) d -> p (a c) d", p=P)) \
                    .then_inc(s[f"m_wb{p}"], 16)
                wait_prev(sp, s["m_y"], t - 1)
                sp.dma_start(b2b[p][:, :], eb2[ds(e, 1), :].rearrange("a d -> (a d)").partition_broadcast(P)) \
                    .then_inc(s[f"m_b{p}"], 16)

            load(0, 0, 0)
            load(1, 0, 1)
            with sp.Fori(1, NTILE // 2) as k:
                load(2 * k, k, 0)
                load(2 * k + 1, k, 1)
            load(NTILE - 1, NTILE // 2, 0)
            sp.wait_ge(s["m_add"], 16 * NTILE)
            sp.dma_start(out.rearrange("b t e -> (b t) e"), acc_d[0:NT * P, :]).then_inc(s["out_done"], 16)
            sp.wait_ge(s["out_done"], 16)

        def moe_tensor(pe):
            pe.wait_ge(s["r_cnt"], 1)
            f = r_cnt[:, :, :].rearrange("p t e -> p (t e)")
            nc.tensor.matmul(M0, tri[:, :], f, start=True, stop=True).then_inc(s["pe_rank"], 1)
            nc.tensor.matmul(M1, ones[:, :], f, start=True, stop=True).then_inc(s["pe_tot"], 1)

            def rows_T(t, k, p):
                pe.wait_ge(s[f"m_x{p}"], 16 * k + 16)
                wait_prev(pe, s["m_xT"], t - 1)
                for c in range(2):
                    last = nc.tensor.matmul(XT[p][0:KH, c * P:(c + 1) * P], xt[p][:, c * KH:(c + 1) * KH],
                                            ident[:, :], start=True, stop=True, is_transpose=True)
                last.then_inc(s["m_tr"], 1)

            def up(t, k, p):
                pe.wait_ge(s["m_xT"], t + 1)
                pe.wait_ge(s[f"m_wa{p}"], 32 * k + 32)
                wait_prev(pe, s["m_gelu"], t - 1)
                for c in range(FC):
                    o = H[p][:, c * P:(c + 1) * P]
                    nc.tensor.matmul(o, w1b[p][0:KH, 0, c * P:(c + 1) * P], xtT[p][0:KH, 0, :], start=True, stop=False)
                    last = nc.tensor.matmul(o, w1b[p][:, 1, c * P:(c + 1) * P], xtT[p][:, 1, :],
                                            start=False, stop=True)
                last.then_inc(s["m_s1"], 1)

            def down(t, k, p):
                pe.wait_ge(s["m_gelu"], t + 1)
                pe.wait_ge(s[f"m_wb{p}"], 16 * k + 16)
                wait_prev(pe, s["m_y"], t - 1)
                for c in range(FC):
                    last = nc.tensor.matmul(Y[p], hT[p][:, c * P:(c + 1) * P], w2b[p][:, c, :],
                                            start=(c == 0), stop=(c == FC - 1))
                last.then_inc(s["m_s2"], 1)

            rows_T(0, 0, 0)
            rows_T(1, 0, 1)
            up(0, 0, 0)
            up(1, 0, 1)
            rows_T(2, 1, 0)
            down(0, 0, 0)
            up(2, 1, 0)
            rows_T(3, 1, 1)
            down(1, 0, 1)
            with pe.Fori(1, (NTILE - 3) // 2) as k:
                up(2 * k + 1, k, 1)
                rows_T(2 * k + 2, k + 1, 0)
                down(2 * k, k, 0)
                up(2 * k + 2, k + 1, 0)
                rows_T(2 * k + 3, k + 1, 1)
                down(2 * k + 1, k, 1)
            t = NTILE - 3
            up(t + 1, t // 2, 1)
            rows_T(t + 2, t // 2 + 1, 0)
            down(t, t // 2, 0)
            up(t + 2, t // 2 + 1, 0)
            down(t + 1, t // 2, 1)
            down(t + 2, t // 2 + 1, 0)

        def moe_scalar(act):
            act.wait_ge(s["r_ls"], 1)
            nc.scalar.activation(r_p[:, :, :], r_ls[:, :, :], ACT.Exp).then_inc(s["r_exp"], 1)

            def gelu(t, k, p):
                act.wait_ge(s["m_s1"], t + 1)
                wait_prev(act, s["m_s2"], t - 1)
                nc.scalar.activation(hT[p][:, :], H[p], ACT.Gelu).then_inc(s["m_gelu"], 1)

            gelu(0, 0, 0)
            gelu(1, 0, 1)
            with act.Fori(1, NTILE // 2) as k:
                gelu(2 * k, k, 0)
                gelu(2 * k + 1, k, 1)
            gelu(NTILE - 1, NTILE // 2, 0)

        def moe_vector(dve):
            done = [0]

            def then(ins):
                done[0] += 1
                ins.then_inc(s["r_dve"], 1)
                dve.wait_ge(s["r_dve"], done[0])

            def over_e(a):
                return a.unsqueeze(2).to_broadcast([P, NT, NE])

            V = nc.vector
            for p in range(2):
                V.memset(xtT[p][KH:KH + 1, :, :], 1.0)
            dve.wait_ge(s["dve_lg"], B)
            then(V.tensor_reduce(r_mx[:, :], lg[:, :, :], AX.X, ALU.max))
            V.tensor_tensor(r_ls[:, :, :], lg[:, :, :], over_e(r_mx[:, :]), ALU.subtract).then_inc(s["r_ls"], 1)
            dve.wait_ge(s["r_exp"], 1)
            then(V.tensor_reduce(r_sum[:, :], r_p[:, :, :], AX.X, ALU.add))
            then(V.reciprocal(r_mx[:, :], r_sum[:, :]))
            then(V.tensor_tensor(r_p[:, :, :], r_p[:, :, :], over_e(r_mx[:, :]), ALU.mult))
            for k in range(TOPK):
                then(V.tensor_reduce(r_gate[k][:, :], r_p[:, :, :], AX.X, ALU.max))
                then(V.tensor_tensor(r_eq[:, :, :], r_p[:, :, :], over_e(r_gate[k][:, :]), ALU.is_equal))
                then(V.scalar_tensor_tensor(r_key[:, :, :], r_eq[:, :, :], -float(NE),
                                            iota[:, 0:NE].unsqueeze(1).to_broadcast([P, NT, NE]), ALU.mult, ALU.add))
                then(V.tensor_reduce(r_km[:, :], r_key[:, :, :], AX.X, ALU.min))
                then(V.tensor_tensor(r_hot[k][:, :, :], r_key[:, :, :], over_e(r_km[:, :]), ALU.is_equal))
                if k == 0:
                    then(V.scalar_tensor_tensor(r_p[:, :, :], r_hot[0][:, :, :], -2.0, r_p[:, :, :],
                                                ALU.mult, ALU.add))
            V.tensor_tensor(r_cnt[:, :, :], r_hot[0][:, :, :], r_hot[1][:, :, :], ALU.add).then_inc(s["r_cnt"], 1)
            V.tensor_copy(xrow[:, :, GATE], r_gate[0][:, :]).then_inc(s["r_gate1"], 1)
            dve.wait_ge(s["pe_tot"], 1)
            tot = M1.rearrange("p (t e) -> p t e", e=NE)
            then(V.tensor_copy(r_ta[0][:, :, :], tot))
            a, b, sh = 0, 1, 1
            while sh < NT:
                V.tensor_copy(r_ta[b][:, 0:sh, :], r_ta[a][:, 0:sh, :])
                then(V.tensor_tensor(r_ta[b][:, sh:NT, :], r_ta[a][:, sh:NT, :], r_ta[a][:, 0:NT - sh, :], ALU.add))
                a, b, sh = b, a, 2 * sh
            then(V.tensor_scalar(r_ci[:, :], r_ta[a][:, NT - 1, :], float(P - 1), None, ALU.add))
            then(V.tensor_scalar(r_ti[:, :], r_ci[:, :], P.bit_length() - 1, None, ALU.arith_shift_right))
            then(V.tensor_copy(r_tn[:, :], r_ti[:, :]))
            then(V.tensor_copy(r_te[0][:, :], r_tn[:, :]))
            c, d, sh = 0, 1, 1
            while sh < NE:
                V.tensor_copy(r_te[d][:, 0:sh], r_te[c][:, 0:sh])
                then(V.tensor_tensor(r_te[d][:, sh:NE], r_te[c][:, sh:NE], r_te[c][:, 0:NE - sh], ALU.add))
                c, d, sh = d, c, 2 * sh
            then(V.tensor_tensor(r_base[:, :], r_te[c][:, :], r_tn[:, :], ALU.subtract))
            then(V.scalar_tensor_tensor(r_sl[:, :, :], r_base[:, :].unsqueeze(1).to_broadcast([P, NT, NE]), float(P),
                                        r_ta[a][:, :, :], ALU.mult, ALU.add))
            then(V.tensor_tensor(r_sl[:, :, :], r_sl[:, :, :], tot, ALU.subtract))
            dve.wait_ge(s["pe_rank"], 1)
            then(V.tensor_tensor(r_sl[:, :, :], r_sl[:, :, :], M0.rearrange("p (t e) -> p t e", e=NE), ALU.add))
            for k in range(TOPK):
                then(V.tensor_tensor(r_eq[:, :, :], r_sl[:, :, :], r_hot[k][:, :, :], ALU.mult))
                then(V.tensor_reduce(r_slf[:, :], r_eq[:, :, :], AX.X, ALU.add))
                ins = V.tensor_copy(slot[k][:, :], r_slf[:, :])
                then(ins) if k == 0 else ins.then_inc(s["r_slot"], 1)
            then(V.tensor_tensor(r_tt[:, :, :], r_te[c][:, :].unsqueeze(1).to_broadcast([P, NTILE, NE]),
                                 iota[:, :].unsqueeze(2).to_broadcast([P, NTILE, NE]), ALU.is_le))
            then(V.tensor_reduce(r_tf[:, :], r_tt[:, :, :], AX.X, ALU.add))
            V.tensor_scalar(tab[:, :], r_tf[:, :], float(NE - 1), None, ALU.min).then_inc(s["r_tab"], 1)
            dve.wait_ge(s["sc1"], 16 * NT)
            V.tensor_copy(xrow[:, :, GATE], r_gate[1][:, :]).then_inc(s["r_gate2"], 1)

            def rows_T(t, k, p):
                dve.wait_ge(s["m_tr"], t + 1)
                wait_prev(dve, s["m_s1"], t - 1)
                V.tensor_copy(xtT[p][0:KH, :, :], XT[p][0:KH, 0:2 * P].rearrange("p (c t) -> p c t", c=2)) \
                    .then_inc(s["m_xT"], 1)

            def biased(t, k, p):
                dve.wait_ge(s["m_s2"], t + 1)
                dve.wait_ge(s[f"m_b{p}"], 16 * k + 16)
                wait_prev(dve, s["m_yg"], t - 1)
                V.tensor_tensor(ysum[p][:, :], Y[p], b2b[p][:, :], ALU.add).then_inc(s["m_y"], 1)

            rows_T(0, 0, 0)
            rows_T(1, 0, 1)
            rows_T(2, 1, 0)
            biased(0, 0, 0)
            rows_T(3, 1, 1)
            biased(1, 0, 1)
            with dve.Fori(1, (NTILE - 3) // 2) as k:
                rows_T(2 * k + 2, k + 1, 0)
                biased(2 * k, k, 0)
                rows_T(2 * k + 3, k + 1, 1)
                biased(2 * k + 1, k, 1)
            t = NTILE - 3
            rows_T(t + 2, t // 2 + 1, 0)
            biased(t, t // 2, 0)
            biased(t + 1, t // 2, 1)
            biased(t + 2, t // 2 + 1, 0)

        def moe_gpsimd(pool):
            pool.wait_ge(s["ld_pad"], 32)
            pool.wait_ge(s["r_slot"], 1)
            pool.wait_ge(s["r_gate1"], 1)
            pool.wait_ge(s["pool_r"], B)
            for t in range(NT):
                nc.gpsimd.indirect_dma_start(xs_d, bass.IndirectOffsetOnAxis(slot[0][:, t:t + 1], 0),
                                             xrow[:, t, :], None).then_inc(s["sc1"], 16)
            pool.wait_ge(s["r_gate2"], 1)
            for t in range(NT):
                nc.gpsimd.indirect_dma_start(xs_d, bass.IndirectOffsetOnAxis(slot[1][:, t:t + 1], 0),
                                             xrow[:, t, :], None).then_inc(s["sc2"], 16)
            pool.wait_ge(s["st_acc"], 16)

            def load_meta(t, p):
                pool.dma_start(meta[p][:, :], xs_d[ds(t * P, P), E:ROW]).then_inc(s[f"m_meta{p}"], 16)

            def add(t, k, p, more=True):
                pool.wait_ge(s["m_y"], t + 1)
                pool.wait_ge(s[f"m_meta{p}"], 16 * k + 16)
                wait_prev(pool, s["m_add"], 16 * t)
                nc.gpsimd.tensor_tensor(yg8[p][:, :], ysum[p][:, :], meta[p][:, 1:2].to_broadcast([P, E]),
                                        ALU.mult).then_inc(s["m_yg"], 1)
                if more:
                    load_meta(t + 1, 1 - p)
                apart(pool)
                pool.wait_ge(s["m_yg"], t + 1)
                nc.gpsimd.indirect_dma_start(acc_d, bass.IndirectOffsetOnAxis(meta[p][:, 0:1].bitcast(i32), 0),
                                             yg8[p][:, :], None, compute_op=ALU.add).then_inc(s["m_add"], 16)

            pool.wait_ge(s["sc2"], 16 * NT)
            pool.wait_ge(s["sc1"], 16 * NT)
            load_meta(0, 0)
            add(0, 0, 0)
            add(1, 0, 1)
            with pool.Fori(1, NTILE // 2) as k:
                add(2 * k, k, 0)
                add(2 * k + 1, k, 1)
            add(NTILE - 1, NTILE // 2, 0, more=False)

        @block.sync
        def _(sp):
            sp.dma_start(i0[:, :, :], idx0.rearrange("(c p g) -> p c g", c=TT, g=GP)).then_inc(s["ld_idx0"], 16)
            sp.dma_start(i2[:, :], idx2.rearrange("(p c) -> p c", p=P)).then_inc(s["ld_idx2"], 16)
            sp.dma_start(i1[:, :], idx1.rearrange("(p g) -> p g", g=GP)).then_inc(s["ld_idx1"], 16)
            consts = [
                (ident[:, :], c_ident), (tri[:, :], c_tri), (iota[:, :], c_iota),
                (w1s[:, :, :], w1t.rearrange("(c p) e -> p c e", p=KH)),
                (w2s[:, :, :], w2t.rearrange("(c p) e -> p c e", p=KH)),
                (bias01[:, :], b012[0:P, :]), (bias2[:, :], b012[P:P + EM, :]),
                (wfa[:, :], wft[0:P, :]), (wfb[0:EM, :], wft[P:E, :]), (wfb[EM:EM + 1, :], bf),
                (wqkv[:, :, :], w_qkv.rearrange("(c p) n -> p c n", p=KH)),
                (wo[:, :, :], w_out.rearrange("(c p) n -> p c n", p=KH)),
                (wr[:, :, :], wrt.rearrange("(c p) n -> p c n", p=KH)),
                (bout_b[:, :], b_out.partition_broadcast(P)), (lng_b[:, :], ln_g.partition_broadcast(P)),
                (lnb_b[:, :], ln_b.partition_broadcast(P)),
            ]
            for dst, src in consts:
                sp.dma_start(dst, src).then_inc(s["ld_const"], 16)
            sp.wait_ge(s["dve_init"], 1)
            for dst, src in ((bd[0:GP * C0, 0:EM], w0t), (rr[P - T1:P, :], c_interp1), (rr2[0:T2, :], c_interp2)):
                sp.dma_start(dst, src).then_inc(s["ld_w"], 16)
            sp.wait_ge(s["pool_init"], 3)
            sp.dma_start(xs_d.rearrange("(t p) n -> p t n", p=P),
                         padrow[:, :].unsqueeze(1).to_broadcast([P, NTILE, ROW])).then_inc(s["ld_pad"], 16)
            sp.dma_start(acc_d[NT * P:NT * P + P, :], padrow[:, 0:E]).then_inc(s["ld_pad"], 16)

            def a_mx(i, p, v):
                sp.wait_ge(s["act_nmT"], 2 * i + v + 1)
                for part in range(NPART):
                    sp.dma_start(qs[p][KS + part:KS + part + 1, v * HH:(v + 1) * HH, :],
                                 nmT[part * HH:(part + 1) * HH, v, :]).then_inc(s[f"ld_mx{v}"], 16)

            def f_qk(n, p, m):
                apart(sp)
                sp.wait_ge(s["dve_k3"], n + 1)
                wait_prev(sp, s["pe_st"], U * (n - 1))
                sp.dma_start(qk_d[p].rearrange("a b (c r) t -> r a b c t", r=KH), qk[:, :, :, :, :]) \
                    .then_inc(s[f"st_qk{p}"], 16)
                sp.wait_ge(s[f"st_qk{p}"], 16 * m + 16)
                for dst, a, parts in ((qs[p], 0, QPART), (ks[p], 1, KPART)):
                    for r, b in enumerate(parts):
                        sp.dma_start(dst[r * HD:(r + 1) * HD, :, :],
                                     qk_d[p, a, b].rearrange("(h d) t -> d h t", d=HD)) \
                            .then_inc(s[f"ld_qk{p}"], 16)

            def f_xs2(n, p):
                wait_prev(sp, s["pe_xT"], n - 1)
                sp.dma_start(xs2[p][:, :, :], g2_d.rearrange("(t g) (b c) -> b t g c", g=GP, c=C2)[ds(n, 1)]
                             .rearrange("a t g c -> (a t) g c")).then_inc(s[f"ld_xs2{p}"], 16)

            def step(i, p, tok, att, clo):
                if tok and more(i + 1):
                    f_xs2(i + 2, p)
                if att:
                    a_mx(i, p, 0)
                    a_mx(i, p, 1)
                if tok:
                    f_qk(i + 1, 1 - p, half(i + 1, 1 - p))

            sp.wait_ge(s["ga2"], 16 * (T2 * GP // P))
            sp.dma_start(g2_d.rearrange("(p c) n -> p c n", p=P), g2[:, :, :]).then_inc(s["st_g2"], 16)
            sp.wait_ge(s["st_g2"], 16)
            f_xs2(0, 0)

            over_images(sp, step)
            sp.wait_ge(s["pool_r"], B)
            sp.dma_start(acc_d[0:NT * P, :].rearrange("(t p) e -> p t e", p=P), hr[:, :, :]).then_inc(s["st_acc"], 16)
            moe_loads(sp)

        @block.tensor
        def _(pe):
            pe.wait_ge(s["ld_const"], n_const)
            pe.wait_ge(s["ld_w"], 48)
            pe.wait_ge(s["dve_init"], 3)

            def transpose(dst, src, n):
                return nc.tensor.matmul(dst, src, ident[0:n, 0:n], start=True, stop=True, is_transpose=True)

            def f_xT(n, p):
                if isinstance(n, int) and n == 0:
                    pe.wait_ge(s["pool_xs"], 1)
                    pe.wait_ge(s["ld_xs20"], 16)
                for c in range(TT):
                    transpose(M0[0:GP * C0, c * P:(c + 1) * P], xs0[:, c, :, :].rearrange("p g c -> p (g c)"), P)
                f = xs1[:, :, :].rearrange("p g c -> p (g c)")
                for c in range(NX1):
                    transpose(M0[0:KH, T + c * T1:T + (c + 1) * T1], f[:, c * KH:(c + 1) * KH], T1)
                f = xs2[p][:, :, :].rearrange("p g c -> p (g c)")
                at = T + NX1 * T1
                for c in range(NX2):
                    last = transpose(M0[0:KH, at + c * T2:at + (c + 1) * T2], f[:, c * KH:(c + 1) * KH], T2)
                last.then_inc(s["pe_xT"], 1)

            def f_o12(n):
                pe.wait_ge(s["act_xT"], n + 1)
                for c in range(NX1):
                    nc.tensor.matmul(M0[P - T1:P, 0:EM], x12T[:, c * T1:(c + 1) * T1], w1s[:, c, :],
                                     start=(c == 0), stop=(c == NX1 - 1))
                at = NX1 * T1
                for c in range(NX2):
                    last = nc.tensor.matmul(M0[0:T2, EM:2 * EM], x12T[:, at + c * T2:at + (c + 1) * T2],
                                            w2s[:, c, :], start=(c == 0), stop=(c == NX2 - 1))
                last.then_inc(s["pe_o12"], 1)

            def f_y(n):
                pe.wait_ge(s["act_o12"], n + 1)
                nc.tensor.matmul(M0[:, 0:T], bd[:, :], rr[:, :], start=True, stop=True)
                nc.tensor.matmul(M0[0:EM, T:2 * T], bd2[:, :], rr2[:, :], start=True, stop=True) \
                    .then_inc(s["pe_y"], 1)

            def f_h(n):
                pe.wait_ge(s["act_y"], n + 1)
                for c in range(TT):
                    o = M0[:, c * E:(c + 1) * E]
                    nc.tensor.matmul(o, y01[:, c * P:(c + 1) * P], wfa[:, :], start=True, stop=False)
                    last = nc.tensor.matmul(o, y2[:, c * P:(c + 1) * P], wfb[:, :], start=False, stop=True)
                last.then_inc(s["pe_h"], 1)

            def f_x1T(n):
                pe.wait_ge(s["dve_x1"], n + 1)
                for c in range(2):
                    for t in range(TT):
                        last = transpose(M0[0:KH, (c * TT + t) * P:(c * TT + t + 1) * P],
                                         xn1[:, t, c * KH:(c + 1) * KH], P)
                last.then_inc(s["pe_x1T"], 1)

            def f_qk(n, which, free, done):
                pe.wait_ge(free, n + 1)
                for h in range(2):
                    at = which * E + h * KH
                    for c in range(2):
                        last = nc.tensor.matmul(M0[0:KH, h * T:(h + 1) * T], wqkv[:, c, at:at + KH], x1T[:, c, :],
                                                start=(c == 0), stop=(c == 1))
                last.then_inc(done, 1)

            def f_v(n):
                pe.wait_ge(s["dve_k"], n + 1)
                for t in range(TT):
                    for c in range(2):
                        last = nc.tensor.matmul(M0[:, t * E:(t + 1) * E], x1T[:, c, t * P:(t + 1) * P],
                                                wqkv[:, c, 2 * E:3 * E], start=(c == 0), stop=(c == 1))
                last.then_inc(s["pe_v"], 1)

            def a_s(i, p, u):
                if u == 0:
                    pe.wait_ge(s[f"ld_qk{p}"], N_QK * half(i, p) + N_QK)
                wait_prev(pe, s["dve_max"], U * i + u)
                for t in range(TT):
                    for a in range(HU):
                        h = HU * u + a
                        last = nc.tensor.matmul(S[:, a, t * T:(t + 1) * T], qs[p][0:KS, h, t * P:(t + 1) * P],
                                                ks[p][0:KS, h, :], start=True, stop=True)
                last.then_inc(s["pe_s"], 1)

            def a_nmT(i, v):
                pe.wait_ge(s["dve_nm"], 2 * i + v + 1)
                for t in range(TT):
                    last = nc.tensor.matmul(M1[0:NPART * HH, t * P:(t + 1) * P],
                                            nm[:, v, t, :, :].rearrange("p a h -> p (a h)"), ident16[:, :],
                                            start=True, stop=True)
                last.then_inc(s["pe_nmT"], 1)

            def a_st(i, p, u):
                if u % 2 == 0:
                    pe.wait_ge(s[f"ld_mx{u // 2}"], 16 * NPART * (i + 1))
                wait_prev(pe, s["act_exp"], U * i + u)
                for t in range(TT):
                    for a in range(HU):
                        h = HU * u + a
                        last = nc.tensor.matmul(ST[:, a, t * T:(t + 1) * T], ks[p][:, h, t * P:(t + 1) * P],
                                                qs[p][:, h, :], start=True, stop=True)
                last.then_inc(s["pe_st"], 1)

            def a_pv(i, p, u):
                if u == 0:
                    pe.wait_ge(s["dve_v"], i + 1)
                pe.wait_ge(s["act_exp"], U * i + u + 1)
                for t in range(TT):
                    for a in range(HU):
                        last = nc.tensor.matmul(M1[32 * a:32 * a + 32, 0:T], v[p][:, t, HU * u + a, :],
                                                pT[u % 2][:, a, t * T:(t + 1) * T],
                                                start=(t == 0), stop=(t == TT - 1))
                last.then_inc(s["pe_pv"], 1)

            def b_oT(j, t):
                if t == 0:
                    pe.wait_ge(s["act_oT"], U * j + U)
                else:
                    pe.wait_ge(s["dve_on"], TT * j + t)
                for u in range(U):
                    last = transpose(M1[:, u * HU * 32:(u + 1) * HU * 32], oT[:, u, t * P:(t + 1) * P], HU * 32)
                last.then_inc(s["pe_oT"], 1)

            def b_onT(j):
                pe.wait_ge(s["dve_on"], TT * j + TT)
                for c in range(2):
                    for t in range(TT):
                        f = on[:, t, :, :].rearrange("p h d -> p (h d)")
                        last = transpose(M1[0:KH, (c * TT + t) * P:(c * TT + t + 1) * P],
                                         f[:, c * KH:(c + 1) * KH], P)
                last.then_inc(s["pe_onT"], 1)

            def b_y(j):
                pe.wait_ge(s["act_onT"], j + 1)
                for t in range(TT):
                    for c in range(2):
                        last = nc.tensor.matmul(M1[:, t * E:(t + 1) * E],
                                                onT[:, (c * TT + t) * P:(c * TT + t + 1) * P], wo[:, c, :],
                                                start=(c == 0), stop=(c == 1))
                last.then_inc(s["pe_yat"], 1)

            def b_x2T(j):
                pe.wait_ge(s["dve_x2"], j + 1)
                for c in range(2):
                    for t in range(TT):
                        last = transpose(M1[0:KH, (c * TT + t) * P:(c * TT + t + 1) * P],
                                         x2c[:, t, c * KH:(c + 1) * KH], P)
                last.then_inc(s["pe_x2T"], 1)

            def b_lg(j):
                pe.wait_ge(s["act_x2T"], j + 1)
                for t in range(TT):
                    for c in range(2):
                        last = nc.tensor.matmul(M1[:, t * NE:(t + 1) * NE],
                                                x2T[:, (c * TT + t) * P:(c * TT + t + 1) * P], wr[:, c, :],
                                                start=(c == 0), stop=(c == 1))
                last.then_inc(s["pe_lg"], 1)

            def step(i, p, tok, att, clo):
                n, j = i + 1, i - 1
                if tok:
                    f_xT(n, 1 - p)
                if clo:
                    b_oT(j, 0)
                if att:
                    a_s(i, p, 0)
                if clo:
                    b_oT(j, 1)
                if tok:
                    f_o12(n)
                if att:
                    a_s(i, p, 1)
                if clo:
                    b_onT(j)
                if tok:
                    f_y(n)
                if att:
                    if clo:
                        pe.wait_ge(s["act_onT"], j + 1)
                    a_nmT(i, 0)
                    a_s(i, p, 2)
                if tok:
                    f_h(n)
                if clo:
                    if att:
                        pe.wait_ge(s["act_nmT"], 2 * i + 1)
                    b_y(j)
                if att:
                    a_s(i, p, 3)
                    pe.wait_ge(s["dve_yb"], j + 1) if clo else pe.wait_ge(s["act_nmT"], 2 * i + 1)
                    a_nmT(i, 1)
                if tok:
                    f_x1T(n)
                if att:
                    a_st(i, p, 0)
                if tok:
                    f_qk(n, 0, s["act_x1T"], s["pe_q"])
                if att:
                    pe.wait_ge(s["act_nmT"], 2 * i + 2)
                    a_pv(i, p, 0)
                    a_st(i, p, 1)
                if tok:
                    f_qk(n, 1, s["dve_q"], s["pe_k"])
                if att:
                    pe.wait_ge(s["act_oT"], U * i + 1)
                    a_pv(i, p, 1)
                    a_st(i, p, 2)
                if clo:
                    pe.wait_ge(s["act_oT"], U * i + 2) if att else pe.wait_ge(s["dve_yb"], j + 1)
                    b_x2T(j)
                if att:
                    pe.wait_ge(s["act_x2T"], j + 1) if clo else pe.wait_ge(s["act_oT"], U * i + 2)
                    a_pv(i, p, 2)
                    a_st(i, p, 3)
                if tok:
                    if more(n):
                        pe.wait_ge(s[f"ld_xs2{p}"], 16 * half(n + 1, p) + 16)
                        pe.wait_ge(s["pool_xs"], n + 2)
                    f_v(n)
                if clo:
                    if att:
                        pe.wait_ge(s["act_oT"], U * i + 3)
                    b_lg(j)
                if att:
                    pe.wait_ge(s["dve_lg"], j + 1) if clo else pe.wait_ge(s["act_oT"], U * i + 3)
                    a_pv(i, p, 3)
                if tok:
                    apart(pe)
                    pe.wait_ge(s["dve_v"], n + 1)

            over_images(pe, step)
            moe_tensor(pe)

        @block.scalar
        def _(act):
            act.wait_ge(s["ld_const"], n_const)

            def f_xT(n):
                act.wait_ge(s["pe_xT"], n + 1)
                wait_prev(act, s["pe_y"], n)
                nc.scalar.activation(rr[0:GP * C0, :], M0[0:GP * C0, 0:T], ACT.Copy)
                nc.scalar.activation(x12T[:, :], M0[0:KH, T:2 * T], ACT.Copy).then_inc(s["act_xT"], 1)

            def f_o12(n):
                act.wait_ge(s["pe_o12"], n + 1)
                nc.scalar.activation(bd[P - T1:P, EM:2 * EM], M0[P - T1:P, 0:EM], ACT.Copy)
                nc.scalar.activation(bd2[0:T2, :], M0[0:T2, EM:2 * EM], ACT.Copy) \
                    .then_inc(s["act_o12"], 1)

            def f_y(n):
                act.wait_ge(s["pe_y"], n + 1)
                wait_prev(act, s["pe_h"], n)
                nc.scalar.activation(y01[:, :], M0[:, 0:T], ACT.Identity, bias=bias01[:, :])
                nc.scalar.activation(y2[0:EM, :], M0[0:EM, T:2 * T], ACT.Identity, bias=bias2[:, :]) \
                    .then_inc(s["act_y"], 1)

            def f_x1T(n):
                act.wait_ge(s["pe_x1T"], n + 1)
                wait_prev(act, s["pe_v"], n)
                nc.scalar.activation(x1T[:, :, :].rearrange("p c t -> p (c t)"), M0[0:KH, :], ACT.Copy) \
                    .then_inc(s["act_x1T"], 1)

            def f_qk(n, p, which, scale, ready, done):
                act.wait_ge(ready, n + 1)
                if which == 0:
                    wait_prev(act, s[f"st_qk{1 - p}"], 16 * half(n + 1, 1 - p))
                nc.scalar.activation(qk[:, which, 0, :, :].rearrange("p h t -> p (h t)"), M0[0:KH, :], ACT.Copy,
                                     scale=scale).then_inc(done, 1)

            def a_nmT(i, v):
                act.wait_ge(s["pe_nmT"], 2 * i + v + 1)
                nc.scalar.activation(nmT[:, v, :], M1[0:NPART * HH, 0:T], ACT.Copy).then_inc(s["act_nmT"], 1)

            def a_exp(i, u):
                act.wait_ge(s["pe_st"], U * i + u + 1)
                wait_prev(act, s["pe_pv"], U * i + u - 1)
                nc.scalar.activation(pT[u % 2][:, :, :], ST[:, :, :], ACT.Exp).then_inc(s["act_exp"], 1)

            def a_oT(i, u):
                act.wait_ge(s["pe_pv"], U * i + u + 1)
                if u == 0:
                    wait_prev(act, s["pe_oT"], TT * i)
                nc.scalar.activation(oT[:, u, :], M1[0:HU * 32, 0:T], ACT.Copy).then_inc(s["act_oT"], 1)

            def b_onT(j):
                act.wait_ge(s["pe_onT"], j + 1)
                wait_prev(act, s["pe_yat"], j)
                nc.scalar.activation(onT[:, :], M1[0:KH, :], ACT.Copy).then_inc(s["act_onT"], 1)

            def b_x2T(j):
                act.wait_ge(s["pe_x2T"], j + 1)
                wait_prev(act, s["pe_lg"], j)
                nc.scalar.activation(x2T[:, :], M1[0:KH, :], ACT.Copy).then_inc(s["act_x2T"], 1)

            def step(i, p, tok, att, clo):
                n, j = i + 1, i - 1
                if tok:
                    f_xT(n)
                    f_o12(n)
                if clo:
                    b_onT(j)
                if tok:
                    f_y(n)
                if att:
                    a_nmT(i, 0)
                    a_nmT(i, 1)
                if tok:
                    f_x1T(n)
                if att:
                    a_exp(i, 0)
                if tok:
                    f_qk(n, 1 - p, 0, SCALE, s["pe_q"], s["act_q"])
                if att:
                    a_oT(i, 0)
                    a_exp(i, 1)
                if tok:
                    f_qk(n, 1 - p, 1, 1.0, s["pe_k"], s["act_k"])
                if att:
                    a_oT(i, 1)
                    a_exp(i, 2)
                if clo:
                    b_x2T(j)
                if att:
                    a_oT(i, 2)
                    a_exp(i, 3)
                    a_oT(i, 3)

            over_images(act, step)
            moe_scalar(act)

        @block.vector
        def _(dve):
            for a in (bd, rr, bd2):
                nc.vector.memset(a[:, :], 0.0)
            nc.vector.memset(rr2[:, :], 0.0).then_inc(s["dve_init"], 1)
            for p in range(2):
                nc.vector.memset(v[p][:, :, :, :], 1.0)
                nc.vector.memset(ks[p][KS:KM, :, :], 1.0)
            nc.vector.memset(ones[:, :], 1.0)
            nc.vector.memset(y2[EM:EM + 1, :], 1.0).then_inc(s["dve_init"], 1)
            dve.wait_ge(s["dve_init"], 2)
            dve.wait_ge(s["ld_const"], n_const)
            nc.vector.tensor_copy(ident16[:, :], ident[:, :]).then_inc(s["dve_init"], 1)

            def norm_stats(src, st, mv, done_st, done_mv, n):
                for t in range(TT):
                    last = nc.vector.bn_stats(st[:, t, :], src(t))
                last.then_inc(done_st, 1)
                apart(dve)
                dve.wait_ge(done_st, n + 1)
                for t in range(TT):
                    last = nc.vector.bn_aggr(mv[:, t, :], st[:, t, :])
                last.then_inc(done_mv, 1)

            def normalize(dst, src, mv, rs):
                for t in range(TT):
                    last = nc.vector.tensor_scalar(dst(t), src(t), mv[:, t, 0:1], rs[:, t:t + 1],
                                                   ALU.subtract, ALU.mult)
                return last

            def f_h(n):
                dve.wait_ge(s["pe_h"], n + 1)
                dst = hr[:, ds(TT * n, TT), :]
                nc.vector.tensor_copy(dst, M0[:, 0:TT * E].rearrange("p (t e) -> p t e", e=E)) \
                    .then_inc(s["dve_h"], 1)
                apart(dve)
                dve.wait_ge(s["dve_h"], n + 1)
                wait_prev(dve, s["pool_rs1"], n)
                norm_stats(lambda t: hr[:, ds(TT * n + t, 1), :].rearrange("p a e -> p (a e)"),
                           st1, mv1, s["dve_st1"], s["dve_mv1"], n)

            def f_x1(n):
                dve.wait_ge(s["pool_rs1"], n + 1)
                wait_prev(dve, s["pe_x1T"], n)
                normalize(lambda t: xn1[:, t, :], lambda t: hr[:, ds(TT * n + t, 1), :].rearrange("p a e -> p (a e)"),
                          mv1, rs1).then_inc(s["dve_x1"], 1)

            def f_qk(n, which, scale, ready, done):
                dve.wait_ge(ready, n + 1)
                nc.vector.scalar_tensor_tensor(qkr[which][:, :], M0[0:KH, :], scale,
                                               qk[:, which, 0, :, :].rearrange("p h t -> p (h t)"),
                                               ALU.mult, ALU.subtract).then_inc(done, 1)

            def f_qk3(n, which, ready, done):
                dve.wait_ge(ready, n + 1)
                nc.vector.tensor_tensor(qk[:, which, 2, :, :].rearrange("p h t -> p (h t)"), qkr[which][:, :],
                                        qk[:, which, 1, :, :].rearrange("p h t -> p (h t)"),
                                        ALU.subtract).then_inc(done, 1)

            def f_v(n, p):
                dve.wait_ge(s["pe_v"], n + 1)
                wait_prev(dve, s["pe_pv"], U * (n - 1))
                nc.vector.tensor_copy(v[p][:, :, :, 0:HD],
                                      M0[:, 0:TT * E].rearrange("p (t h d) -> p t h d", t=TT, d=HD)) \
                    .then_inc(s["dve_v"], 1)

            def a_max(i, u):
                dve.wait_ge(s["pe_s"], U * i + u + 1)
                nc.vector.tensor_reduce(negmax[:, :, HU * u:HU * u + HU].rearrange("p t h -> p h t"),
                                        S[:, :, :].rearrange("p a (t k) -> p a t k", t=TT), AX.X, ALU.max,
                                        negate=True).then_inc(s["dve_max"], 1)

            def a_nm(i, v):
                dve.wait_ge(s["dve_max"], U * i + 2 * v + 2)
                wait_prev(dve, s["pe_nmT"], 2 * i)
                m, at = negmax[:, :, v * HH:(v + 1) * HH], NPART * (2 * i + v)
                nc.vector.tensor_copy(nm[:, v, :, 0, :], m).then_inc(s["dve_nmp"], 1)
                dve.wait_ge(s["dve_nmp"], at + 1)
                nc.vector.tensor_tensor(nmr[:, v, :, :], m, nm[:, v, :, 0, :], ALU.subtract).then_inc(s["dve_nmp"], 1)
                dve.wait_ge(s["dve_nmp"], at + 2)
                nc.vector.tensor_copy(nm[:, v, :, 1, :], nmr[:, v, :, :]).then_inc(s["dve_nmp"], 1)
                dve.wait_ge(s["dve_nmp"], at + 3)
                nc.vector.tensor_tensor(nm[:, v, :, 2, :], nmr[:, v, :, :], nm[:, v, :, 1, :], ALU.subtract) \
                    .then_inc(s["dve_nm"], 1)

            def b_on(j, t):
                dve.wait_ge(s["pe_oT"], TT * j + t + 1)
                if t == 0:
                    wait_prev(dve, s["pe_onT"], j)
                m = M1[:, 0:HEADS * 32].rearrange("p (h d) -> p h d", d=32)
                nc.vector.reciprocal(rden[:, t, :], m[:, :, HD]).then_inc(s["dve_rden"], 1)
                dve.wait_ge(s["dve_rden"], TT * j + t + 1)
                nc.vector.tensor_tensor(on[:, t, :, :], m[:, :, 0:HD],
                                        rden[:, t, :].unsqueeze(2).to_broadcast([P, HEADS, HD]), ALU.mult) \
                    .then_inc(s["dve_on"], 1)

            def b_yb(j):
                dve.wait_ge(s["pe_yat"], j + 1)
                nc.vector.tensor_tensor(yb[:, :, :], M1[:, 0:TT * E].rearrange("p (t e) -> p t e", e=E),
                                        bout_b[:, :].unsqueeze(1).to_broadcast([P, TT, E]), ALU.add) \
                    .then_inc(s["dve_yb"], 1)
                apart(dve)
                dve.wait_ge(s["dve_yb"], j + 1)
                norm_stats(lambda t: yb[:, t, :], st2, mv2, s["dve_st2"], s["dve_mv2"], j)

            def b_yn(j):
                dve.wait_ge(s["pool_rs2"], j + 1)
                wait_prev(dve, s["pool_h2"], j)
                normalize(lambda t: yn[:, t, :], lambda t: yb[:, t, :], mv2, rs2).then_inc(s["dve_yn"], 1)

            def b_stats(j):
                apart(dve)
                dve.wait_ge(s["pool_h2"], j + 1)
                wait_prev(dve, s["pool_rs3"], j)
                norm_stats(lambda t: hr[:, ds(TT * j + t, 1), :].rearrange("p a e -> p (a e)"),
                           st3, mv3, s["dve_st3"], s["dve_mv3"], j)

            def b_x2(j):
                dve.wait_ge(s["pool_rs3"], j + 1)
                wait_prev(dve, s["pool_r"], j)
                wait_prev(dve, s["pe_x2T"], j)
                normalize(lambda t: x2c[:, t, :], lambda t: hr[:, ds(TT * j + t, 1), :].rearrange("p a e -> p (a e)"),
                          mv3, rs3).then_inc(s["dve_x2"], 1)

            def b_lg(j):
                dve.wait_ge(s["pe_lg"], j + 1)
                nc.vector.tensor_copy(lg[:, ds(TT * j, TT), :], M1[:, 0:TT * NE].rearrange("p (t e) -> p t e", e=NE)) \
                    .then_inc(s["dve_lg"], 1)

            def step(i, p, tok, att, clo):
                n, j = i + 1, i - 1
                if clo:
                    b_on(j, 0)
                if att:
                    a_max(i, 0)
                if clo:
                    b_on(j, 1)
                if att:
                    a_max(i, 1)
                    a_nm(i, 0)
                    a_max(i, 2)
                if tok:
                    f_h(n)
                if clo:
                    b_yb(j)
                if att:
                    a_max(i, 3)
                    a_nm(i, 1)
                if tok:
                    f_x1(n)
                if clo:
                    b_yn(j)
                if tok:
                    f_qk(n, 0, SCALE, s["act_q"], s["dve_q"])
                if clo:
                    b_stats(j)
                if tok:
                    f_qk3(n, 0, s["pool_q"], s["dve_q3"])
                    f_qk(n, 1, 1.0, s["act_k"], s["dve_k"])
                if clo:
                    b_x2(j)
                if tok:
                    f_qk3(n, 1, s["pool_k"], s["dve_k3"])
                    f_v(n, 1 - p)
                if clo:
                    b_lg(j)

            over_images(dve, step)
            moe_vector(dve)

        @block.gpsimd
        def _(pool):
            nc.gpsimd.memset(mhalf[:, :], -0.5)
            nc.gpsimd.memset(epsc[:, :], EPS)
            nc.gpsimd.memset(padrow[:, :], 0.0).then_inc(s["pool_init"], 1)
            pool.wait_ge(s["pool_init"], 1)
            nc.gpsimd.iota(padrow[:, ID:ID + 1].bitcast(i32), [[0, 1]], base=NT * P, channel_multiplier=1) \
                .then_inc(s["pool_init"], 1)
            nc.gpsimd.iota(xrow[:, :, ID].bitcast(i32), [[P, NT]], base=0, channel_multiplier=1) \
                .then_inc(s["pool_init"], 1)
            pool.wait_ge(s["ld_idx2"], 16)
            for c in range(T2 * GP // P):
                nc.gpsimd.indirect_dma_start(g2[:, c, :], None, x2,
                                             bass.IndirectOffsetOnAxis(i2[:, c:c + 1], 0)).then_inc(s["ga2"], 16)
            pool.wait_ge(s["ld_idx1"], 16)
            for g in range(GP):
                nc.gpsimd.indirect_dma_start(g1[:, g, :], None, x1,
                                             bass.IndirectOffsetOnAxis(i1[:, g:g + 1], 0)).then_inc(s["ga1"], 16)
            pool.wait_ge(s["ld_idx0"], 16)
            for c in range(TT):
                for g in range(GP):
                    nc.gpsimd.indirect_dma_start(g0[:, c, g, :], None, x0,
                                                 bass.IndirectOffsetOnAxis(i0[:, c, g:g + 1], 0)) \
                        .then_inc(s["ga0"], 16)
            for k, n in (("ga1", GP), ("ga0", TT * GP)):
                pool.wait_ge(s[k], 16 * n)

            def f_xs(n):
                wait_prev(pool, s["pe_xT"], n)
                nc.gpsimd.tensor_copy(xs1[:, :, :], g1[:, :, ds(n * C1, C1)])
                nc.gpsimd.tensor_copy(xs0[:, :, :, :].rearrange("p t g c -> p (t g) c"),
                                      g0[:, :, :, ds(n * C0, C0)].rearrange("p t g c -> p (t g) c")) \
                    .then_inc(s["pool_xs"], 1)

            def rsqrt(rs, mv, var, ready, free, added, done, n):
                pool.wait_ge(ready, n + 1)
                wait_prev(pool, free, n)
                nc.gpsimd.tensor_tensor(var[:, :], mv[:, :, 1], epsc[:, :], ALU.add).then_inc(added, 1)
                pool.wait_ge(added, n + 1)
                nc.gpsimd.tensor_tensor(rs[:, :], var[:, :], mhalf[:, :], ALU.pow).then_inc(done, 1)

            def f_qk2(n, which, ready, done):
                apart(pool)
                pool.wait_ge(ready, n + 1)
                nc.gpsimd.tensor_copy(qk[:, which, 1, :, :].rearrange("p h t -> p (h t)"), qkr[which][:, :]) \
                    .then_inc(done, 1)

            def step(i, p, tok, att, clo):
                n, j = i + 1, i - 1
                if isinstance(n, int) and n == 0:
                    f_xs(0)
                if tok and more(n):
                    f_xs(n + 1)
                if clo:
                    rsqrt(rs2, mv2, var2, s["dve_mv2"], s["dve_yn"], s["pool_var2"], s["pool_rs2"], j)
                if tok:
                    rsqrt(rs1, mv1, var1, s["dve_mv1"], s["dve_x1"], s["pool_var1"], s["pool_rs1"], n)
                if clo:
                    hj = hr[:, ds(TT * j, TT), :]
                    pool.wait_ge(s["dve_yn"], j + 1)
                    nc.gpsimd.tensor_tensor(yg[:, :, :], yn[:, :, :], lng_b[:, :].unsqueeze(1).to_broadcast([P, TT, E]),
                                            ALU.mult).then_inc(s["pool_ln"], 1)
                    pool.wait_ge(s["pool_ln"], 2 * j + 1)
                    nc.gpsimd.tensor_tensor(yl[:, :, :], yg[:, :, :], lnb_b[:, :].unsqueeze(1).to_broadcast([P, TT, E]),
                                            ALU.add).then_inc(s["pool_ln"], 1)
                    pool.wait_ge(s["pool_ln"], 2 * j + 2)
                    nc.gpsimd.tensor_tensor(hj, hj, yl[:, :, :], ALU.add).then_inc(s["pool_h2"], 1)
                    apart(pool)
                    pool.wait_ge(s["pool_h2"], j + 1)
                if tok:
                    f_qk2(n, 0, s["dve_q"], s["pool_q"])
                if clo:
                    rsqrt(rs3, mv3, var3, s["dve_mv3"], s["dve_x2"], s["pool_var3"], s["pool_rs3"], j)
                if tok:
                    f_qk2(n, 1, s["dve_k"], s["pool_k"])
                if clo:
                    pool.wait_ge(s["dve_x2"], j + 1)
                    nc.gpsimd.tensor_copy(xrow[:, ds(TT * j, TT), 0:E], x2c[:, :, :])
                    nc.gpsimd.tensor_tensor(hj, hj, x2c[:, :, :], ALU.add).then_inc(s["pool_r"], 1)

            over_images(pool, step)
            moe_gpsimd(pool)


def _interpolation(n_in, n_out):
    import numpy as np
    pos = (np.arange(n_out, dtype=np.float32) + np.float32(0.5)) * np.float32(n_in / n_out) - np.float32(0.5)
    pos = np.clip(pos, 0.0, n_in - 1).astype(np.float32)
    lo = np.floor(pos).astype(np.int64)
    hi = np.minimum(lo + 1, n_in - 1)
    w = (pos - lo).astype(np.float32)
    m = np.zeros((n_in, n_out), np.float32)
    m[lo, np.arange(n_out)] += 1 - w
    m[hi, np.arange(n_out)] += w
    return m


def kernel(**inputs):
    import numpy as np
    import concourse.bacc as bacc
    from concourse import mybir
    from concourse.bass_utils import run_bass_kernel_spmd

    a = {k: np.asarray(v) for k, v in inputs.items()}
    x = a["x"]
    B, C, H, _ = x.shape
    T, P = 256, 128

    def patches(p):
        h = H // p
        t = x.reshape(B, C, h, p, h, p).transpose(2, 4, 0, 3, 5, 1)
        return t.reshape(h * h, B * p * p * C)

    k = "L0_tok_"
    arrays = {
        "x0": patches(1), "x1": patches(2), "x2": patches(4),
        "w0t": a[k + "W0"].T, "w1t": a[k + "W1"].T, "w2t": a[k + "W2"].T,
        "b012": np.concatenate([a[k + "b0"], a[k + "b1"], a[k + "b2"]])[:, None],
        "wft": a[k + "Wf"].T, "bf": a[k + "bf"][None, :],
        "idx0": a[k + "idx0"], "idx1": a[k + "idx1"], "idx2": a[k + "idx2"],
        "w_qkv": a["L0_attn_w_qkv"], "w_out": a["L0_attn_w_out"], "b_out": a["L0_attn_b_out"],
        "ln_g": a["L0_attn_ln_g"], "ln_b": a["L0_attn_ln_b"], "wrt": a["L0_ffn_Wr"].T,
        "ew1": a["L0_ffn_W1"], "eb1": a["L0_ffn_b1"], "ew2": a["L0_ffn_W2"], "eb2": a["L0_ffn_b2"],
        "c_ident": np.eye(P, dtype=np.float32), "c_tri": np.triu(np.ones((P, P), np.float32), 1),
        "c_interp1": _interpolation(a[k + "idx1"].size // 16, T),
        "c_interp2": _interpolation(a[k + "idx2"].size // 16, T),
        "c_iota": np.tile(np.arange(2 * B * T // P + 15, dtype=np.float32), (P, 1)),
    }
    arrays = {n: np.ascontiguousarray(v) for n, v in arrays.items()}
    nc = bacc.Bacc("TRN2", target_bir_lowering=False, num_devices=1)
    args = [nc.dram_tensor(n, v.shape, mybir.dt.from_np(v.dtype), kind="ExternalInput").ap()
            for n, v in arrays.items()]
    args.append(nc.dram_tensor("out", (B, T, 192), mybir.dt.float32, kind="ExternalOutput").ap())
    vit_tower(nc, *args)
    r = run_bass_kernel_spmd(nc, [arrays], core_ids=[0])
    return r.results[0]["out"]
```

```python
import concourse.bass as bass
from concourse import mybir
from contextlib import ExitStack


def vit_tower(nc, x0, x1, x2, w0t, w1t, w2t, b012, wft, bf, idx0, idx1, idx2, w_qkv, w_out, b_out, ln_g, ln_b,
              wrt, ew1, eb1, ew2, eb2, c_ident, c_tri, c_interp1, c_interp2, c_iota, out):
    fp32, bf16, i32 = mybir.dt.float32, mybir.dt.bfloat16, mybir.dt.int32
    ALU, ACT, AX = mybir.AluOpType, mybir.ActivationFunctionType, mybir.AxisListType
    ds = bass.ds

    P = 128
    B, T, E = out.shape
    TT = T // P
    NT = B * TT
    GP = 16
    C0, C1, C2 = (a.shape[1] // B for a in (x0, x1, x2))
    T1, T2 = idx1.shape[0] // GP, idx2.shape[0] // GP
    EM = w0t.shape[1]
    KH = E // 2
    HD, HEADS = 16, E // 16
    U, HU = 4, HEADS // 4
    HH = HEADS // 2
    NPART = 3
    QPART, KPART = (0, 1, 2, 0, 1, 0), (0, 0, 0, 1, 1, 2)
    KS = len(QPART) * HD
    KM = KS + NPART
    NX1, NX2 = GP * C1 // KH, GP * C2 // KH
    NE, DM, FF = ew1.shape
    FC = FF // P
    TOPK = 2
    PAIRS = TOPK * NT
    NTILE = PAIRS + NE - 1
    CG = 8
    EPS = 1e-5
    SCALE = 1.0 / HD ** 0.5
    HILO = 512 // P

    x2_d = nc.dram_tensor("x2_rows", ((NT + 1) * P, E), fp32).ap()
    g1_d = nc.dram_tensor("level1_patches", (idx1.shape[0], x1.shape[1]), fp32).ap()
    g2_d = nc.dram_tensor("level2_patches", (idx2.shape[0], x2.shape[1]), fp32).ap()
    qk_d = nc.dram_tensor("qk_parts", (2, 2, NPART, E, T), bf16).ap()
    acc_d = nc.dram_tensor("acc_rows", (NT * P + P, E), fp32).ap()

    ctx = ExitStack()
    with ctx:
        def sb(name, shape, dt=fp32):
            return ctx.enter_context(nc.sbuf_tensor(name, shape, dt))

        def ps(name, shape):
            return ctx.enter_context(nc.psum_tensor(name, shape, fp32))

        def sem(name):
            return ctx.enter_context(nc.semaphore(name))

        ident = sb("ident", [P, P])
        ident16 = sb("ident16", [P, P], bf16)
        tri = sb("tri", [P, P])
        ones = sb("ones", [P, P])
        mhalf = sb("mhalf", [P, TT])
        epsc = sb("epsc", [P, TT])
        bd = sb("bd", [P, P])
        rr = sb("rr", [P, T])
        bd2 = sb("bd2", [P, EM])
        rr2 = sb("rr2", [P, T])
        w1s = sb("w1s", [KH, NX1, EM])
        w2s = sb("w2s", [KH, NX2, EM])
        bias01 = sb("bias01", [P, 1])
        bias2 = sb("bias2", [EM, 1])
        wfa = sb("wfa", [P, E])
        wfb = sb("wfb", [EM + 1, E])
        wqkv = sb("wqkv", [KH, 2, 3 * E])
        wo = sb("wo", [KH, 2, E])
        wr = sb("wr", [KH, 2, NE])
        bout_b = sb("bout_b", [P, E])
        lng_b = sb("lng_b", [P, E])
        lnb_b = sb("lnb_b", [P, E])
        i0 = sb("i0", [P, TT, GP], i32)
        i1 = sb("i1", [P, T1 * GP // P], i32)
        i2 = sb("i2", [P, T2 * GP // P], i32)
        n_shared, n_pixels = 17800, 5840
        shared = sb("shared", [P, n_shared])
        pixels = sb("pixels", [P, n_pixels])

        def carve(memory, size):
            at = [0]

            def part(shape, dt=fp32):
                n = 1
                for d in shape[1:]:
                    n *= d
                if dt == bf16:
                    n //= 2
                a = memory[0:shape[0], at[0]:at[0] + n]
                at[0] += n
                assert at[0] <= size
                if dt != fp32:
                    a = a.bitcast(dt)
                names = "abcd"[:len(shape) - 1]
                if len(shape) == 2:
                    return a
                return a.rearrange(f"p ({' '.join(names)}) -> p {' '.join(names)}",
                                   **dict(zip(names[1:], shape[2:])))
            return part

        early_pixels = carve(pixels, n_pixels)
        g2 = early_pixels([P, T2 * GP // P, B * C2])
        g1r = early_pixels([P, T1 * GP // P, B * C1])
        g0 = early_pixels([P, TT, GP, B * C0])
        g1 = carve(pixels, n_pixels)([T1, GP, B * C1])
        xs0 = sb("xs0", [P, TT, GP, C0])
        xs1 = sb("xs1", [T1, GP, C1])
        xs2 = [sb(f"xs2{p}", [T2, GP, C2]) for p in range(2)]
        x12T = sb("x12T", [KH, NX1 * T1 + NX2 * T2])
        y01 = sb("y01", [P, T])
        y2 = sb("y2", [EM + 1, T])
        hr = sb("hr", [P, NT, E])
        st1 = sb("st1", [P, TT, 6])
        mv1 = sb("mv1", [P, TT, 2])
        rs1 = sb("rs1", [P, TT])
        var1 = sb("var1", [P, TT])
        xn1 = sb("xn1", [P, TT, E])
        x1T = sb("x1T", [KH, 2, T])
        early = carve(shared, n_shared)
        qk = early([KH, 2, NPART, 2, T], bf16)
        qkr = [early([KH, 2 * T]) for which in range(2)]
        qs = [early([KM, HEADS, T], bf16) for p in range(2)]
        ks = [early([KM, HEADS, T], bf16) for p in range(2)]
        v = [sb(f"v{p}", [P, TT, HEADS, 2 * HD]) for p in range(2)]
        negmax = sb("negmax", [P, TT, HEADS])
        nmr = sb("nmr", [P, 2, TT, HH])
        nm = sb("nm", [P, 2, TT, NPART, HH], bf16)
        nmT = sb("nmT", [NPART * HH, 2, T], bf16)
        pT = [early([P, HU, 2 * T]) for p in range(2)]
        oT = sb("oT", [HU * 32, U, T])
        rden = sb("rden", [P, TT, HEADS])
        on = sb("on", [P, TT, HEADS, HD])
        onT = sb("onT", [KH, 2 * T])
        yb = sb("yb", [P, TT, E])
        st2 = sb("st2", [P, TT, 6])
        mv2 = sb("mv2", [P, TT, 2])
        rs2 = sb("rs2", [P, TT])
        var2 = sb("var2", [P, TT])
        yn = sb("yn", [P, TT, E])
        yg = sb("yg", [P, TT, E])
        yl = sb("yl", [P, TT, E])
        st3 = sb("st3", [P, TT, 6])
        mv3 = sb("mv3", [P, TT, 2])
        rs3 = sb("rs3", [P, TT])
        var3 = sb("var3", [P, TT])
        xrow = sb("xrow", [P, NT, E])
        x2T = sb("x2T", [KH, 2 * T])
        lg = sb("lg", [P, NT, NE])

        x2c = sb("x2c", [P, TT, E])
        padrow = sb("padrow", [P, E])
        tokid_i = sb("tokid_i", [P, NT], i32)
        padid_i = sb("padid_i", [P, 1], i32)
        late = carve(shared, n_shared)
        onehot = carve(pixels, n_pixels)
        iota = sb("iota", [P, P])
        r_mx = late([P, NT])
        r_ls = late([P, NT, NE])
        r_p = late([P, NT, NE])
        r_sum = late([P, NT])
        r_gates = late([P, TOPK, NT])
        r_gate = [r_gates[:, k, :] for k in range(2)]
        r_eq = late([P, NT, NE])
        r_key = late([P, NT, NE])
        r_km = late([P, NT])
        r_hot = [late([P, NT, NE]) for k in range(2)]
        r_cnt = late([P, NT, NE])
        r_ta = [late([P, NT, NE]) for k in range(2)]
        r_sl = late([P, NT, NE])
        r_ci = late([P, NE], i32)
        r_ti = late([P, NE], i32)
        r_tn = late([P, NE])
        r_te = [late([P, NE]) for k in range(2)]
        r_base = late([P, NE])
        r_slf = late([P, TOPK, NT])
        r_sli = late([P, TOPK, NT], i32)
        r_hii = late([P, TOPK, NT], i32)
        r_hi = late([P, TOPK, NT])
        r_lo = late([P, TOPK, NT])
        r_id = late([P, TOPK, NT])
        r_pad = late([P, 1])
        oh_lo = [onehot([P, CG, P]) for p in range(2)]
        oh_hi = [onehot([P, CG, NTILE]) for p in range(2)]
        oh_v = [onehot([P, CG, 2, NTILE]) for p in range(2)]
        r_emp = late([P, NTILE])
        r_tt = late([P, NTILE, NE])
        r_tf = late([P, NTILE])
        tab = late([P, NTILE], i32)
        w1b = [late([KH + 1, 2, FF]) for p in range(2)]
        w2b = [late([P, FC, E]) for p in range(2)]
        b2b = [late([P, E]) for p in range(2)]
        xt = [late([P, E]) for p in range(2)]
        t_id = late([P, NTILE], i32)
        t_gate = late([P, NTILE])
        gid = [late([P, 1], i32) for p in range(2)]
        aid = [late([P, 1], i32) for p in range(2)]
        xtT = [late([KH + 1, 2, P]) for p in range(2)]
        hT = [late([P, FF]) for p in range(2)]
        ysum = [late([P, E]) for p in range(2)]
        yg8 = [late([P, E]) for p in range(2)]

        BK = ps("BK", [P, 8, 512])
        S, ST, M0, M1 = BK[:, 0:HU, :], BK[:, HU:2 * HU, :], BK[:, 6, :], BK[:, 7, :]
        H = [BK[:, 2 * p:2 * p + 2, :].rearrange("p b n -> p (b n)")[:, 0:FF] for p in range(2)]
        XT = [BK[:, 4 + p, :] for p in range(2)]
        Y = [BK[:, 6 + p, 0:E] for p in range(2)]

        names = ("ld_const ld_idx0 ld_idx1 ld_idx2 ga0 ga1 ga2 ld_w dve_init pool_init pool_zero ld_pad pool_xs "
                 "pe_xT pe_o12 pe_y pe_h pe_x1T pe_q pe_k pe_v pe_s pe_nmT pe_st pe_pv "
                 "pe_oT pe_onT pe_yat pe_x2T pe_lg act_xT act_o12 act_y act_x1T act_q act_k act_nmT act_exp "
                 "act_oT act_onT act_x2T dve_max dve_nmp dve_nm dve_on dve_rden dve_h dve_st1 dve_mv1 dve_x1 dve_q dve_k pool_q3 pool_k3 act_q2 act_k2 act_v "
                 "dve_yb dve_st2 dve_mv2 dve_yn dve_st3 dve_mv3 dve_x2 dve_lg pool_rs1 pool_rs2 pool_rs3 "
                 "ld_xs20 ld_xs21 st_g2 st_g1 ld_g1 st_qk0 st_qk1 ld_qk0 ld_qk1 ld_mx0 ld_mx1 pool_var1 pool_var2 pool_var3 pool_ln pool_h2 pool_r st_acc "
                 "r_dve r_ls r_exp r_cnt pe_rank pe_tot r_id r_tab r_meta oh_hi oh_id oh_gate oh_pe st_x2 "
                 "m_x0 m_x1 m_wa0 m_wa1 m_wb0 m_wb1 m_b0 m_b1 m_tr m_xT m_s1 m_gelu m_s2 m_y m_yg m_add m_gid m_gid01 out_done").split()
        s = {n: sem(n) for n in names}

        N_QK = 16 * 2 * NPART
        n_const = 16 * 16

        block = ctx.enter_context(nc.Block())

        def over_images(eng, step):
            step(-2, 0, True, False, False, False, False)
            step(-1, 1, True, True, False, False, False)
            step(0, 0, True, True, True, False, False)
            step(1, 1, True, True, True, True, False)
            step(2, 0, True, True, True, True, True)
            with eng.Fori(1, B // 2 - 2) as k:
                step(2 * k + 1, 1, True, True, True, True, True)
                step(2 * k + 2, 0, True, True, True, True, True)
            step(B - 3, (B - 3) % 2, True, True, True, True, True)
            step(B - 2, (B - 2) % 2, False, True, True, True, True)
            step(B - 1, (B - 1) % 2, False, False, True, True, True)
            step(B, B % 2, False, False, False, True, True)
            step(B + 1, (B + 1) % 2, False, False, False, False, True)

        def apart(eng):
            eng.wait_ge(s["ld_const"], n_const)

        def more(n):
            return not isinstance(n, int) or n + 1 < B

        def half(i, p):
            return (i - p) // 2

        def wait_prev(eng, which, count):
            if not (isinstance(count, int) and count <= 0):
                eng.wait_ge(which, count)

        def moe_loads(sp):
            sp.wait_ge(s["r_tab"], 1)
            def expert(t):
                return sp.value_load(tab[0:1, ds(t, 1)], min_val=0, max_val=NE - 1)

            def first(t, p):
                e = expert(t)
                wait_prev(sp, s["m_s1"], t - 1)
                sp.dma_start(w1b[p][0:KH, :, :], ew1[ds(e, 1), :, :].rearrange("a (c p) f -> p (a c) f", p=KH)) \
                    .then_inc(s[f"m_wa{p}"], 16)
                sp.dma_start(w1b[p][KH:KH + 1, 1, :], eb1[ds(e, 1), :]).then_inc(s[f"m_wa{p}"], 16)

            def second(t, p):
                e = expert(t)
                wait_prev(sp, s["m_s2"], t - 1)
                sp.dma_start(w2b[p][:, :, :], ew2[ds(e, 1), :, :].rearrange("a (c p) d -> p (a c) d", p=P)) \
                    .then_inc(s[f"m_wb{p}"], 16)
                wait_prev(sp, s["m_y"], t - 1)
                sp.dma_start(b2b[p][:, :], eb2[ds(e, 1), :].rearrange("a d -> (a d)").partition_broadcast(P)) \
                    .then_inc(s[f"m_b{p}"], 16)

            first(0, 0)
            first(1, 1)
            second(0, 0)
            first(2, 0)
            second(1, 1)
            with sp.Fori(1, (NTILE - 3) // 2) as k:
                first(2 * k + 1, 1)
                second(2 * k, 0)
                first(2 * k + 2, 0)
                second(2 * k + 1, 1)
            t = NTILE - 3
            first(t + 1, 1)
            second(t, 0)
            first(t + 2, 0)
            second(t + 1, 1)
            second(t + 2, 0)
            sp.wait_ge(s["m_add"], 16 * NTILE)
            sp.dma_start(out.rearrange("b t e -> (b t) e"), acc_d[0:NT * P, :]).then_inc(s["out_done"], 16)
            sp.wait_ge(s["out_done"], 16)

        def moe_tensor(pe):
            pe.wait_ge(s["r_cnt"], 1)
            f = r_cnt[:, :, :].rearrange("p t e -> p (t e)")
            nc.tensor.matmul(M0, tri[:, :], f, start=True, stop=True).then_inc(s["pe_rank"], 1)
            nc.tensor.matmul(M1, ones[:, :], f, start=True, stop=True).then_inc(s["pe_tot"], 1)
            for c in range(PAIRS // CG):
                pe.wait_ge(s["oh_id"], c + 1)
                pe.wait_ge(s["oh_gate"], c + 1)
                for g in range(CG):
                    last = nc.tensor.matmul(BK[:, 0, 0:2 * NTILE], oh_lo[c % 2][:, g, :],
                                            oh_v[c % 2][:, g, :, :].rearrange("p v t -> p (v t)"),
                                            start=(c == 0 and g == 0), stop=(c == PAIRS // CG - 1 and g == CG - 1))
                last.then_inc(s["oh_pe"], 1)
            pe.wait_ge(s["r_meta"], 1)

            def rows_T(t, k, p):
                pe.wait_ge(s[f"m_x{p}"], 16 * k + 16)
                wait_prev(pe, s["m_xT"], t - 1)
                for c in range(2):
                    last = nc.tensor.matmul(XT[p][0:KH, c * P:(c + 1) * P], xt[p][:, c * KH:(c + 1) * KH],
                                            ident[:, :], start=True, stop=True, is_transpose=True)
                last.then_inc(s["m_tr"], 1)

            def up(t, k, p):
                pe.wait_ge(s["m_xT"], t + 1)
                pe.wait_ge(s[f"m_wa{p}"], 32 * k + 32)
                wait_prev(pe, s["m_gelu"], t - 1)
                for c in range(FC):
                    o = H[p][:, c * P:(c + 1) * P]
                    nc.tensor.matmul(o, w1b[p][0:KH, 0, c * P:(c + 1) * P], xtT[p][0:KH, 0, :], start=True, stop=False)
                    last = nc.tensor.matmul(o, w1b[p][:, 1, c * P:(c + 1) * P], xtT[p][:, 1, :],
                                            start=False, stop=True)
                last.then_inc(s["m_s1"], 1)

            def down(t, k, p):
                pe.wait_ge(s["m_gelu"], t + 1)
                pe.wait_ge(s[f"m_wb{p}"], 16 * k + 16)
                wait_prev(pe, s["m_y"], t - 1)
                for c in range(FC):
                    last = nc.tensor.matmul(Y[p], hT[p][:, c * P:(c + 1) * P], w2b[p][:, c, :],
                                            start=(c == 0), stop=(c == FC - 1))
                last.then_inc(s["m_s2"], 1)

            rows_T(0, 0, 0)
            rows_T(1, 0, 1)
            up(0, 0, 0)
            up(1, 0, 1)
            rows_T(2, 1, 0)
            down(0, 0, 0)
            up(2, 1, 0)
            rows_T(3, 1, 1)
            down(1, 0, 1)
            with pe.Fori(1, (NTILE - 3) // 2) as k:
                up(2 * k + 1, k, 1)
                rows_T(2 * k + 2, k + 1, 0)
                down(2 * k, k, 0)
                up(2 * k + 2, k + 1, 0)
                rows_T(2 * k + 3, k + 1, 1)
                down(2 * k + 1, k, 1)
            t = NTILE - 3
            up(t + 1, t // 2, 1)
            rows_T(t + 2, t // 2 + 1, 0)
            down(t, t // 2, 0)
            up(t + 2, t // 2 + 1, 0)
            down(t + 1, t // 2, 1)
            down(t + 2, t // 2 + 1, 0)

        def moe_scalar(act):
            act.wait_ge(s["r_ls"], 1)
            nc.scalar.activation(r_p[:, :, :], r_ls[:, :, :], ACT.Exp).then_inc(s["r_exp"], 1)

            def gelu(t, k, p):
                act.wait_ge(s["m_s1"], t + 1)
                wait_prev(act, s["m_s2"], t - 1)
                nc.scalar.activation(hT[p][:, :], H[p], ACT.Gelu).then_inc(s["m_gelu"], 1)

            gelu(0, 0, 0)
            gelu(1, 0, 1)
            with act.Fori(1, NTILE // 2) as k:
                gelu(2 * k, k, 0)
                gelu(2 * k + 1, k, 1)
            gelu(NTILE - 1, NTILE // 2, 0)

        def moe_vector(dve):
            done = [0]

            def then(ins):
                done[0] += 1
                ins.then_inc(s["r_dve"], 1)
                dve.wait_ge(s["r_dve"], done[0])

            def over_e(a):
                return a.unsqueeze(2).to_broadcast([P, NT, NE])

            V = nc.vector
            for p in range(2):
                V.memset(xtT[p][KH:KH + 1, :, :], 1.0)
            dve.wait_ge(s["dve_lg"], B)
            then(V.tensor_reduce(r_mx[:, :], lg[:, :, :], AX.X, ALU.max))
            V.tensor_tensor(r_ls[:, :, :], lg[:, :, :], over_e(r_mx[:, :]), ALU.subtract).then_inc(s["r_ls"], 1)
            dve.wait_ge(s["r_exp"], 1)
            then(V.tensor_reduce(r_sum[:, :], r_p[:, :, :], AX.X, ALU.add))
            then(V.reciprocal(r_mx[:, :], r_sum[:, :]))
            then(V.tensor_tensor(r_p[:, :, :], r_p[:, :, :], over_e(r_mx[:, :]), ALU.mult))
            for k in range(TOPK):
                then(V.tensor_reduce(r_gate[k][:, :], r_p[:, :, :], AX.X, ALU.max))
                then(V.tensor_tensor(r_eq[:, :, :], r_p[:, :, :], over_e(r_gate[k][:, :]), ALU.is_equal))
                then(V.scalar_tensor_tensor(r_key[:, :, :], r_eq[:, :, :], -float(NE),
                                            iota[:, 0:NE].unsqueeze(1).to_broadcast([P, NT, NE]), ALU.mult, ALU.add))
                then(V.tensor_reduce(r_km[:, :], r_key[:, :, :], AX.X, ALU.min))
                then(V.tensor_tensor(r_hot[k][:, :, :], r_key[:, :, :], over_e(r_km[:, :]), ALU.is_equal))
                if k == 0:
                    then(V.scalar_tensor_tensor(r_p[:, :, :], r_hot[0][:, :, :], -2.0, r_p[:, :, :],
                                                ALU.mult, ALU.add))
            V.tensor_tensor(r_cnt[:, :, :], r_hot[0][:, :, :], r_hot[1][:, :, :], ALU.add).then_inc(s["r_cnt"], 1)
            V.tensor_copy(r_pad[:, :], padid_i[:, :])
            V.tensor_copy(r_id[:, 0, :], tokid_i[:, :])
            then(V.tensor_copy(r_id[:, 1, :], tokid_i[:, :]))
            dve.wait_ge(s["pe_tot"], 1)
            tot = M1.rearrange("p (t e) -> p t e", e=NE)
            then(V.tensor_copy(r_ta[0][:, :, :], tot))
            a, b, sh = 0, 1, 1
            while sh < NT:
                V.tensor_copy(r_ta[b][:, 0:sh, :], r_ta[a][:, 0:sh, :])
                then(V.tensor_tensor(r_ta[b][:, sh:NT, :], r_ta[a][:, sh:NT, :], r_ta[a][:, 0:NT - sh, :], ALU.add))
                a, b, sh = b, a, 2 * sh
            then(V.tensor_scalar(r_ci[:, :], r_ta[a][:, NT - 1, :], float(P - 1), None, ALU.add))
            then(V.tensor_scalar(r_ti[:, :], r_ci[:, :], P.bit_length() - 1, None, ALU.arith_shift_right))
            then(V.tensor_copy(r_tn[:, :], r_ti[:, :]))
            then(V.tensor_copy(r_te[0][:, :], r_tn[:, :]))
            c, d, sh = 0, 1, 1
            while sh < NE:
                V.tensor_copy(r_te[d][:, 0:sh], r_te[c][:, 0:sh])
                then(V.tensor_tensor(r_te[d][:, sh:NE], r_te[c][:, sh:NE], r_te[c][:, 0:NE - sh], ALU.add))
                c, d, sh = d, c, 2 * sh
            then(V.tensor_tensor(r_base[:, :], r_te[c][:, :], r_tn[:, :], ALU.subtract))
            then(V.scalar_tensor_tensor(r_sl[:, :, :], r_base[:, :].unsqueeze(1).to_broadcast([P, NT, NE]), float(P),
                                        r_ta[a][:, :, :], ALU.mult, ALU.add))
            then(V.tensor_tensor(r_sl[:, :, :], r_sl[:, :, :], tot, ALU.subtract))
            dve.wait_ge(s["pe_rank"], 1)
            then(V.tensor_tensor(r_sl[:, :, :], r_sl[:, :, :], M0.rearrange("p (t e) -> p t e", e=NE), ALU.add))
            for k in range(TOPK):
                then(V.tensor_tensor(r_eq[:, :, :], r_sl[:, :, :], r_hot[k][:, :, :], ALU.mult))
                then(V.tensor_reduce(r_slf[:, k, :], r_eq[:, :, :], AX.X, ALU.add))
            then(V.tensor_tensor(r_tt[:, :, :], r_te[c][:, :].unsqueeze(1).to_broadcast([P, NTILE, NE]),
                                 iota[:, 0:NTILE].unsqueeze(2).to_broadcast([P, NTILE, NE]), ALU.is_le))
            then(V.tensor_reduce(r_tf[:, :], r_tt[:, :, :], AX.X, ALU.add))
            V.tensor_scalar(tab[:, :], r_tf[:, :], float(NE - 1), None, ALU.min).then_inc(s["r_tab"], 1)
            then(V.tensor_copy(r_sli[:, :, :], r_slf[:, :, :]))
            then(V.tensor_scalar(r_hii[:, :, :], r_sli[:, :, :], P.bit_length() - 1, None, ALU.arith_shift_right))
            then(V.tensor_copy(r_hi[:, :, :], r_hii[:, :, :]))
            then(V.scalar_tensor_tensor(r_lo[:, :, :], r_hi[:, :, :], -float(P), r_slf[:, :, :], ALU.mult, ALU.add))
            lo, hi, tok = (a[:, :, :].rearrange("p k t -> p (k t)") for a in (r_lo, r_hi, r_id))
            for c in range(PAIRS // CG):
                b, at = c % 2, slice(c * CG, (c + 1) * CG)
                if c >= 2:
                    dve.wait_ge(s["oh_gate"], c - 1)
                V.tensor_tensor(oh_hi[b][:, :, :], iota[:, 0:NTILE].unsqueeze(1).to_broadcast([P, CG, NTILE]),
                                hi[:, at].unsqueeze(2).to_broadcast([P, CG, NTILE]), ALU.is_equal) \
                    .then_inc(s["oh_hi"], 1)
                if c >= 2:
                    dve.wait_ge(s["oh_pe"], c - 1)
                V.tensor_tensor(oh_lo[b][:, :, :], iota[:, :].unsqueeze(1).to_broadcast([P, CG, P]),
                                lo[:, at].unsqueeze(2).to_broadcast([P, CG, P]), ALU.is_equal)
                dve.wait_ge(s["oh_hi"], c + 1)
                V.tensor_tensor(oh_v[b][:, :, 0, :], oh_hi[b][:, :, :],
                                tok[:, at].unsqueeze(2).to_broadcast([P, CG, NTILE]), ALU.mult).then_inc(s["oh_id"], 1)
            dve.wait_ge(s["oh_pe"], PAIRS // CG)
            then(V.tensor_scalar(r_emp[:, :], BK[:, 0, 0:NTILE], 0.0, None, ALU.is_equal))
            then(V.tensor_scalar(r_emp[:, :], r_emp[:, :], r_pad[:, 0:1], None, ALU.mult))
            V.tensor_copy(t_gate[:, :], BK[:, 0, NTILE:2 * NTILE])
            V.scalar_tensor_tensor(t_id[:, :], BK[:, 0, 0:NTILE], -1.0, r_emp[:, :], ALU.add, ALU.add) \
                .then_inc(s["r_meta"], 1)

            def rows_T(t, k, p):
                dve.wait_ge(s["m_tr"], t + 1)
                wait_prev(dve, s["m_s1"], t - 1)
                V.tensor_copy(xtT[p][0:KH, :, :], XT[p][0:KH, 0:2 * P].rearrange("p (c t) -> p c t", c=2)) \
                    .then_inc(s["m_xT"], 1)

            def biased(t, k, p):
                dve.wait_ge(s["m_s2"], t + 1)
                dve.wait_ge(s[f"m_b{p}"], 16 * k + 16)
                wait_prev(dve, s["m_yg"], t - 1)
                V.tensor_tensor(ysum[p][:, :], Y[p], b2b[p][:, :], ALU.add).then_inc(s["m_y"], 1)

            rows_T(0, 0, 0)
            rows_T(1, 0, 1)
            rows_T(2, 1, 0)
            biased(0, 0, 0)
            rows_T(3, 1, 1)
            biased(1, 0, 1)
            with dve.Fori(1, (NTILE - 3) // 2) as k:
                rows_T(2 * k + 2, k + 1, 0)
                biased(2 * k, k, 0)
                rows_T(2 * k + 3, k + 1, 1)
                biased(2 * k + 1, k, 1)
            t = NTILE - 3
            rows_T(t + 2, t // 2 + 1, 0)
            biased(t, t // 2, 0)
            biased(t + 1, t // 2, 1)
            biased(t + 2, t // 2 + 1, 0)

        def moe_gpsimd(pool):
            gate = r_gates[:, :, :].rearrange("p k t -> p (k t)")
            for c in range(PAIRS // CG):
                pool.wait_ge(s["oh_hi"], c + 1)
                if c >= 2:
                    pool.wait_ge(s["oh_pe"], c - 1)
                nc.gpsimd.tensor_tensor(oh_v[c % 2][:, :, 1, :], oh_hi[c % 2][:, :, :],
                                        gate[:, c * CG:(c + 1) * CG].unsqueeze(2).to_broadcast([P, CG, NTILE]),
                                        ALU.mult).then_inc(s["oh_gate"], 1)
            pool.wait_ge(s["r_meta"], 1)
            pool.wait_ge(s["ld_pad"], 32)
            pool.wait_ge(s["st_x2"], 16)
            pool.wait_ge(s["st_acc"], 16)

            def rows(t, p):
                apart(pool)
                wait_prev(pool, s["m_tr"], t - 1)
                if isinstance(t, int) and t < 2:
                    nc.gpsimd.tensor_copy(gid[p][:, :], t_id[:, ds(t, 1)]).then_inc(s["m_gid01"], 1)
                    pool.wait_ge(s["m_gid01"], t + 1)
                else:
                    nc.gpsimd.tensor_copy(gid[p][:, :], t_id[:, ds(t, 1)]).then_inc(s["m_gid"], 1)
                    apart(pool)
                    pool.wait_ge(s["m_gid"], t - 1)
                nc.gpsimd.indirect_dma_start(xt[p][:, :], None, x2_d,
                                             bass.IndirectOffsetOnAxis(gid[p][:, :], 0)).then_inc(s[f"m_x{p}"], 16)

            def add(t, k, p):
                pool.wait_ge(s["m_y"], t + 1)
                wait_prev(pool, s["m_add"], 16 * t)
                nc.gpsimd.tensor_copy(aid[p][:, :], t_id[:, ds(t, 1)])
                nc.gpsimd.tensor_tensor(yg8[p][:, :], ysum[p][:, :], t_gate[:, ds(t, 1)].to_broadcast([P, E]),
                                        ALU.mult).then_inc(s["m_yg"], 1)
                apart(pool)
                pool.wait_ge(s["m_yg"], t + 1)
                nc.gpsimd.indirect_dma_start(acc_d, bass.IndirectOffsetOnAxis(aid[p][:, :], 0),
                                             yg8[p][:, :], None, compute_op=ALU.add).then_inc(s["m_add"], 16)

            for t in range(3):
                rows(t, t % 2)
            for t in range(2):
                rows(t + 3, (t + 3) % 2)
                add(t, t // 2, t % 2)
            with pool.Fori(1, (NTILE - 3) // 2) as k:
                rows(2 * k + 3, 1)
                add(2 * k, k, 0)
                rows(2 * k + 4, 0)
                add(2 * k + 1, k, 1)
            for t in range(NTILE - 3, NTILE):
                add(t, t // 2, t % 2)

        @block.sync
        def _(sp):
            sp.dma_start(i0[:, :, :], idx0.rearrange("(c p g) -> p c g", c=TT, g=GP)).then_inc(s["ld_idx0"], 16)
            sp.dma_start(i2[:, :], idx2.rearrange("(p c) -> p c", p=P)).then_inc(s["ld_idx2"], 16)
            sp.dma_start(i1[:, :], idx1.rearrange("(p c) -> p c", p=P)).then_inc(s["ld_idx1"], 16)
            consts = [
                (ident[:, :], c_ident), (tri[:, :], c_tri), (iota[:, :], c_iota),
                (w1s[:, :, :], w1t.rearrange("(c p) e -> p c e", p=KH)),
                (w2s[:, :, :], w2t.rearrange("(c p) e -> p c e", p=KH)),
                (bias01[:, :], b012[0:P, :]), (bias2[:, :], b012[P:P + EM, :]),
                (wfa[:, :], wft[0:P, :]), (wfb[0:EM, :], wft[P:E, :]), (wfb[EM:EM + 1, :], bf),
                (wqkv[:, :, :], w_qkv.rearrange("(c p) n -> p c n", p=KH)),
                (wo[:, :, :], w_out.rearrange("(c p) n -> p c n", p=KH)),
                (wr[:, :, :], wrt.rearrange("(c p) n -> p c n", p=KH)),
                (bout_b[:, :], b_out.partition_broadcast(P)), (lng_b[:, :], ln_g.partition_broadcast(P)),
                (lnb_b[:, :], ln_b.partition_broadcast(P)),
            ]
            for dst, src in consts:
                sp.dma_start(dst, src).then_inc(s["ld_const"], 16)
            sp.wait_ge(s["dve_init"], 1)
            for dst, src in ((bd[0:GP * C0, 0:EM], w0t), (rr[P - T1:P, :], c_interp1), (rr2[0:T2, :], c_interp2)):
                sp.dma_start(dst, src).then_inc(s["ld_w"], 16)
            sp.wait_ge(s["pool_init"], 3)
            sp.dma_start(x2_d[NT * P:NT * P + P, :], padrow[:, :]).then_inc(s["ld_pad"], 16)
            sp.dma_start(acc_d[NT * P:NT * P + P, :], padrow[:, :]).then_inc(s["ld_pad"], 16)

            def a_mx(i, p, v):
                sp.wait_ge(s["act_nmT"], 2 * i + v + 1)
                sp.dma_start(qs[p][KS:KM, v * HH:(v + 1) * HH, :], nmT[:, v, :]).then_inc(s[f"ld_mx{v}"], 16)

            def st_qk(n, p, which):
                apart(sp)
                sp.wait_ge(s["pool_k3" if which else "pool_q3"], n + 1)
                sp.dma_start(qk_d[p, which].rearrange("b (c r) t -> r b c t", r=KH), qk[:, which, :, :, :]) \
                    .then_inc(s[f"st_qk{p}"], 16)

            def ld_qk(p, m, which):
                sp.wait_ge(s[f"st_qk{p}"], 32 * m + 16 * which + 16)
                at, src = 0, qk_d[p, which]
                for kb in range(NPART):
                    nq = NPART - kb
                    dst = (ks if which else qs)[p][at * HD:(at + nq) * HD, :, :]
                    part = (src[kb:kb + 1].to_broadcast([nq, E, T]) if which else src[0:nq])
                    sp.dma_start(dst, part.rearrange("b (d h) t -> b d h t", d=HD)).then_inc(s[f"ld_qk{p}"], 16)
                    at += nq

            def f_xs2(n, p):
                wait_prev(sp, s["pe_xT"], n - 1)
                sp.dma_start(xs2[p][:, :, :], g2_d.rearrange("(t g) (b c) -> b t g c", g=GP, c=C2)[ds(n, 1)]
                             .rearrange("a t g c -> (a t) g c")).then_inc(s[f"ld_xs2{p}"], 16)

            def step(i, p, ta, tb, att, clo, fin):
                n, q = i + 1, 1 - p
                if att:
                    a_mx(i, p, 0)
                if tb:
                    m = half(n, q)
                    st_qk(n, q, 0)
                    ld_qk(q, m, 0)
                    st_qk(n, q, 1)
                if att:
                    a_mx(i, p, 1)
                if tb:
                    ld_qk(q, m, 1)
                if att:
                    sp.wait_ge(s["pe_st"], U * i + U)
                if ta and more(i + 2):
                    f_xs2(i + 3, q)

            sp.wait_ge(s["ga2"], 16 * (T2 * GP // P))
            sp.dma_start(g2_d.rearrange("(p c) n -> p c n", p=P), g2[:, :, :]).then_inc(s["st_g2"], 16)
            sp.wait_ge(s["ga1"], 16 * (T1 * GP // P))
            sp.dma_start(g1_d.rearrange("(p c) n -> p c n", p=P), g1r[:, :, :]).then_inc(s["st_g1"], 16)
            sp.wait_ge(s["st_g2"], 16)
            sp.wait_ge(s["st_g1"], 16)
            sp.dma_start(g1[:, :, :], g1_d.rearrange("(t g) n -> t g n", g=GP)).then_inc(s["ld_g1"], 16)
            f_xs2(0, 0)

            over_images(sp, step)
            sp.wait_ge(s["pool_r"], B)
            sp.dma_start(x2_d[0:NT * P, :].rearrange("(t p) e -> p t e", p=P), xrow[:, :, :]).then_inc(s["st_x2"], 16)
            sp.dma_start(acc_d[0:NT * P, :].rearrange("(t p) e -> p t e", p=P), hr[:, :, :]).then_inc(s["st_acc"], 16)
            moe_loads(sp)

        @block.tensor
        def _(pe):
            pe.wait_ge(s["ld_const"], n_const)
            pe.wait_ge(s["ld_w"], 48)
            pe.wait_ge(s["dve_init"], 3)

            def transpose(dst, src, n):
                return nc.tensor.matmul(dst, src, ident[0:n, 0:n], start=True, stop=True, is_transpose=True)

            def f_xT(n, p):
                for c in range(TT):
                    transpose(M0[0:GP * C0, c * P:(c + 1) * P], xs0[:, c, :, :].rearrange("p g c -> p (g c)"), P)
                f = xs1[:, :, :].rearrange("p g c -> p (g c)")
                for c in range(NX1):
                    transpose(M0[0:KH, T + c * T1:T + (c + 1) * T1], f[:, c * KH:(c + 1) * KH], T1)
                f = xs2[p][:, :, :].rearrange("p g c -> p (g c)")
                at = T + NX1 * T1
                for c in range(NX2):
                    last = transpose(M0[0:KH, at + c * T2:at + (c + 1) * T2], f[:, c * KH:(c + 1) * KH], T2)
                last.then_inc(s["pe_xT"], 1)

            def f_o12(n):
                pe.wait_ge(s["act_xT"], n + 1)
                for c in range(NX1):
                    nc.tensor.matmul(M0[P - T1:P, 0:EM], x12T[:, c * T1:(c + 1) * T1], w1s[:, c, :],
                                     start=(c == 0), stop=(c == NX1 - 1))
                at = NX1 * T1
                for c in range(NX2):
                    last = nc.tensor.matmul(M0[0:T2, EM:2 * EM], x12T[:, at + c * T2:at + (c + 1) * T2],
                                            w2s[:, c, :], start=(c == 0), stop=(c == NX2 - 1))
                last.then_inc(s["pe_o12"], 1)

            def f_y(n):
                pe.wait_ge(s["act_o12"], n + 1)
                nc.tensor.matmul(M0[:, 0:T], bd[:, :], rr[:, :], start=True, stop=True)
                nc.tensor.matmul(M0[0:EM, T:2 * T], bd2[:, :], rr2[:, :], start=True, stop=True) \
                    .then_inc(s["pe_y"], 1)

            def f_h(n):
                pe.wait_ge(s["act_y"], n + 1)
                for c in range(TT):
                    o = M0[:, c * E:(c + 1) * E]
                    nc.tensor.matmul(o, y01[:, c * P:(c + 1) * P], wfa[:, :], start=True, stop=False)
                    last = nc.tensor.matmul(o, y2[:, c * P:(c + 1) * P], wfb[:, :], start=False, stop=True)
                last.then_inc(s["pe_h"], 1)

            def f_x1T(n):
                pe.wait_ge(s["dve_x1"], n + 1)
                for c in range(2):
                    for t in range(TT):
                        last = transpose(M0[0:KH, (c * TT + t) * P:(c * TT + t + 1) * P],
                                         xn1[:, t, c * KH:(c + 1) * KH], P)
                last.then_inc(s["pe_x1T"], 1)

            def f_qk(n, which, free, done):
                pe.wait_ge(free, n + 1)
                for h in range(2):
                    at = which * E + h * KH
                    for c in range(2):
                        last = nc.tensor.matmul(M0[0:KH, h * T:(h + 1) * T], wqkv[:, c, at:at + KH], x1T[:, c, :],
                                                start=(c == 0), stop=(c == 1))
                last.then_inc(done, 1)

            def f_v(n):
                pe.wait_ge(s["dve_k"], n + 1)
                for t in range(TT):
                    for c in range(2):
                        last = nc.tensor.matmul(M0[:, t * E:(t + 1) * E], x1T[:, c, t * P:(t + 1) * P],
                                                wqkv[:, c, 2 * E:3 * E], start=(c == 0), stop=(c == 1))
                last.then_inc(s["pe_v"], 1)

            def a_s(i, p, u):
                if u == 0:
                    pe.wait_ge(s[f"ld_qk{p}"], N_QK * half(i, p) + N_QK)
                wait_prev(pe, s["dve_max"], U * i + u)
                for t in range(TT):
                    for a in range(HU):
                        h = HU * u + a
                        last = nc.tensor.matmul(S[:, a, t * T:(t + 1) * T], qs[p][0:KS, h, t * P:(t + 1) * P],
                                                ks[p][0:KS, h, :], start=True, stop=True)
                last.then_inc(s["pe_s"], 1)

            def a_nmT(i, v):
                pe.wait_ge(s["dve_nm"], 2 * i + v + 1)
                for t in range(TT):
                    last = nc.tensor.matmul(M1[0:NPART * HH, t * P:(t + 1) * P],
                                            nm[:, v, t, :, :].rearrange("p a h -> p (a h)"), ident16[:, :],
                                            start=True, stop=True)
                last.then_inc(s["pe_nmT"], 1)

            def a_st(i, p, u):
                if u % 2 == 0:
                    pe.wait_ge(s[f"ld_mx{u // 2}"], 16 * (i + 1))
                wait_prev(pe, s["act_exp"], U * i + u)
                for t in range(TT):
                    for a in range(HU):
                        h = HU * u + a
                        last = nc.tensor.matmul(ST[:, a, t * T:(t + 1) * T], ks[p][:, h, t * P:(t + 1) * P],
                                                qs[p][:, h, :], start=True, stop=True)
                last.then_inc(s["pe_st"], 1)

            def a_pv(i, p, u):
                if u == 0:
                    pe.wait_ge(s["act_v"], i + 1)
                pe.wait_ge(s["act_exp"], U * i + u + 1)
                for t in range(TT):
                    for a in range(HU):
                        last = nc.tensor.matmul(M1[32 * a:32 * a + 32, 0:T], v[p][:, t, HU * u + a, :],
                                                pT[u % 2][:, a, t * T:(t + 1) * T],
                                                start=(t == 0), stop=(t == TT - 1))
                last.then_inc(s["pe_pv"], 1)

            def b_oT(j, t):
                if t == 0:
                    pe.wait_ge(s["act_oT"], U * j + U)
                else:
                    pe.wait_ge(s["dve_on"], TT * j + t)
                for u in range(U):
                    last = transpose(M1[:, u * HU * 32:(u + 1) * HU * 32], oT[:, u, t * P:(t + 1) * P], HU * 32)
                last.then_inc(s["pe_oT"], 1)

            def b_onT(j):
                pe.wait_ge(s["dve_on"], TT * j + TT)
                for c in range(2):
                    for t in range(TT):
                        f = on[:, t, :, :].rearrange("p h d -> p (h d)")
                        last = transpose(M1[0:KH, (c * TT + t) * P:(c * TT + t + 1) * P],
                                         f[:, c * KH:(c + 1) * KH], P)
                last.then_inc(s["pe_onT"], 1)

            def b_y(j):
                pe.wait_ge(s["act_onT"], j + 1)
                for t in range(TT):
                    for c in range(2):
                        last = nc.tensor.matmul(M1[:, t * E:(t + 1) * E],
                                                onT[:, (c * TT + t) * P:(c * TT + t + 1) * P], wo[:, c, :],
                                                start=(c == 0), stop=(c == 1))
                last.then_inc(s["pe_yat"], 1)

            def b_x2T(j):
                pe.wait_ge(s["dve_x2"], j + 1)
                for c in range(2):
                    for t in range(TT):
                        last = transpose(M1[0:KH, (c * TT + t) * P:(c * TT + t + 1) * P],
                                         x2c[:, t, c * KH:(c + 1) * KH], P)
                last.then_inc(s["pe_x2T"], 1)

            def b_lg(j):
                pe.wait_ge(s["act_x2T"], j + 1)
                for t in range(TT):
                    for c in range(2):
                        last = nc.tensor.matmul(M1[:, t * NE:(t + 1) * NE],
                                                x2T[:, (c * TT + t) * P:(c * TT + t + 1) * P], wr[:, c, :],
                                                start=(c == 0), stop=(c == 1))
                last.then_inc(s["pe_lg"], 1)

            def step(i, p, ta, tb, att, clo, fin):
                n2, n, j, j2 = i + 2, i + 1, i - 1, i - 2
                if att:
                    a_s(i, p, 0)
                if clo:
                    pe.wait_ge(s["act_oT"], U * j + 3)
                    a_pv(j, 1 - p, 3)
                if tb:
                    f_x1T(n)
                if clo:
                    b_oT(j, 0)
                if att:
                    a_s(i, p, 1)
                if clo:
                    b_oT(j, 1)
                if tb:
                    f_qk(n, 0, s["act_x1T"], s["pe_q"])
                if att:
                    a_s(i, p, 2)
                    if clo:
                        pe.wait_ge(s["dve_on"], TT * j + TT)
                    a_nmT(i, 0)
                if tb:
                    f_qk(n, 1, s["dve_q"], s["pe_k"])
                if att:
                    a_s(i, p, 3)
                if clo:
                    if att:
                        pe.wait_ge(s["act_nmT"], 2 * i + 1)
                    b_onT(j)
                if att:
                    a_st(i, p, 0)
                if clo:
                    b_y(j)
                if ta:
                    pe.wait_ge(s[f"ld_xs2{p}"], 16 * half(n2, p) + 16)
                    pe.wait_ge(s["pool_xs"], n2 + 1)
                if tb:
                    f_v(n)
                if att:
                    pe.wait_ge(s["dve_yb"], j + 1) if clo else pe.wait_ge(s["act_nmT"], 2 * i + 1)
                    a_nmT(i, 1)
                    a_st(i, p, 1)
                if ta:
                    if tb:
                        apart(pe)
                        pe.wait_ge(s["act_v"], n + 1)
                    f_xT(n2, p)
                if att:
                    pe.wait_ge(s["act_nmT"], 2 * i + 2)
                    a_pv(i, p, 0)
                if ta:
                    f_o12(n2)
                if att:
                    pe.wait_ge(s["act_oT"], U * i + 1)
                    a_pv(i, p, 1)
                if ta:
                    f_y(n2)
                if fin:
                    if att:
                        pe.wait_ge(s["act_oT"], U * i + 2)
                    elif clo:
                        pe.wait_ge(s["dve_yb"], j + 1)
                    b_x2T(j2)
                if att:
                    a_st(i, p, 2)
                if ta:
                    f_h(n2)
                if fin:
                    b_lg(j2)
                if att:
                    a_st(i, p, 3)
                    pe.wait_ge(s["dve_lg"], j2 + 1) if fin else pe.wait_ge(s["act_oT"], U * i + 2)
                    a_pv(i, p, 2)

            over_images(pe, step)
            moe_tensor(pe)

        @block.scalar
        def _(act):
            act.wait_ge(s["ld_const"], n_const)

            def f_xT(n):
                act.wait_ge(s["pe_xT"], n + 1)
                wait_prev(act, s["pe_y"], n)
                nc.scalar.activation(rr[0:GP * C0, :], M0[0:GP * C0, 0:T], ACT.Copy)
                nc.scalar.activation(x12T[:, :], M0[0:KH, T:2 * T], ACT.Copy).then_inc(s["act_xT"], 1)

            def f_o12(n):
                act.wait_ge(s["pe_o12"], n + 1)
                nc.scalar.activation(bd[P - T1:P, EM:2 * EM], M0[P - T1:P, 0:EM], ACT.Copy)
                nc.scalar.activation(bd2[0:T2, :], M0[0:T2, EM:2 * EM], ACT.Copy) \
                    .then_inc(s["act_o12"], 1)

            def f_y(n):
                act.wait_ge(s["pe_y"], n + 1)
                wait_prev(act, s["pe_h"], n)
                nc.scalar.activation(y01[:, :], M0[:, 0:T], ACT.Identity, bias=bias01[:, :])
                nc.scalar.activation(y2[0:EM, :], M0[0:EM, T:2 * T], ACT.Identity, bias=bias2[:, :]) \
                    .then_inc(s["act_y"], 1)

            def f_x1T(n):
                act.wait_ge(s["pe_x1T"], n + 1)
                wait_prev(act, s["pe_v"], n)
                nc.scalar.activation(x1T[:, :, :].rearrange("p c t -> p (c t)"), M0[0:KH, :], ACT.Copy) \
                    .then_inc(s["act_x1T"], 1)

            def f_qk(n, p, which, scale, ready, done):
                act.wait_ge(ready, n + 1)
                if which == 0:
                    wait_prev(act, s[f"st_qk{1 - p}"], 32 * half(n + 1, 1 - p))
                nc.scalar.activation(qk[:, which, 0, :, :].rearrange("p h t -> p (h t)"), M0[0:KH, :], ACT.Copy,
                                     scale=scale).then_inc(done, 1)

            def f_qk2(n, which, ready, done):
                act.wait_ge(ready, n + 1)
                nc.scalar.activation(qk[:, which, 1, :, :].rearrange("p h t -> p (h t)"), qkr[which][:, :], ACT.Copy) \
                    .then_inc(done, 1)

            def f_v(n, p):
                act.wait_ge(s["pe_v"], n + 1)
                wait_prev(act, s["pe_pv"], U * (n - 1))
                nc.scalar.activation(v[p][:, :, :, 0:HD],
                                     M0[:, 0:TT * E].rearrange("p (t h d) -> p t h d", t=TT, d=HD), ACT.Copy) \
                    .then_inc(s["act_v"], 1)

            def a_nmT(i, v):
                act.wait_ge(s["pe_nmT"], 2 * i + v + 1)
                nc.scalar.activation(nmT[:, v, :], M1[0:NPART * HH, 0:T], ACT.Copy).then_inc(s["act_nmT"], 1)

            def a_exp(i, u):
                act.wait_ge(s["pe_st"], U * i + u + 1)
                wait_prev(act, s["pe_pv"], U * i + u - 1)
                nc.scalar.activation(pT[u % 2][:, :, :], ST[:, :, :], ACT.Exp).then_inc(s["act_exp"], 1)

            def a_oT(i, u):
                act.wait_ge(s["pe_pv"], U * i + u + 1)
                if u == 0:
                    wait_prev(act, s["pe_oT"], TT * i)
                nc.scalar.activation(oT[:, u, :], M1[0:HU * 32, 0:T], ACT.Copy).then_inc(s["act_oT"], 1)

            def b_onT(j):
                act.wait_ge(s["pe_onT"], j + 1)
                wait_prev(act, s["pe_yat"], j)
                nc.scalar.activation(onT[:, :], M1[0:KH, :], ACT.Copy).then_inc(s["act_onT"], 1)

            def b_x2T(j):
                act.wait_ge(s["pe_x2T"], j + 1)
                wait_prev(act, s["pe_lg"], j)
                nc.scalar.activation(x2T[:, :], M1[0:KH, :], ACT.Copy).then_inc(s["act_x2T"], 1)

            def step(i, p, ta, tb, att, clo, fin):
                n2, n, j, j2 = i + 2, i + 1, i - 1, i - 2
                if clo:
                    a_oT(j, 3)
                if tb:
                    f_x1T(n)
                    f_qk(n, 1 - p, 0, SCALE, s["pe_q"], s["act_q"])
                if att:
                    a_nmT(i, 0)
                if tb:
                    f_qk2(n, 0, s["dve_q"], s["act_q2"])
                    f_qk(n, 1 - p, 1, 1.0, s["pe_k"], s["act_k"])
                if clo:
                    b_onT(j)
                if tb:
                    f_qk2(n, 1, s["dve_k"], s["act_k2"])
                if att:
                    a_exp(i, 0)
                if tb:
                    f_v(n, 1 - p)
                if att:
                    a_nmT(i, 1)
                    a_exp(i, 1)
                if ta:
                    f_xT(n2)
                if att:
                    a_oT(i, 0)
                if ta:
                    f_o12(n2)
                if att:
                    a_oT(i, 1)
                if ta:
                    f_y(n2)
                if fin:
                    b_x2T(j2)
                if att:
                    a_exp(i, 2)
                    a_exp(i, 3)
                    a_oT(i, 2)

            over_images(act, step)
            moe_scalar(act)

        @block.vector
        def _(dve):
            for a in (bd, rr, bd2):
                nc.vector.memset(a[:, :], 0.0)
            nc.vector.memset(rr2[:, :], 0.0).then_inc(s["dve_init"], 1)
            for p in range(2):
                nc.vector.memset(v[p][:, :, :, :], 1.0)
                nc.vector.memset(ks[p][KS:KM, :, :], 1.0)
            nc.vector.memset(ones[:, :], 1.0)
            nc.vector.memset(y2[EM:EM + 1, :], 1.0).then_inc(s["dve_init"], 1)
            dve.wait_ge(s["dve_init"], 2)
            dve.wait_ge(s["ld_const"], n_const)
            nc.vector.tensor_copy(ident16[:, :], ident[:, :]).then_inc(s["dve_init"], 1)

            def norm_stats(src, st, mv, done_st, done_mv, n):
                for t in range(TT):
                    last = nc.vector.bn_stats(st[:, t, :], src(t))
                last.then_inc(done_st, 1)
                apart(dve)
                dve.wait_ge(done_st, n + 1)
                for t in range(TT):
                    last = nc.vector.bn_aggr(mv[:, t, :], st[:, t, :])
                last.then_inc(done_mv, 1)

            def normalize(dst, src, mv, rs):
                for t in range(TT):
                    last = nc.vector.tensor_scalar(dst(t), src(t), mv[:, t, 0:1], rs[:, t:t + 1],
                                                   ALU.subtract, ALU.mult)
                return last

            def f_h(n):
                dve.wait_ge(s["pe_h"], n + 1)
                dst = hr[:, ds(TT * n, TT), :]
                nc.vector.tensor_copy(dst, M0[:, 0:TT * E].rearrange("p (t e) -> p t e", e=E)) \
                    .then_inc(s["dve_h"], 1)

            def f_hst(n):
                apart(dve)
                dve.wait_ge(s["dve_h"], n + 1)
                wait_prev(dve, s["pool_rs1"], n)
                norm_stats(lambda t: hr[:, ds(TT * n + t, 1), :].rearrange("p a e -> p (a e)"),
                           st1, mv1, s["dve_st1"], s["dve_mv1"], n)

            def f_x1(n):
                dve.wait_ge(s["pool_rs1"], n + 1)
                wait_prev(dve, s["pe_x1T"], n)
                normalize(lambda t: xn1[:, t, :], lambda t: hr[:, ds(TT * n + t, 1), :].rearrange("p a e -> p (a e)"),
                          mv1, rs1).then_inc(s["dve_x1"], 1)

            def f_qk(n, which, scale, ready, done):
                dve.wait_ge(ready, n + 1)
                nc.vector.scalar_tensor_tensor(qkr[which][:, :], M0[0:KH, :], scale,
                                               qk[:, which, 0, :, :].rearrange("p h t -> p (h t)"),
                                               ALU.mult, ALU.subtract).then_inc(done, 1)

            def a_max(i, u):
                dve.wait_ge(s["pe_s"], U * i + u + 1)
                nc.vector.tensor_reduce(negmax[:, :, HU * u:HU * u + HU].rearrange("p t h -> p h t"),
                                        S[:, :, :].rearrange("p a (t k) -> p a t k", t=TT), AX.X, ALU.max,
                                        negate=True).then_inc(s["dve_max"], 1)

            def a_nm(i, v):
                dve.wait_ge(s["dve_max"], U * i + 2 * v + 2)
                wait_prev(dve, s["pe_nmT"], 2 * i)
                m, at = negmax[:, :, v * HH:(v + 1) * HH], NPART * (2 * i + v)
                nc.vector.tensor_copy(nm[:, v, :, 0, :], m).then_inc(s["dve_nmp"], 1)
                dve.wait_ge(s["dve_nmp"], at + 1)
                nc.vector.tensor_tensor(nmr[:, v, :, :], m, nm[:, v, :, 0, :], ALU.subtract).then_inc(s["dve_nmp"], 1)
                dve.wait_ge(s["dve_nmp"], at + 2)
                nc.vector.tensor_copy(nm[:, v, :, 1, :], nmr[:, v, :, :]).then_inc(s["dve_nmp"], 1)
                dve.wait_ge(s["dve_nmp"], at + 3)
                nc.vector.tensor_tensor(nm[:, v, :, 2, :], nmr[:, v, :, :], nm[:, v, :, 1, :], ALU.subtract) \
                    .then_inc(s["dve_nm"], 1)

            def b_on(j, t):
                dve.wait_ge(s["pe_oT"], TT * j + t + 1)
                if t == 0:
                    wait_prev(dve, s["pe_onT"], j)
                m = M1[:, 0:HEADS * 32].rearrange("p (h d) -> p h d", d=32)
                nc.vector.reciprocal(rden[:, t, :], m[:, :, HD]).then_inc(s["dve_rden"], 1)
                dve.wait_ge(s["dve_rden"], TT * j + t + 1)
                nc.vector.tensor_tensor(on[:, t, :, :], m[:, :, 0:HD],
                                        rden[:, t, :].unsqueeze(2).to_broadcast([P, HEADS, HD]), ALU.mult) \
                    .then_inc(s["dve_on"], 1)

            def b_yb(j):
                dve.wait_ge(s["pe_yat"], j + 1)
                nc.vector.tensor_tensor(yb[:, :, :], M1[:, 0:TT * E].rearrange("p (t e) -> p t e", e=E),
                                        bout_b[:, :].unsqueeze(1).to_broadcast([P, TT, E]), ALU.add) \
                    .then_inc(s["dve_yb"], 1)

            def b_yst(j):
                apart(dve)
                dve.wait_ge(s["dve_yb"], j + 1)
                norm_stats(lambda t: yb[:, t, :], st2, mv2, s["dve_st2"], s["dve_mv2"], j)

            def b_yn(j):
                dve.wait_ge(s["pool_rs2"], j + 1)
                wait_prev(dve, s["pool_h2"], j)
                normalize(lambda t: yn[:, t, :], lambda t: yb[:, t, :], mv2, rs2).then_inc(s["dve_yn"], 1)

            def b_stats(j):
                apart(dve)
                dve.wait_ge(s["pool_h2"], j + 1)
                wait_prev(dve, s["pool_rs3"], j)
                norm_stats(lambda t: hr[:, ds(TT * j + t, 1), :].rearrange("p a e -> p (a e)"),
                           st3, mv3, s["dve_st3"], s["dve_mv3"], j)

            def b_x2(j):
                dve.wait_ge(s["pool_rs3"], j + 1)
                wait_prev(dve, s["pool_r"], j)
                wait_prev(dve, s["pe_x2T"], j)
                normalize(lambda t: x2c[:, t, :], lambda t: hr[:, ds(TT * j + t, 1), :].rearrange("p a e -> p (a e)"),
                          mv3, rs3).then_inc(s["dve_x2"], 1)

            def b_lg(j):
                dve.wait_ge(s["pe_lg"], j + 1)
                nc.vector.tensor_copy(lg[:, ds(TT * j, TT), :], M1[:, 0:TT * NE].rearrange("p (t e) -> p t e", e=NE)) \
                    .then_inc(s["dve_lg"], 1)

            def step(i, p, ta, tb, att, clo, fin):
                n2, n, j, j2 = i + 2, i + 1, i - 1, i - 2
                if att:
                    a_max(i, 0)
                if clo:
                    b_on(j, 0)
                if att:
                    a_max(i, 1)
                if clo:
                    b_on(j, 1)
                if att:
                    a_nm(i, 0)
                if tb:
                    f_qk(n, 0, SCALE, s["act_q"], s["dve_q"])
                if att:
                    a_max(i, 2)
                if tb:
                    f_qk(n, 1, 1.0, s["act_k"], s["dve_k"])
                if att:
                    a_max(i, 3)
                if clo:
                    b_yb(j)
                if att:
                    a_nm(i, 1)
                if clo:
                    b_yst(j)
                if fin:
                    b_x2(j2)
                if clo:
                    b_yn(j)
                if ta:
                    f_h(n2)
                if fin:
                    b_lg(j2)
                if ta:
                    f_hst(n2)
                if clo:
                    b_stats(j)
                if ta:
                    f_x1(n2)

            over_images(dve, step)
            moe_vector(dve)

        @block.gpsimd
        def _(pool):
            nc.gpsimd.memset(mhalf[:, :], -0.5)
            nc.gpsimd.memset(epsc[:, :], EPS)
            nc.gpsimd.memset(padrow[:, :], 0.0).then_inc(s["pool_init"], 1)
            pool.wait_ge(s["pool_init"], 1)
            nc.gpsimd.iota(padid_i[:, :], [[0, 1]], base=NT * P + 1, channel_multiplier=1) \
                .then_inc(s["pool_init"], 1)
            nc.gpsimd.iota(tokid_i[:, :], [[P, NT]], base=1, channel_multiplier=1).then_inc(s["pool_init"], 1)
            pool.wait_ge(s["ld_idx2"], 16)
            for c in range(T2 * GP // P):
                nc.gpsimd.indirect_dma_start(g2[:, c, :], None, x2,
                                             bass.IndirectOffsetOnAxis(i2[:, c:c + 1], 0)).then_inc(s["ga2"], 16)
            pool.wait_ge(s["ld_idx1"], 16)
            for c in range(T1 * GP // P):
                nc.gpsimd.indirect_dma_start(g1r[:, c, :], None, x1,
                                             bass.IndirectOffsetOnAxis(i1[:, c:c + 1], 0)).then_inc(s["ga1"], 16)
            pool.wait_ge(s["ld_idx0"], 16)
            for c in range(TT):
                for g in range(GP):
                    nc.gpsimd.indirect_dma_start(g0[:, c, g, :], None, x0,
                                                 bass.IndirectOffsetOnAxis(i0[:, c, g:g + 1], 0)) \
                        .then_inc(s["ga0"], 16)
            pool.wait_ge(s["ga0"], 16 * TT * GP)
            pool.wait_ge(s["ld_g1"], 16)

            def f_xs(n):
                wait_prev(pool, s["pe_xT"], n)
                nc.gpsimd.tensor_copy(xs1[:, :, :], g1[:, :, ds(n * C1, C1)])
                nc.gpsimd.tensor_copy(xs0[:, :, :, :].rearrange("p t g c -> p (t g) c"),
                                      g0[:, :, :, ds(n * C0, C0)].rearrange("p t g c -> p (t g) c")) \
                    .then_inc(s["pool_xs"], 1)

            def rsqrt(rs, mv, var, ready, free, added, done, n):
                pool.wait_ge(ready, n + 1)
                wait_prev(pool, free, n)
                nc.gpsimd.tensor_tensor(var[:, :], mv[:, :, 1], epsc[:, :], ALU.add).then_inc(added, 1)
                pool.wait_ge(added, n + 1)
                nc.gpsimd.tensor_tensor(rs[:, :], var[:, :], mhalf[:, :], ALU.pow).then_inc(done, 1)

            def f_qk3(n, which, ready, done):
                pool.wait_ge(ready, n + 1)
                nc.gpsimd.tensor_tensor(qk[:, which, 2, :, :].rearrange("p h t -> p (h t)"), qkr[which][:, :],
                                        qk[:, which, 1, :, :].rearrange("p h t -> p (h t)"),
                                        ALU.subtract).then_inc(done, 1)

            def step(i, p, ta, tb, att, clo, fin):
                n2, n, j, j2 = i + 2, i + 1, i - 1, i - 2
                if tb:
                    f_qk3(n, 0, s["act_q2"], s["pool_q3"])
                    f_qk3(n, 1, s["act_k2"], s["pool_k3"])
                if clo:
                    hj = hr[:, ds(TT * j, TT), :]
                    rsqrt(rs2, mv2, var2, s["dve_mv2"], s["dve_yn"], s["pool_var2"], s["pool_rs2"], j)
                    pool.wait_ge(s["dve_yn"], j + 1)
                    nc.gpsimd.tensor_tensor(yg[:, :, :], yn[:, :, :], lng_b[:, :].unsqueeze(1).to_broadcast([P, TT, E]),
                                            ALU.mult).then_inc(s["pool_ln"], 1)
                    pool.wait_ge(s["pool_ln"], 2 * j + 1)
                    nc.gpsimd.tensor_tensor(yl[:, :, :], yg[:, :, :], lnb_b[:, :].unsqueeze(1).to_broadcast([P, TT, E]),
                                            ALU.add).then_inc(s["pool_ln"], 1)
                    pool.wait_ge(s["pool_ln"], 2 * j + 2)
                    nc.gpsimd.tensor_tensor(hj, hj, yl[:, :, :], ALU.add).then_inc(s["pool_h2"], 1)
                    apart(pool)
                    pool.wait_ge(s["pool_h2"], j + 1)
                if fin:
                    hj2 = hr[:, ds(TT * j2, TT), :]
                    pool.wait_ge(s["dve_x2"], j2 + 1)
                    nc.gpsimd.tensor_copy(xrow[:, ds(TT * j2, TT), :], x2c[:, :, :])
                    nc.gpsimd.tensor_tensor(hj2, hj2, x2c[:, :, :], ALU.add).then_inc(s["pool_r"], 1)
                if ta:
                    rsqrt(rs1, mv1, var1, s["dve_mv1"], s["dve_x1"], s["pool_var1"], s["pool_rs1"], n2)
                if clo:
                    rsqrt(rs3, mv3, var3, s["dve_mv3"], s["dve_x2"], s["pool_var3"], s["pool_rs3"], j)
                if ta and more(n2):
                    f_xs(n2 + 1)

            f_xs(0)
            over_images(pool, step)
            moe_gpsimd(pool)


def _interpolation(n_in, n_out):
    import numpy as np
    pos = (np.arange(n_out, dtype=np.float32) + np.float32(0.5)) * np.float32(n_in / n_out) - np.float32(0.5)
    pos = np.clip(pos, 0.0, n_in - 1).astype(np.float32)
    lo = np.floor(pos).astype(np.int64)
    hi = np.minimum(lo + 1, n_in - 1)
    w = (pos - lo).astype(np.float32)
    m = np.zeros((n_in, n_out), np.float32)
    m[lo, np.arange(n_out)] += 1 - w
    m[hi, np.arange(n_out)] += w
    return m


def kernel(**inputs):
    import numpy as np
    import concourse.bacc as bacc
    from concourse import mybir
    from concourse.bass_utils import run_bass_kernel_spmd

    a = {k: np.asarray(v) for k, v in inputs.items()}
    x = a["x"]
    B, C, H, _ = x.shape
    T, P = 256, 128

    def patches(p):
        h = H // p
        t = x.reshape(B, C, h, p, h, p).transpose(2, 4, 0, 3, 5, 1)
        return t.reshape(h * h, B * p * p * C)

    w_qkv = a["L0_attn_w_qkv"].reshape(192, 3, 12, 16)
    w_qkv = np.concatenate([w_qkv[:, :2].transpose(0, 1, 3, 2).reshape(192, 384), w_qkv[:, 2].reshape(192, 192)], 1)
    k = "L0_tok_"
    arrays = {
        "x0": patches(1), "x1": patches(2), "x2": patches(4),
        "w0t": a[k + "W0"].T, "w1t": a[k + "W1"].T, "w2t": a[k + "W2"].T,
        "b012": np.concatenate([a[k + "b0"], a[k + "b1"], a[k + "b2"]])[:, None],
        "wft": a[k + "Wf"].T, "bf": a[k + "bf"][None, :],
        "idx0": a[k + "idx0"], "idx1": a[k + "idx1"], "idx2": a[k + "idx2"],
        "w_qkv": w_qkv, "w_out": a["L0_attn_w_out"], "b_out": a["L0_attn_b_out"],
        "ln_g": a["L0_attn_ln_g"], "ln_b": a["L0_attn_ln_b"], "wrt": a["L0_ffn_Wr"].T,
        "ew1": a["L0_ffn_W1"], "eb1": a["L0_ffn_b1"], "ew2": a["L0_ffn_W2"], "eb2": a["L0_ffn_b2"],
        "c_ident": np.eye(P, dtype=np.float32), "c_tri": np.triu(np.ones((P, P), np.float32), 1),
        "c_interp1": _interpolation(a[k + "idx1"].size // 16, T),
        "c_interp2": _interpolation(a[k + "idx2"].size // 16, T),
        "c_iota": np.tile(np.arange(P, dtype=np.float32), (P, 1)),
    }
    arrays = {n: np.ascontiguousarray(v) for n, v in arrays.items()}
    nc = bacc.Bacc("TRN2", target_bir_lowering=False, num_devices=1)
    args = [nc.dram_tensor(n, v.shape, mybir.dt.from_np(v.dtype), kind="ExternalInput").ap()
            for n, v in arrays.items()]
    args.append(nc.dram_tensor("out", (B, T, 192), mybir.dt.float32, kind="ExternalOutput").ap())
    vit_tower(nc, *args)
    r = run_bass_kernel_spmd(nc, [arrays], core_ids=[0])
    return r.results[0]["out"]
```
